# Optimizing a Trainium2 kernel written in Bass

```python
import numpy as np
import jax
import jax.numpy as jnp

def _softmax(x, axis=-1):
    return jax.nn.softmax(x, axis=axis)

def _gelu(x):
    return jax.nn.gelu(x, approximate=True)

def _silu(x):
    return jax.nn.silu(x)

def _sigmoid(x):
    return jax.nn.sigmoid(x)

def _layernorm(x, axis=-1, eps=1e-05):
    m = jnp.mean(x, axis=axis, keepdims=True)
    v = jnp.var(x, axis=axis, keepdims=True)
    return (x - m) / jnp.sqrt(v + eps)

def _scatter_add(tgt, idx, src, axis=0):
    return tgt.at[idx].add(src)

def _segment_sum(src, seg, n):
    return jax.ops.segment_sum(src, seg, n)
kernel_name = 'mk_recurrent_d1_jaxref_r4_467379'

def setup_inputs(seed: int=0):
    np.random.seed(seed)
    _w = jnp.asarray

    def _L0_attn_setup():
        import jax, jax.numpy as jnp
        import numpy as np
        B, S, D, H = (2, 512, 512, 16)
        HD = D // H
        key = jax.random.key(seed)
        ks = jax.random.split(key, 5)
        scale = 0.02
        return {'hidden_states': jax.random.normal(ks[0], (B, S, D), dtype=jnp.float32), 'Wqkv_w': jax.random.normal(ks[1], (3 * D, D), dtype=jnp.float32) * scale, 'Wqkv_b': jax.random.normal(ks[2], (3 * D,), dtype=jnp.float32) * scale, 'out_w': jax.random.normal(ks[3], (D, D), dtype=jnp.float32) * scale, 'out_b': jax.random.normal(ks[4], (D,), dtype=jnp.float32) * scale}
    _L0_attn_in = _L0_attn_setup()

    def _L0_ffn_setup():
        import math
        import jax, jax.numpy as jnp
        import numpy as np
        from jax import lax
        D = 512
        I = 256
        E = 32
        K = 4
        NG = 8
        TKG = 3
        NSH = 2
        SCALE = 2.5
        CF = 1.25
        B, S = (2, 512)

        def _router(x, router_w, e_bias):
            scores = jax.nn.sigmoid(x @ router_w.T)
            sc = scores + e_bias[None, :]
            T = x.shape[0]
            gs = sc.reshape(T, NG, E // NG)
            group_scores = lax.top_k(gs, 2)[0].sum(-1)
            _, gidx = lax.top_k(group_scores, TKG)
            gmask = jnp.zeros((T, NG), sc.dtype).at[jnp.arange(T)[:, None], gidx].set(1.0)
            smask = jnp.repeat(gmask, E // NG, axis=1)
            masked = jnp.where(smask > 0, sc, 0.0)
            _, topk_idx = lax.top_k(masked, K)
            topk_w = jnp.take_along_axis(scores, topk_idx, axis=1)
            topk_w = topk_w / (topk_w.sum(-1, keepdims=True) + 1e-20)
            topk_w = topk_w * SCALE
            return (topk_idx.astype(jnp.int32), topk_w)

        def _moe_forward(hidden_states, router_w, e_bias, W_gate, W_up, W_down, shared_gate, shared_up, shared_down):
            b, s, d = hidden_states.shape
            T = b * s
            C = int(math.ceil(CF * T / E))
            EC = E * C
            x = hidden_states.reshape(T, d)
            topk_idx, topk_w = _router(x, router_w, e_bias)
            expert_flat = topk_idx.reshape(-1)
            w_flat = topk_w.reshape(-1)
            tok_flat = jnp.repeat(jnp.arange(T, dtype=jnp.int32), K)
            sort_ix = jnp.argsort(expert_flat)
            e_sorted = expert_flat[sort_ix]
            tok_s = tok_flat[sort_ix]
            w_s = w_flat[sort_ix]
            counts = jnp.zeros(E, jnp.int32).at[e_sorted].add(1)
            group_start = jnp.concatenate([jnp.zeros(1, jnp.int32), jnp.cumsum(counts)[:-1].astype(jnp.int32)])
            pos = jnp.arange(T * K, dtype=jnp.int32) - group_start[e_sorted]
            valid = pos < C
            dest = e_sorted * C + jnp.where(valid, pos, 0)
            slots_token = jnp.zeros(EC, jnp.int32).at[dest].add(jnp.where(valid, tok_s, 0))
            slots_w = jnp.zeros(EC, w_s.dtype).at[dest].add(jnp.where(valid, w_s, 0.0))
            Xp = x[slots_token].reshape(E, C, d)
            G = jnp.einsum('ecd,edi->eci', Xp, W_gate)
            U = jnp.einsum('ecd,edi->eci', Xp, W_up)
            Y = jnp.einsum('eci,eid->ecd', jax.nn.silu(G) * U, W_down)
            Yf = Y.reshape(EC, d) * slots_w[:, None]
            out = jnp.zeros((T, d), x.dtype).at[slots_token].add(Yf)
            shared = jax.nn.silu(x @ shared_gate.T) * (x @ shared_up.T) @ shared_down.T
            return (out + shared).reshape(b, s, d)
        key = jax.random.key(seed)
        ks = jax.random.split(key, 8)

        def rn(k, shape, scale=0.02):
            return jax.random.normal(k, shape, jnp.float32) * scale
        return {'hidden_states': jax.random.normal(ks[0], (B, S, D), jnp.float32), 'router_w': rn(ks[1], (E, D)), 'e_bias': jnp.zeros((E,), jnp.float32), 'W_gate': rn(ks[2], (E, D, I)), 'W_up': rn(ks[3], (E, D, I)), 'W_down': rn(ks[4], (E, I, D)), 'shared_gate': rn(ks[5], (I * NSH, D)), 'shared_up': rn(ks[6], (I * NSH, D)), 'shared_down': rn(ks[7], (D, I * NSH))}
    _L0_ffn_in = _L0_ffn_setup()
    _d = {'L0_attn_hidden_states': _L0_attn_in['hidden_states'], 'L0_attn_Wqkv_w': _L0_attn_in['Wqkv_w'], 'L0_attn_Wqkv_b': _L0_attn_in['Wqkv_b'], 'L0_attn_out_w': _L0_attn_in['out_w'], 'L0_attn_out_b': _L0_attn_in['out_b'], 'L0_ffn_router_w': _L0_ffn_in['router_w'], 'L0_ffn_e_bias': _L0_ffn_in['e_bias'], 'L0_ffn_W_gate': _L0_ffn_in['W_gate'], 'L0_ffn_W_up': _L0_ffn_in['W_up'], 'L0_ffn_W_down': _L0_ffn_in['W_down'], 'L0_ffn_shared_gate': _L0_ffn_in['shared_gate'], 'L0_ffn_shared_up': _L0_ffn_in['shared_up'], 'L0_ffn_shared_down': _L0_ffn_in['shared_down']}
    _x0 = _d['L0_attn_hidden_states']
    _d['L0_attn_hidden_states'] = jax.random.normal(jax.random.fold_in(jax.random.key(seed), 1), (8, 512, 512), dtype=_x0.dtype)
    del _x0
    return _d

def reference(L0_attn_hidden_states, L0_attn_Wqkv_w, L0_attn_Wqkv_b, L0_attn_out_w, L0_attn_out_b, L0_ffn_router_w, L0_ffn_e_bias, L0_ffn_W_gate, L0_ffn_W_up, L0_ffn_W_down, L0_ffn_shared_gate, L0_ffn_shared_up, L0_ffn_shared_down):

    def _L0_attn_ref(hidden_states, Wqkv_w, Wqkv_b, out_w, out_b):
        import jax, jax.numpy as jnp
        import numpy as np
        B, S, D, H = (2, 512, 512, 16)
        HD = D // H
        b, s, d = hidden_states.shape
        qkv = hidden_states @ Wqkv_w.T + Wqkv_b
        qkv = qkv.reshape(b, s, 3, H, HD)
        q, k, v = (qkv[:, :, 0], qkv[:, :, 1], qkv[:, :, 2])
        softmax_scale = 1.0 / np.float32(np.sqrt(HD))
        scores = jnp.einsum('bthd,bshd->bhts', q, k) * softmax_scale
        attn = jax.nn.softmax(scores, axis=-1)
        ctx = jnp.einsum('bhts,bshd->bthd', attn, v)
        ctx = ctx.reshape(b, s, d)
        return ctx @ out_w.T + out_b

    def _L0_ffn_ref(hidden_states, router_w, e_bias, W_gate, W_up, W_down, shared_gate, shared_up, shared_down):
        import math
        import jax, jax.numpy as jnp
        import numpy as np
        from jax import lax
        D = 512
        I = 256
        E = 32
        K = 4
        NG = 8
        TKG = 3
        NSH = 2
        SCALE = 2.5
        CF = 1.25
        B, S = (2, 512)

        def _router(x, router_w, e_bias):
            scores = jax.nn.sigmoid(x @ router_w.T)
            sc = scores + e_bias[None, :]
            T = x.shape[0]
            gs = sc.reshape(T, NG, E // NG)
            group_scores = lax.top_k(gs, 2)[0].sum(-1)
            _, gidx = lax.top_k(group_scores, TKG)
            gmask = jnp.zeros((T, NG), sc.dtype).at[jnp.arange(T)[:, None], gidx].set(1.0)
            smask = jnp.repeat(gmask, E // NG, axis=1)
            masked = jnp.where(smask > 0, sc, 0.0)
            _, topk_idx = lax.top_k(masked, K)
            topk_w = jnp.take_along_axis(scores, topk_idx, axis=1)
            topk_w = topk_w / (topk_w.sum(-1, keepdims=True) + 1e-20)
            topk_w = topk_w * SCALE
            return (topk_idx.astype(jnp.int32), topk_w)

        def _moe_forward(hidden_states, router_w, e_bias, W_gate, W_up, W_down, shared_gate, shared_up, shared_down):
            b, s, d = hidden_states.shape
            T = b * s
            C = int(math.ceil(CF * T / E))
            EC = E * C
            x = hidden_states.reshape(T, d)
            topk_idx, topk_w = _router(x, router_w, e_bias)
            expert_flat = topk_idx.reshape(-1)
            w_flat = topk_w.reshape(-1)
            tok_flat = jnp.repeat(jnp.arange(T, dtype=jnp.int32), K)
            sort_ix = jnp.argsort(expert_flat)
            e_sorted = expert_flat[sort_ix]
            tok_s = tok_flat[sort_ix]
            w_s = w_flat[sort_ix]
            counts = jnp.zeros(E, jnp.int32).at[e_sorted].add(1)
            group_start = jnp.concatenate([jnp.zeros(1, jnp.int32), jnp.cumsum(counts)[:-1].astype(jnp.int32)])
            pos = jnp.arange(T * K, dtype=jnp.int32) - group_start[e_sorted]
            valid = pos < C
            dest = e_sorted * C + jnp.where(valid, pos, 0)
            slots_token = jnp.zeros(EC, jnp.int32).at[dest].add(jnp.where(valid, tok_s, 0))
            slots_w = jnp.zeros(EC, w_s.dtype).at[dest].add(jnp.where(valid, w_s, 0.0))
            Xp = x[slots_token].reshape(E, C, d)
            G = jnp.einsum('ecd,edi->eci', Xp, W_gate)
            U = jnp.einsum('ecd,edi->eci', Xp, W_up)
            Y = jnp.einsum('eci,eid->ecd', jax.nn.silu(G) * U, W_down)
            Yf = Y.reshape(EC, d) * slots_w[:, None]
            out = jnp.zeros((T, d), x.dtype).at[slots_token].add(Yf)
            shared = jax.nn.silu(x @ shared_gate.T) * (x @ shared_up.T) @ shared_down.T
            return (out + shared).reshape(b, s, d)
        return _moe_forward(hidden_states, router_w, e_bias, W_gate, W_up, W_down, shared_gate, shared_up, shared_down)
    x = L0_attn_hidden_states
    xn = _layernorm(x, axis=-1)
    s = _L0_attn_ref(xn, L0_attn_Wqkv_w, L0_attn_Wqkv_b, L0_attn_out_w, L0_attn_out_b)
    g = _silu(_L0_ffn_ref(xn, L0_ffn_router_w, L0_ffn_e_bias, L0_ffn_W_gate, L0_ffn_W_up, L0_ffn_W_down, L0_ffn_shared_gate, L0_ffn_shared_up, L0_ffn_shared_down))
    x = x + s * g
    return x

_drawn_inputs = setup_inputs


def setup_inputs(seed=0):
    import zlib

    import numpy as np

    out = dict(_drawn_inputs(seed))
    spreads = {'L0_ffn_e_bias': (0.0, 0.8)}
    factors = {'L0_attn_Wqkv_w': 8.0,
     'L0_attn_Wqkv_b': 8.0,
     'L0_attn_out_w': 8.0,
     'L0_attn_out_b': 35.443,
     'L0_ffn_router_w': 8.0,
     'L0_ffn_W_gate': 8.0,
     'L0_ffn_W_up': 8.0,
     'L0_ffn_W_down': 8.0,
     'L0_ffn_shared_gate': 8.0,
     'L0_ffn_shared_up': 8.0,
     'L0_ffn_shared_down': 8.0}
    for name, (base, spread) in spreads.items():
        noise = np.random.default_rng([zlib.crc32(name.encode()), seed]).standard_normal(out[name].shape)
        drawn = base * np.exp(spread * noise) if base else spread * noise
        out[name] = jnp.asarray(drawn.astype(out[name].dtype))
    for name, factor in factors.items():
        out[name] = (out[name] * factor).astype(out[name].dtype)
    return out
```

```python
import concourse.bass as bass
from concourse import mybir
from contextlib import ExitStack

F32 = mybir.dt.float32
F32R = mybir.dt.float32r
BF16 = mybir.dt.bfloat16
I32 = mybir.dt.int32
U32 = mybir.dt.uint32
ALU = mybir.AluOpType
ACT = mybir.ActivationFunctionType
AX = mybir.AxisListType

P = 128
D = 512
KT = D // P
B, S = 8, 512
T = B * S
TT = S // P
H, HD = 16, 32
GH = P // HD
G = H // GH
E, K, NG, TKG = 32, 4, 8, 3
EG = E // NG
I = 256
IT = I // P
IS = 512
MT = IS // P
ROUTE_SCALE = 2.5
CAP = -(-5 * T // (4 * E))
HALF = CAP // 2
SLOTS = E * CAP
EPS = 1e-5
SENTINEL = 1.0e6
ROWS = T + CAP




def tokens_phase(nc, consts, x, router_wT, e_bias, gateT, upT, downT, qkvT, outT,
                 xn_rows, acc_rows, table, wb_hi, wb_lo, xT):
    ident, = consts
    KC = 29

    with ExitStack() as ctx:
        def sb(name, shape, dt=F32):
            return ctx.enter_context(nc.sbuf_tensor(name, shape, dt))

        def pb(name, shape):
            return ctx.enter_context(nc.psum_tensor(name, shape, F32))

        def sem(name):
            return ctx.enter_context(nc.semaphore(name))

        before = sb("before", [P, P], BF16)
        ones = sb("ones", [P, P], BF16)
        bias_row = sb("bias_row", [P, E])
        slot_base = sb("slot_base", [P, E])
        expert_no = sb("expert_no", [P, E])
        lower_no = sb("lower_no", [P, NG, NG])
        empty = sb("empty", [E, CAP, 2], I32)
        zero_rows = sb("zero_rows", [P, D])
        carrier = sb("carrier", [P, 2])
        rw_raw = sb("rw_raw", [P, KT, E])
        rw_hi = sb("rw_hi", [P, KT, E], F32R)
        rw_lo = sb("rw_lo", [P, KT, E], F32R)
        sw_raw = sb("sw_raw", [P, 2, 3 * IS])
        sw_hi = sb("sw_hi", [P, KT, 3 * IS], F32R)
        sw_lo = sb("sw_lo", [P, KT, 3 * IS], F32R)
        wb_raw = sb("wb_raw", [P, 1024])
        wb_h = sb("wb_h", [P, 1024], F32R)
        wb_l = sb("wb_l", [P, 1024], F32R)
        xin = [sb(f"xin{i}", [P, TT, D]) for i in range(2)]
        xn = [sb(f"xn{i}", [P, TT, D]) for i in range(2)]
        xT_hi = [sb(f"xT_hi{i}", [P, KT, S], F32R) for i in range(2)]
        xT_lo = [sb(f"xT_lo{i}", [P, KT, S], F32R) for i in range(2)]
        stats = sb("stats", [P, TT, 6])
        mv = sb("mv", [P, TT, 2])
        var_eps = sb("var_eps", [P, TT])
        std = sb("std", [P, TT])
        rstd = sb("rstd", [P, TT])
        silu_g = sb("silu_g", [P, 2, S])
        hid = sb("hid", [P, 2, S])
        hid_hi = sb("hid_hi", [P, MT, S], F32R)
        hid_lo = sb("hid_lo", [P, MT, S], F32R)
        ybuf = sb("ybuf", [P, TT, D])
        score = sb("score", [P, TT, E])
        biased = sb("biased", [P, TT, E])
        pair_hi = sb("pair_hi", [P, TT * NG, 2])
        pair_lo = sb("pair_lo", [P, TT * NG, 2])
        top1 = sb("top1", [P, TT * NG])
        low1 = sb("low1", [P, TT * NG])
        low2 = sb("low2", [P, TT * NG])
        top2 = sb("top2", [P, TT * NG])
        gscore = sb("gscore", [P, TT, NG])
        above = sb("above", [P, TT, NG, NG])
        equal = sb("equal", [P, TT, NG, NG])
        rank = sb("rank", [P, TT, NG])
        gmask = sb("gmask", [P, TT, NG])
        masked0 = sb("masked0", [P, TT, E])
        masked = sb("masked", [P, TT, E])
        best = sb("best", [P, TT, 8])
        best_no = sb("best_no", [P, TT, 8], U32)
        best_f = sb("best_f", [P, TT, K])
        onehot = sb("onehot", [P, TT * K, E])
        chosen = sb("chosen", [P, TT, E], BF16)
        onehot_x = sb("onehot_x", [P, TT * K, E])
        weight = sb("weight", [P, TT, K])
        wsum = sb("wsum", [P, TT])
        wsum1 = sb("wsum1", [P, TT])
        wrec = sb("wrec", [P, TT])
        wnorm = sb("wnorm", [P, TT, K])
        carry = sb("carry", [P, E])
        place = sb("place", [P, TT, E])
        over = sb("over", [P, TT, E])
        slot0 = sb("slot0", [P, TT, E])
        slot = sb("slot", [P, TT, E])
        slot_x = sb("slot_x", [P, TT * K, E])
        slot_f = sb("slot_f", [P, TT * K])
        slot_no = sb("slot_no", [P, TT * K], U32)
        token_f = sb("token_f", [P, TT])
        entry = sb("entry", [P, TT, K, 2], I32)

        gu = [pb(f"gu{i}", [P, 2, S]) for i in range(2)]
        tp = pb("tp", [P, 2, S])
        lg = pb("lg", [P, TT, E])
        px = pb("px", [P, TT + 1, E])

        consts_done = sem("a_consts")
        table_set = sem("a_table_set")
        x_loaded = [sem(f"a_x_loaded{i}") for i in range(2)]
        xn_stored = [sem(f"a_xn_stored{i}") for i in range(2)]
        xT_stored = [sem(f"a_xT_stored{i}") for i in range(2)]
        y_stored = sem("a_y_stored")
        sw_loaded = [sem(f"a_sw_loaded{i}") for i in range(2)]
        rw_loaded = sem("a_rw_loaded")
        split_hi = sem("a_split_hi")
        split_lo = sem("a_split_lo")
        wb_loaded = sem("a_wb_loaded")
        wb_split = sem("a_wb_split")
        wb_own = sem("a_wb_own")
        wb_stored = sem("a_wb_stored")
        stat_step = sem("a_stat_step")
        var_ready = sem("a_var_ready")
        std_ready = sem("a_std_ready")
        ln_done = sem("a_ln_done")
        tr_done = sem("a_tr_done")
        xhi_done = sem("a_xhi_done")
        xlo_done = sem("a_xlo_done")
        logits_done = sem("a_logits_done")
        score_done = sem("a_score_done")
        route_step = sem("a_route_step")
        chosen_done = sem("a_chosen_done")
        prefix_done = sem("a_prefix_done")
        entry_done = sem("a_entry_done")
        scattered = sem("a_scattered")
        gu_done = sem("a_gu_done")
        silu_done = sem("a_silu_done")
        hid_done = sem("a_hid_done")
        hhi_done = sem("a_hhi_done")
        hlo_done = sem("a_hlo_done")
        down_done = sem("a_down_done")
        y_copied = sem("a_y_copied")

        x_v = x.rearrange("(b t p) d -> b p t d", p=P, t=TT)
        xn_v = xn_rows[0:T, :].rearrange("(b t p) d -> b p t d", p=P, t=TT)
        acc_v = acc_rows[0:T, :].rearrange("(b t p) d -> b p t d", p=P, t=TT)

        block = ctx.enter_context(nc.Block())

        @block.sync
        def _(sp):
            sp.dma_start(xin[0][:], x_v[0]).then_inc(x_loaded[0], 16)
            sp.dma_start(rw_raw[:], router_wT.rearrange("(k p) e -> p k e", p=P)).then_inc(rw_loaded, 16)
            sp.dma_start(bias_row[:], e_bias.rearrange("(a e) -> a e", a=1).to_broadcast([P, E])
                         ).then_inc(rw_loaded, 16)
            for k in range(KT):
                if k >= 2:
                    sp.wait_ge(split_lo, k)
                for j, w in enumerate((gateT, upT, downT)):
                    sp.dma_start(sw_raw[:, k % 2, j * IS:(j + 1) * IS], w[k * P:(k + 1) * P, :]
                                 ).then_inc(sw_loaded[k % 2], 16)
            sp.dma_start(xin[1][:], x_v[1]).then_inc(x_loaded[1], 16)
            with sp.Fori(0, B // 2) as i:
                for u in range(2):
                    n = 2 * i + u
                    c, d = u, 1 - u
                    sp.wait_ge(wb_stored, 32 * n)
                    if u == 0:
                        sp.dma_start(wb_raw[:], qkvT[bass.ts(i, P), 0:1024]).then_inc(wb_loaded, 32)
                    else:
                        sp.dma_start(wb_raw[:, 0:512], qkvT[bass.ts(i, P), 1024:1536]).then_inc(wb_loaded, 16)
                        sp.dma_start(wb_raw[:, 512:1024], outT[bass.ts(i, P), :]).then_inc(wb_loaded, 16)
                    sp.wait_ge(ln_done, n + 1)
                    sp.dma_start(xin[c][:], x_v[(n + 2) % B]).then_inc(x_loaded[c], 16)
                    sp.dma_start(xn_v[n], xn[c][:]).then_inc(xn_stored[c], 16)
                    sp.wait_ge(wb_split, n + 1)
                    sp.dma_start(wb_hi[bass.ts(i, P), u * 1024:(u + 1) * 1024], wb_h[:].bitcast(F32)).then_inc(wb_stored, 16)
                    sp.dma_start(wb_lo[bass.ts(i, P), u * 1024:(u + 1) * 1024], wb_l[:].bitcast(F32)).then_inc(wb_stored, 16)
                    sp.wait_ge(xlo_done, 2 * n + 2)
                    for part, xt in enumerate((xT_hi[c], xT_lo[c])):
                        sp.dma_start(xT[n, part].rearrange("p (k s) -> p k s", k=KT), xt[:].bitcast(F32)
                                     ).then_inc(xT_stored[c], 16)
                    sp.wait_ge(y_copied, TT * (n + 1))
                    sp.dma_start(acc_v[n], ybuf[:]).then_inc(y_stored, 16)
            sp.wait_ge(y_stored, 16 * B)
            sp.wait_ge(wb_stored, 32 * B)
            for c in range(2):
                sp.wait_ge(xn_stored[c], 16 * (B // 2))
                sp.wait_ge(xT_stored[c], 32 * (B // 2))
                sp.wait_ge(x_loaded[c], 16 * (B // 2 + 1))

        @block.gpsimd
        def _(pool):
            pool.memset(ident[:], 0.0).then_inc(wb_own, 1)
            pool.memset(before[:], 0.0).then_inc(wb_own, 1)
            pool.memset(lower_no[:], 0.0).then_inc(wb_own, 1)
            pool.memset(ones[:], 1.0).then_inc(consts_done, 1)
            pool.memset(zero_rows[:], 0.0).then_inc(consts_done, 1)
            pool.memset(carry[:], 0.0).then_inc(consts_done, 1)
            pool.memset(empty[:], 0).then_inc(wb_own, 1)
            pool.wait_ge(wb_own, 4)
            pool.affine_select(out=ident[:], in_=ident[:], compare_op=ALU.not_equal, fill=1.0, base=0,
                               pattern=[[-1, P]], channel_multiplier=1).then_inc(consts_done, 1)
            pool.affine_select(out=before[:], in_=before[:], compare_op=ALU.is_ge, fill=1.0, base=0,
                               pattern=[[-1, P]], channel_multiplier=1).then_inc(consts_done, 1)
            pool.affine_select(out=lower_no[:], in_=lower_no[:], compare_op=ALU.is_ge, fill=1.0, base=0,
                               pattern=[[-1, NG], [1, NG]], channel_multiplier=0).then_inc(consts_done, 1)
            pool.iota(slot_base[:], [[CAP, E]], base=0, channel_multiplier=0,
                      allow_small_or_imprecise_dtypes=True).then_inc(consts_done, 1)
            pool.iota(expert_no[:], [[1, E]], base=0, channel_multiplier=0,
                      allow_small_or_imprecise_dtypes=True).then_inc(consts_done, 1)
            pool.iota(token_f[:], [[P, TT]], base=0, channel_multiplier=1,
                      allow_small_or_imprecise_dtypes=True).then_inc(consts_done, 1)
            pool.iota(empty[:, :, 0], [[1, CAP]], base=T, channel_multiplier=0).then_inc(consts_done, 1)
            pool.wait_ge(consts_done, 10)
            pool.dma_start(table.rearrange("(e s) c -> e s c", e=E), empty[:]).then_inc(table_set, 16)
            for rows in (xn_rows, acc_rows):
                pool.dma_start(rows[T:T + P, :], zero_rows[:]).then_inc(table_set, 16)
                pool.dma_start(rows[T + P:ROWS, :], zero_rows[0:CAP - P, :]).then_inc(table_set, 16)
            pool.wait_ge(table_set, 16 * 5)
            with pool.Fori(0, B) as n:
                pool.wait_ge(wb_loaded, 32 * n + 32)
                pool.tensor_tensor(wb_h[:], wb_raw[:], zero_rows[:, 0:1].to_broadcast([P, 1024]), ALU.add
                                   ).then_inc(wb_own, 1)
                pool.wait_ge(wb_own, n + 5)
                pool.tensor_tensor(wb_l[:], wb_raw[:], wb_h[:].bitcast(F32), ALU.subtract).then_inc(wb_split, 1)
                pool.wait_ge(entry_done, 2 * n + 2)
                pool.tensor_tensor(carrier[:, 0:1], zero_rows[:, 0:1], zero_rows[:, 1:2], ALU.add)
                for t in range(TT):
                    for k in range(K):
                        j = t * K + k
                        pool.indirect_dma_start(
                            out=table, out_offset=bass.IndirectOffsetOnAxis(ap=slot_no[:, j:j + 1], axis=0),
                            in_=entry[:, t, k, :], in_offset=None, bounds_check=SLOTS - 1, oob_is_err=False,
                        ).then_inc(scattered, 16)
            pool.wait_ge(scattered, 16 * TT * K * B)

        @block.scalar
        def _(act):
            def std_of(m):
                act.wait_ge(var_ready, m + 1)
                act.activation(std[:], var_eps[:], ACT.Sqrt).then_inc(std_ready, 1)

            def xhi(m, buf, pair):
                act.wait_ge(tr_done, 2 * m + pair + 1)
                act.activation(xT_hi[buf][:, 2 * pair:2 * pair + 2, :], tp[:], ACT.Copy).then_inc(xhi_done, 1)

            std_of(0)
            act.wait_ge(rw_loaded, 32)
            act.activation(rw_hi[:], rw_raw[:], ACT.Copy).then_inc(split_hi, 1)
            for k in range(KT):
                act.wait_ge(sw_loaded[k % 2], 48 * (k // 2 + 1))
                act.activation(sw_hi[:, k, :], sw_raw[:, k % 2, :], ACT.Copy).then_inc(split_hi, 1)
            for pair in range(2):
                xhi(0, 0, pair)
            with act.Fori(0, B // 2) as i:
                for u in range(2):
                    n = 2 * i + u
                    c, d = u, 1 - u

                    def silu(mt):
                        act.wait_ge(gu_done, MT * n + mt + 1)
                        act.activation(silu_g[:, mt % 2, :], gu[mt % 2][:, 0, :], ACT.Silu).then_inc(silu_done, 1)

                    def hid_high(mt):
                        if mt == 0:
                            act.wait_ge(down_done, TT * n)
                        act.wait_ge(hid_done, MT * n + mt + 1)
                        act.activation(hid_hi[:, mt, :], hid[:, mt % 2, :], ACT.Copy).then_inc(hhi_done, 1)

                    std_of(n + 1)
                    act.wait_ge(logits_done, n + 1)
                    act.activation(score[:], lg[:], ACT.Sigmoid).then_inc(score_done, 1)
                    silu(0)
                    hid_high(0)
                    silu(1)
                    hid_high(1)
                    act.wait_ge(xT_stored[d], 32 * (i + u))
                    xhi(n + 1, d, 0)
                    silu(2)
                    hid_high(2)
                    xhi(n + 1, d, 1)
                    silu(3)
                    hid_high(3)
                    act.wait_ge(y_stored, 16 * n)
                    for t in range(TT):
                        act.wait_ge(down_done, TT * n + t + 1)
                        act.activation(ybuf[:, t, :], tp[:, t % 2, :], ACT.Copy).then_inc(y_copied, 1)

        @block.vector
        def _(dve):
            def normalise(m, buf, loads, stores):
                dve.wait_ge(x_loaded[buf], 16 * loads)
                for t in range(TT):
                    last = dve.bn_stats(stats[:, t, :], xin[buf][:, t, :])
                last.then_inc(stat_step, 1)
                dve.wait_ge(stat_step, 3 * m + 1)
                dve.memset(carrier[:, 1:2], 0.0)
                for t in range(TT):
                    last = dve.bn_aggr(mv[:, t, :], stats[:, t, :])
                last.then_inc(stat_step, 1)
                dve.wait_ge(stat_step, 3 * m + 2)
                dve.tensor_scalar(var_eps[:], mv[:, :, 1], EPS, None, ALU.add).then_inc(var_ready, 1)
                dve.wait_ge(std_ready, m + 1)
                dve.reciprocal(rstd[:], std[:]).then_inc(stat_step, 1)
                dve.wait_ge(stat_step, 3 * m + 3)
                dve.wait_ge(xn_stored[buf], 16 * stores)
                for t in range(TT):
                    last = dve.tensor_scalar(xn[buf][:, t, :], xin[buf][:, t, :], mv[:, t, 0:1], rstd[:, t:t + 1],
                                             ALU.subtract, ALU.mult)
                last.then_inc(ln_done, 1)

            def xlo(m, buf, pair):
                dve.wait_ge(xhi_done, 2 * m + pair + 1)
                dve.tensor_tensor(xT_lo[buf][:, 2 * pair:2 * pair + 2, :], tp[:],
                                  xT_hi[buf][:, 2 * pair:2 * pair + 2, :].bitcast(F32), ALU.subtract
                                  ).then_inc(xlo_done, 1)

            normalise(0, 0, 1, 0)
            dve.wait_ge(split_hi, 1)
            dve.tensor_tensor(rw_lo[:], rw_raw[:], rw_hi[:].bitcast(F32), ALU.subtract).then_inc(split_lo, 1)
            for k in range(KT):
                dve.wait_ge(split_hi, k + 2)
                dve.tensor_tensor(sw_lo[:, k, :], sw_raw[:, k % 2, :], sw_hi[:, k, :].bitcast(F32), ALU.subtract
                                  ).then_inc(split_lo, 1)
            for pair in range(2):
                xlo(0, 0, pair)
            dve.wait_ge(consts_done, 10)
            with dve.Fori(0, B // 2) as i:
                for u in range(2):
                    n = 2 * i + u
                    c, d = u, 1 - u
                    steps = [0]

                    def step(ins):
                        steps[0] += 1
                        ins.then_inc(route_step, 1)
                        dve.wait_ge(route_step, KC * n + steps[0])

                    def hidden(mt):
                        dve.wait_ge(silu_done, MT * n + mt + 1)
                        dve.tensor_tensor(hid[:, mt % 2, :], silu_g[:, mt % 2, :], gu[mt % 2][:, 1, :], ALU.mult
                                          ).then_inc(hid_done, 1)

                    def hid_low(mt):
                        dve.wait_ge(hhi_done, MT * n + mt + 1)
                        dve.tensor_tensor(hid_lo[:, mt, :], hid[:, mt % 2, :], hid_hi[:, mt, :].bitcast(F32),
                                          ALU.subtract).then_inc(hlo_done, 1)

                    def pick_groups():
                        dve.wait_ge(score_done, n + 1)
                        step(dve.tensor_tensor(biased[:], score[:], bias_row[:].unsqueeze(1).to_broadcast([P, TT, E]),
                                               ALU.add))
                        four = biased[:].rearrange("p t (g a b) -> p (t g) a b", a=2, b=2)
                        dve.tensor_tensor(pair_hi[:], four[:, :, :, 0], four[:, :, :, 1], ALU.max)
                        step(dve.tensor_tensor(pair_lo[:], four[:, :, :, 0], four[:, :, :, 1], ALU.min))
                        dve.tensor_tensor(top1[:], pair_hi[:, :, 0], pair_hi[:, :, 1], ALU.max)
                        dve.tensor_tensor(low1[:], pair_hi[:, :, 0], pair_hi[:, :, 1], ALU.min)
                        step(dve.tensor_tensor(low2[:], pair_lo[:, :, 0], pair_lo[:, :, 1], ALU.max))
                        step(dve.tensor_tensor(top2[:], low1[:], low2[:], ALU.max))
                        step(dve.tensor_tensor(gscore[:].rearrange("p t g -> p (t g)"), top1[:], top2[:], ALU.add))
                        other = gscore[:].unsqueeze(2).to_broadcast([P, TT, NG, NG])
                        own = gscore[:].unsqueeze(3).to_broadcast([P, TT, NG, NG])
                        dve.tensor_tensor(above[:], other, own, ALU.is_gt)
                        step(dve.tensor_tensor(equal[:], other, own, ALU.is_equal))
                        step(dve.tensor_tensor(equal[:], equal[:],
                                               lower_no[:].unsqueeze(1).to_broadcast([P, TT, NG, NG]), ALU.mult))
                        step(dve.tensor_tensor(above[:], above[:], equal[:], ALU.add))
                        step(dve.tensor_reduce(rank[:], above[:], AX.X, ALU.add))
                        step(dve.tensor_scalar(gmask[:], rank[:], TKG - 0.5, None, ALU.is_lt))
                        step(dve.tensor_tensor(masked0[:].rearrange("p t (g a) -> p (t g) a", a=EG),
                                               biased[:].rearrange("p t (g a) -> p (t g) a", a=EG),
                                               gmask[:].rearrange("p t g -> p (t g)").unsqueeze(2)
                                               .to_broadcast([P, TT * NG, EG]), ALU.mult))
                        step(dve.tensor_scalar(masked[:], masked0[:], 0.0, None, ALU.add))

                    def pick_experts():
                        for t in range(TT):
                            last = dve.max(best[:, t, :], masked[:, t, :])
                        step(last)
                        dve.memset(carrier[:, 1:2], 0.0)
                        for t in range(TT):
                            last = dve.max_index(best_no[:, t, :], best[:, t, :], masked[:, t, :])
                        step(last)
                        step(dve.tensor_copy(best_f[:], best_no[:, :, 0:K]))
                        step(dve.tensor_tensor(
                            onehot[:], best_f[:].rearrange("p t k -> p (t k)").unsqueeze(2).to_broadcast([P, TT * K, E]),
                            expert_no[:].unsqueeze(1).to_broadcast([P, TT * K, E]), ALU.is_equal))
                        with nc.allow_low_precision(reason="0 or 1"):
                            dve.tensor_reduce(chosen[:], onehot[:].rearrange("p (t k) e -> p t e k", k=K), AX.X, ALU.add
                                              ).then_inc(chosen_done, 1)

                    def weigh():
                        for t in range(TT):
                            last = dve.tensor_tensor(onehot_x[:, t * K:(t + 1) * K, :], onehot[:, t * K:(t + 1) * K, :],
                                                     score[:, t, :].unsqueeze(1).to_broadcast([P, K, E]), ALU.mult)
                        step(last)
                        step(dve.tensor_reduce(weight[:].rearrange("p t k -> p (t k)"), onehot_x[:], AX.X, ALU.add))
                        step(dve.tensor_reduce(wsum[:], weight[:], AX.X, ALU.add))
                        step(dve.tensor_scalar(wsum1[:], wsum[:], 1e-20, None, ALU.add))
                        step(dve.reciprocal(wrec[:], wsum1[:]))
                        step(dve.tensor_tensor(wnorm[:], weight[:], wrec[:].unsqueeze(2).to_broadcast([P, TT, K]),
                                               ALU.mult))
                        dve.wait_ge(scattered, 16 * TT * K * n)
                        dve.tensor_scalar(entry[:, :, :, 1].bitcast(F32), wnorm[:], ROUTE_SCALE, None, ALU.mult
                                          ).then_inc(entry_done, 1)

                    def place_tokens():
                        dve.wait_ge(prefix_done, n + 1)
                        step(dve.tensor_tensor(place[:], px[:, 0:TT, :], carry[:].unsqueeze(1).to_broadcast([P, TT, E]),
                                               ALU.add))
                        dve.tensor_tensor(carry[:], px[:, TT, :], carry[:], ALU.add)
                        dve.tensor_scalar(over[:], place[:], CAP - 0.5, SENTINEL, ALU.is_gt, ALU.mult)
                        step(dve.tensor_tensor(slot0[:], place[:], slot_base[:].unsqueeze(1).to_broadcast([P, TT, E]),
                                               ALU.add))
                        step(dve.tensor_tensor(slot[:], slot0[:], over[:], ALU.add))
                        for t in range(TT):
                            last = dve.tensor_tensor(slot_x[:, t * K:(t + 1) * K, :], onehot[:, t * K:(t + 1) * K, :],
                                                     slot[:, t, :].unsqueeze(1).to_broadcast([P, K, E]), ALU.mult)
                        step(last)
                        step(dve.tensor_reduce(slot_f[:], slot_x[:], AX.X, ALU.add))
                        step(dve.tensor_copy(entry[:, :, :, 0], token_f[:].unsqueeze(2).to_broadcast([P, TT, K])))
                        dve.tensor_copy(slot_no[:], slot_f[:]).then_inc(entry_done, 1)
                        step(dve.tensor_scalar(token_f[:], token_f[:], float(S), None, ALU.add))

                    normalise(n + 1, d, i + 1 + u, i + u)
                    hidden(0)
                    pick_groups()
                    hid_low(0)
                    hidden(1)
                    pick_experts()
                    hid_low(1)
                    xlo(n + 1, d, 0)
                    hidden(2)
                    weigh()
                    hid_low(2)
                    xlo(n + 1, d, 1)
                    hidden(3)
                    hid_low(3)
                    place_tokens()
                    assert steps[0] == KC, steps

        @block.tensor
        def _(pe):
            def transposes(m, buf, pair):
                for k in range(2 * pair, 2 * pair + 2):
                    for t in range(TT):
                        last = pe.transpose(tp[:, k % 2, t * P:(t + 1) * P], xn[buf][:, t, k * P:(k + 1) * P], ident[:])
                last.then_inc(tr_done, 1)

            pe.wait_ge(consts_done, 10)
            pe.wait_ge(ln_done, 1)
            transposes(0, 0, 0)
            pe.wait_ge(xlo_done, 1)
            transposes(0, 0, 1)
            pe.wait_ge(split_lo, KT + 1)
            with pe.Fori(0, B // 2) as i:
                for u in range(2):
                    n = 2 * i + u
                    c, d = u, 1 - u
                    parts = ((xT_hi[c], 0), (xT_lo[c], 0), (xT_hi[c], 1))

                    def gate_up(mt):
                        for j in range(2):
                            at = j * IS + mt * P
                            for k in range(KT):
                                for q, (xt, low) in enumerate(parts):
                                    w = sw_lo if low else sw_hi
                                    last = pe.matmul(gu[mt % 2][:, j, :], w[:, k, at:at + P], xt[:, k, :],
                                                     start=(k == 0 and q == 0), stop=(k == KT - 1 and q == 2))
                        last.then_inc(gu_done, 1)

                    pe.wait_ge(xlo_done, 2 * n + 2)
                    pe.wait_ge(score_done, n)
                    for t in range(TT):
                        for k in range(KT):
                            for q, (xt, low) in enumerate(parts):
                                w = rw_lo if low else rw_hi
                                last = pe.matmul(lg[:, t, :], xt[:, k, t * P:(t + 1) * P], w[:, k, :],
                                                 start=(k == 0 and q == 0), stop=(k == KT - 1 and q == 2))
                    last.then_inc(logits_done, 1)
                    pe.wait_ge(hid_done, MT * n)
                    gate_up(0)
                    gate_up(1)
                    pe.wait_ge(ln_done, n + 2)
                    pe.wait_ge(y_copied, TT * n)
                    transposes(n + 1, d, 0)
                    pe.wait_ge(hid_done, MT * n + 1)
                    gate_up(2)
                    pe.wait_ge(xlo_done, 2 * n + 3)
                    transposes(n + 1, d, 1)
                    pe.wait_ge(hid_done, MT * n + 2)
                    gate_up(3)
                    pe.wait_ge(chosen_done, n + 1)
                    for t in range(TT + 1):
                        if t < TT:
                            pe.matmul(px[:, t, :], before[:], chosen[:, t, :], start=True, stop=(t == 0))
                        for j in range(t):
                            last = pe.matmul(px[:, t, :], ones[:], chosen[:, j, :], start=(t == TT and j == 0),
                                             stop=(j == t - 1))
                    last.then_inc(prefix_done, 1)
                    pe.wait_ge(xlo_done, 2 * n + 4)
                    for t in range(TT):
                        if t >= 2:
                            pe.wait_ge(y_copied, TT * n + t - 1)
                        for mt in range(MT):
                            if t == 0:
                                pe.wait_ge(hlo_done, MT * n + mt + 1)
                            for q, (hp, w) in enumerate(((hid_hi, sw_hi), (hid_lo, sw_hi), (hid_hi, sw_lo))):
                                last = pe.matmul(tp[:, t % 2, :], hp[:, mt, t * P:(t + 1) * P], w[:, mt, 2 * IS:3 * IS],
                                                 start=(mt == 0 and q == 0), stop=(mt == MT - 1 and q == 2))
                        last.then_inc(down_done, 1)


def experts_phase(nc, consts, W_gate, W_up, W_down, xn_rows, acc_rows, table, load_next, wait_next):
    ident, = consts
    C2 = 2 * CAP

    with ExitStack() as ctx:
        def sb(name, shape, dt=F32):
            return ctx.enter_context(nc.sbuf_tensor(name, shape, dt))

        def pb(name, shape):
            return ctx.enter_context(nc.psum_tensor(name, shape, F32))

        def sem(name):
            return ctx.enter_context(nc.semaphore(name))

        ids_g = [sb(f"ids_g{i}", [HALF, 2, 2], I32) for i in range(2)]
        ids_s = [sb(f"ids_s{i}", [HALF, 2, 2], I32) for i in range(2)]
        raw_gu = [sb(f"raw_gu{i}", [P, 2, KT, I]) for i in range(2)]
        gu_hi = [sb(f"gu_hi{i}", [P, 2, KT, I], F32R) for i in range(2)]
        gu_lo = [sb(f"gu_lo{i}", [P, 2, KT, I], F32R) for i in range(2)]
        raw_dn = [sb(f"raw_dn{i}", [P, IT, D]) for i in range(2)]
        dn_hi = [sb(f"dn_hi{i}", [P, IT, D], F32R) for i in range(2)]
        dn_lo = [sb(f"dn_lo{i}", [P, IT, D], F32R) for i in range(2)]
        xs = [sb(f"xs{i}", [HALF, 2, D]) for i in range(2)]
        xt = [sb(f"xt{i}", [P, KT, 2, CAP], F32R) for i in range(2)]
        gu_low = sb("gu_low", [P, IT, 2, CAP])
        gu_sum = sb("gu_sum", [P, IT, 2, CAP])
        silu_e = sb("silu_e", [P, IT, CAP])
        hid_e = sb("hid_e", [P, IT, CAP])
        he_hi = [sb(f"he_hi{i}", [P, IT, CAP], F32R) for i in range(2)]
        he_lo = [sb(f"he_lo{i}", [P, IT, CAP], F32R) for i in range(2)]
        ys = [sb(f"ys{i}", [HALF, 2, D]) for i in range(2)]
        carrier = sb("carrier_e", [P, 2])

        gup = [pb(f"gup{i}", [P, 2, 512]) for i in range(IT)]
        tpe = pb("tpe", [P, 2, 512])
        yp = pb("yp", [P, 2, D])

        zeroed = sem("e_zeroed")
        gu_loaded = [sem(f"e_gu_loaded{i}") for i in range(2)]
        dn_loaded = [sem(f"e_dn_loaded{i}") for i in range(2)]
        idg_loaded = [sem(f"e_idg_loaded{i}") for i in range(2)]
        ids_loaded = [sem(f"e_ids_loaded{i}") for i in range(2)]
        gathered = [sem(f"e_gathered{i}") for i in range(2)]
        scattered = sem("e_scattered")
        carried = sem("e_carried")
        gu_high = sem("e_gu_high")
        g_low = sem("e_g_low")
        u_low = sem("e_u_low")
        dn_high = sem("e_dn_high")
        dn_low = sem("e_dn_low")
        tr_done = sem("e_tr_done")
        xhi_done = sem("e_xhi_done")
        xlo_done = sem("e_xlo_done")
        gu_done = sem("e_gu_done")
        low_copied = sem("e_low_copied")
        summed = sem("e_summed")
        silu_done = sem("e_silu_done")
        hid_done = sem("e_hid_done")
        hhi_done = sem("e_hhi_done")
        hlo_done = sem("e_hlo_done")
        down_done = sem("e_down_done")
        y_done = sem("e_y_done")

        gate_v = W_gate.rearrange("e (p k) i -> e p k i", k=KT)
        up_v = W_up.rearrange("e (p k) i -> e p k i", k=KT)
        down_v = W_down.rearrange("e (p k) n -> e p k n", k=IT)
        table_v = table.rearrange("(e h p) c -> e p h c", e=E, h=2)

        PEEL = 4

        def over_experts(engine, body):
            with engine.Fori(0, (E - PEEL) // 2) as i:
                for u in range(2):
                    body(2 * i + u, i, u)
            for e in range(E - PEEL, E):
                body(e, e // 2, e % 2)

        def exists(e, ahead):
            return not isinstance(e, int) or e + ahead < E

        block = ctx.enter_context(nc.Block())

        @block.sync
        def _(sp):
            def load_gu(e, c):
                sp.dma_start(raw_gu[c][:, 0], gate_v[e]).then_inc(gu_loaded[c], 16)
                sp.dma_start(raw_gu[c][:, 1], up_v[e]).then_inc(gu_loaded[c], 16)

            def load_dn(e, c):
                sp.dma_start(raw_dn[c][:], down_v[e]).then_inc(dn_loaded[c], 16)

            for e in range(2):
                sp.dma_start(ids_g[e][:], table_v[e]).then_inc(idg_loaded[e], 16)
                load_gu(e, e)
            load_dn(0, 0)
            sp.dma_start(ids_s[0][:], table_v[0]).then_inc(ids_loaded[0], 16)
            for e in (2, 3):
                sp.wait_ge(gathered[e - 2], 32)
                sp.dma_start(ids_g[e - 2][:], table_v[e]).then_inc(idg_loaded[e - 2], 16)
            load_dn(1, 1)
            sp.wait_ge(gu_high, 1)
            sp.wait_ge(g_low, 1)
            sp.wait_ge(u_low, 1)
            load_gu(2, 0)

            def body(e, i, u):
                c, d = u, 1 - u
                if exists(e, 3):
                    sp.wait_ge(gu_high, e + 2)
                    sp.wait_ge(g_low, e + 2)
                    sp.wait_ge(u_low, e + 2)
                    load_gu(e + 3, d)
                if exists(e, 2):
                    sp.wait_ge(dn_high, e + 1)
                    sp.wait_ge(dn_low, e + 1)
                    load_dn(e + 2, c)
                if exists(e, 1):
                    sp.wait_ge(scattered, 32 * e)
                    sp.dma_start(ids_s[d][:], table_v[e + 1]).then_inc(ids_loaded[d], 16)
                if exists(e, 4):
                    sp.wait_ge(gathered[c], 32 * (i + 2))
                    sp.dma_start(ids_g[c][:], table_v[e + 4]).then_inc(idg_loaded[c], 16)
                if isinstance(e, int) and e == E - PEEL:
                    load_next(sp)

            over_experts(sp, body)
            sp.wait_ge(scattered, 32 * E)
            wait_next(sp)

        @block.gpsimd
        def _(pool):
            pool.memset(carrier[:], 0.0).then_inc(zeroed, 1)
            pool.wait_ge(zeroed, 1)

            def carry(earlier):
                pool.wait_ge(carried, earlier)
                pool.tensor_tensor(carrier[:, 0:1], carrier[:, 1:2], carrier[:, 1:2], ALU.add).then_inc(carried, 1)

            def gather(c, uses, earlier):
                pool.wait_ge(idg_loaded[c], 16 * uses)
                carry(earlier)
                for h in range(2):
                    pool.indirect_dma_start(
                        out=xs[c][:, h, :], out_offset=None, in_=xn_rows,
                        in_offset=bass.IndirectOffsetOnAxis(ap=ids_g[c][:, h, 0:1].bitcast(U32), axis=0),
                        bounds_check=ROWS - 1, oob_is_err=True).then_inc(gathered[c], 16)

            def up_low(e, c):
                pool.wait_ge(gu_high, e + 1)
                pool.tensor_tensor(gu_lo[c][:, 1], raw_gu[c][:, 1], gu_hi[c][:, 1].bitcast(F32), ALU.subtract
                                   ).then_inc(u_low, 1)

            gather(0, 1, 0)
            gather(1, 1, 1)
            up_low(0, 0)
            up_low(1, 1)
            pool.wait_ge(tr_done, 1)
            gather(0, 2, 2)

            def body(e, i, u):
                c, d = u, 1 - u
                if exists(e, 3):
                    pool.wait_ge(tr_done, e + 2)
                    gather(d, i + 2 + u, 3 + 2 * e)
                if exists(e, 2):
                    up_low(e + 2, c)
                pool.wait_ge(scattered, 32 * e)
                pool.wait_ge(y_done, 2 * e + 2)
                carry(4 + 2 * e if exists(e, 3) else 3 + (E - 3) + e)
                for h in range(2):
                    pool.indirect_dma_start(
                        out=acc_rows, in_=ys[c][:, h, :], in_offset=None,
                        out_offset=bass.IndirectOffsetOnAxis(ap=ids_s[c][:, h, 0:1].bitcast(U32), axis=0),
                        bounds_check=ROWS - 1, oob_is_err=True, compute_op=ALU.add).then_inc(scattered, 16)

            over_experts(pool, body)

        @block.scalar
        def _(act):
            def split_gu(e, c, uses):
                act.wait_ge(gu_loaded[c], 32 * uses)
                act.activation(gu_hi[c][:], raw_gu[c][:], ACT.Copy).then_inc(gu_high, 1)

            def split_dn(c, uses):
                act.wait_ge(dn_loaded[c], 16 * uses)
                act.activation(dn_hi[c][:], raw_dn[c][:], ACT.Copy).then_inc(dn_high, 1)

            def xhi(e, c):
                act.wait_ge(tr_done, e + 1)
                act.activation(xt[c][:, :, 0, :].rearrange("p (a b) s -> p a b s", b=2),
                               tpe[:, :, 0:C2].rearrange("p a (b s) -> p a b s", b=2), ACT.Copy
                               ).then_inc(xhi_done, 1)

            def low(e, it):
                act.wait_ge(gu_done, 2 * e + it + 1)
                act.activation(gu_low[:, it], gup[it][:, :, CAP:C2], ACT.Copy).then_inc(low_copied, 1)

            def silu(e, it):
                act.wait_ge(summed, 2 * e + it + 1)
                act.activation(silu_e[:, it], gu_sum[:, it, 0], ACT.Silu).then_inc(silu_done, 1)

            def hid_high(e, c, it):
                act.wait_ge(hid_done, 2 * e + it + 1)
                act.activation(he_hi[c][:, it], hid_e[:, it], ACT.Copy).then_inc(hhi_done, 1)

            def hidden(e, c):
                for it in range(IT):
                    silu(e, it)
                for it in range(IT):
                    hid_high(e, c, it)

            split_gu(0, 0, 1)
            split_gu(1, 1, 1)
            xhi(0, 0)
            for it in range(IT):
                low(0, it)
            xhi(1, 1)
            hidden(0, 0)
            split_dn(0, 1)

            def body(e, i, u):
                c, d = u, 1 - u
                if exists(e, 2):
                    act.wait_ge(gu_done, 2 * e + 2)
                    split_gu(e + 2, c, i + 2)
                if exists(e, 1):
                    low(e + 1, 0)
                    act.wait_ge(down_done, 2 * e)
                    split_dn(d, i + 1 + u)
                    low(e + 1, 1)
                    hidden(e + 1, d)
                act.wait_ge(ids_loaded[c], 16 * (i + 1))
                for h in range(2):
                    act.wait_ge(down_done, 2 * e + h + 1)
                    act.activation(ys[c][:, h, :], yp[0:HALF, h, :], ACT.Copy,
                                   scale=ids_s[c][:, h, 1:2].bitcast(F32)).then_inc(y_done, 1)
                if exists(e, 2):
                    xhi(e + 2, c)

            over_experts(act, body)

        @block.vector
        def _(dve):
            def g_part(e, c):
                dve.wait_ge(gu_high, e + 1)
                dve.tensor_tensor(gu_lo[c][:, 0], raw_gu[c][:, 0], gu_hi[c][:, 0].bitcast(F32), ALU.subtract
                                  ).then_inc(g_low, 1)

            def dn_part(e, c):
                dve.wait_ge(dn_high, e + 1)
                dve.tensor_tensor(dn_lo[c][:], raw_dn[c][:], dn_hi[c][:].bitcast(F32), ALU.subtract
                                  ).then_inc(dn_low, 1)

            def xlo(e, c):
                dve.wait_ge(xhi_done, e + 1)
                dve.tensor_tensor(xt[c][:, :, 1, :].rearrange("p (a b) s -> p a b s", b=2),
                                  tpe[:, :, 0:C2].rearrange("p a (b s) -> p a b s", b=2),
                                  xt[c][:, :, 0, :].bitcast(F32).rearrange("p (a b) s -> p a b s", b=2), ALU.subtract
                                  ).then_inc(xlo_done, 1)

            def add(e, it):
                dve.wait_ge(low_copied, 2 * e + it + 1)
                dve.tensor_tensor(gu_sum[:, it], gup[it][:, :, 0:CAP], gu_low[:, it], ALU.add).then_inc(summed, 1)

            def hidden(e, c):
                for it in range(IT):
                    dve.wait_ge(silu_done, 2 * e + it + 1)
                    dve.tensor_tensor(hid_e[:, it], silu_e[:, it], gu_sum[:, it, 1], ALU.mult).then_inc(hid_done, 1)
                for it in range(IT):
                    dve.wait_ge(hhi_done, 2 * e + it + 1)
                    dve.tensor_tensor(he_lo[c][:, it], hid_e[:, it], he_hi[c][:, it].bitcast(F32), ALU.subtract
                                      ).then_inc(hlo_done, 1)

            g_part(0, 0)
            g_part(1, 1)
            xlo(0, 0)
            for it in range(IT):
                add(0, it)
            xlo(1, 1)
            hidden(0, 0)
            dn_part(0, 0)

            def body(e, i, u):
                c, d = u, 1 - u
                if exists(e, 2):
                    g_part(e + 2, c)
                if exists(e, 1):
                    add(e + 1, 0)
                    dn_part(e + 1, d)
                    add(e + 1, 1)
                    hidden(e + 1, d)
                if exists(e, 2):
                    xlo(e + 2, c)

            over_experts(dve, body)

        @block.tensor
        def _(pe):
            def turn(e, c, uses):
                pe.wait_ge(gathered[c], 32 * uses)
                for k in range(KT):
                    for h in range(2):
                        at = (k % 2) * CAP + h * HALF
                        last = pe.transpose(tpe[:, k // 2, at:at + HALF], xs[c][:, h, k:D:KT], ident[0:HALF, 0:HALF])
                last.then_inc(tr_done, 1)

            def gate_up(e, c, it):
                for j in range(2):
                    for k in range(KT):
                        at = slice(it, I, IT)
                        pe.matmul(gup[it][:, j, 0:C2], gu_hi[c][:, j, k, at], xt[c][:, k].rearrange("p a s -> p (a s)"),
                                  start=(k == 0), stop=False, skip_group_check=True)
                        last = pe.matmul(gup[it][:, j, 0:CAP], gu_lo[c][:, j, k, at], xt[c][:, k, 0],
                                         start=False, stop=(k == KT - 1), skip_group_check=True)
                last.then_inc(gu_done, 1)

            def down(c):
                for h in range(2):
                    at = slice(h * HALF, (h + 1) * HALF)
                    for it in range(IT):
                        for q, (hp, w) in enumerate(((he_hi, dn_hi), (he_lo, dn_hi), (he_hi, dn_lo))):
                            last = pe.matmul(yp[0:HALF, h, :], hp[c][:, it, at], w[c][:, it, :],
                                             start=(it == 0 and q == 0), stop=(it == IT - 1 and q == 2))
                    last.then_inc(down_done, 1)

            def gu_ready(e):
                pe.wait_ge(xlo_done, e + 1)
                pe.wait_ge(g_low, e + 1)
                pe.wait_ge(u_low, e + 1)

            turn(0, 0, 1)
            gu_ready(0)
            for it in range(IT):
                gate_up(0, 0, it)
            turn(1, 1, 1)

            def body(e, i, u):
                c, d = u, 1 - u
                if exists(e, 1):
                    gu_ready(e + 1)
                    for it in range(IT):
                        pe.wait_ge(summed, 2 * e + it + 1)
                        gate_up(e + 1, d, it)
                pe.wait_ge(hlo_done, 2 * e + 2)
                pe.wait_ge(dn_low, e + 1)
                pe.wait_ge(y_done, 2 * e)
                down(c)
                if exists(e, 2):
                    pe.wait_ge(xlo_done, e + 2)
                    turn(e + 2, c, i + 2)

            over_experts(pe, body)


def attention_phase(nc, consts, w_hi, w_lo, xT_hi, xT_lo, xT, x, acc_rows, qkv_b, out_b, out):
    ident, = consts
    K3 = 3 * HD
    K5 = K3 + 2
    NP = TT // 2
    UNITS = B * H
    VW = 3 * HD
    VB = 5
    SCALE = 1.0 / float(HD) ** 0.5

    with ExitStack() as ctx:
        def sb(name, shape, dt=F32):
            return ctx.enter_context(nc.sbuf_tensor(name, shape, dt))

        def pb(name, shape):
            return ctx.enter_context(nc.psum_tensor(name, shape, F32))

        def sem(name):
            return ctx.enter_context(nc.semaphore(name))

        qk_bias = sb("qk_bias", [P, 2, G])
        v_bias = sb("v_bias", [P, D])
        o_bias = sb("o_bias", [P, D])
        qk_hi = [sb(f"{a}_hi", [P, S], F32R) for a in "qk"]
        qk_lo = [sb(f"{a}_lo", [P, S], F32R) for a in "qk"]
        stack = [[sb(f"{a}_stack{i}", [K5, GH, S], F32R) for i in range(2)] for a in "qk"]
        v_sum = sb("v_sum", [P, 2 * P])
        v_cols = [sb(f"v_cols{i}", [P, TT, GH, VB, HD], F32R) for i in range(2)]
        neg_max = [sb(f"neg_max{i}", [P, 2, TT]) for i in range(2)]
        neg_hi = [sb(f"neg_hi{i}", [2 * TT, P], F32R) for i in range(2)]
        neg_lo = [sb(f"neg_lo{i}", [2 * TT, P], F32R) for i in range(2)]
        probs = [sb(f"probs{i}", [P, 2, S]) for i in range(NP)]
        p_hi = [sb(f"p_hi{i}", [P, 2, S], F32R) for i in range(NP)]
        p_lo = [sb(f"p_lo{i}", [P, 2, S], F32R) for i in range(NP)]
        ctx_low = sb("ctx_low", [HD, S])
        ctx_sum = sb("ctx_sum", [P, S])
        norm = sb("norm", [P, S])
        ctx_hi = sb("ctx_hi", [P, G, S], F32R)
        ctx_lo = sb("ctx_lo", [P, G, S], F32R)
        gate = sb("gate", [P, TT, D])
        att = sb("att", [P, D])
        xin = [sb(f"x_in{i}", [P, D]) for i in range(2)]

        sc = [pb(f"sc{i}", [P, 2, S]) for i in range(NP)]
        mx = pb("mx", [P, 2, S])
        pv = pb("pv", [P, S])
        aux = pb("aux", [P, S])

        bias_loaded = sem("c_bias_loaded")
        ones_set = sem("c_ones_set")
        x_turned = sem("c_x_turned")
        aux_done = sem("c_aux_done")
        aux_high = sem("c_aux_high")
        aux_read = sem("c_aux_read")
        v_high = sem("c_v_high")
        v_low = sem("c_v_low")
        stacked = [sem(f"c_stacked{i}") for i in range(2)]
        neg_stacked = [sem(f"c_neg_stacked{i}") for i in range(2)]
        mx_done = sem("c_mx_done")
        mx_read = sem("c_mx_read")
        sc_done = sem("c_sc_done")
        exp_done = sem("c_exp_done")
        phi_done = sem("c_phi_done")
        plo_done = sem("c_plo_done")
        pv_done = sem("c_pv_done")
        log_done = sem("c_log_done")
        low_copied = sem("c_low_copied")
        ctx_added = sem("c_ctx_added")
        inv_done = sem("c_inv_done")
        nrm_done = sem("c_nrm_done")
        chi_done = sem("c_chi_done")
        clo_done = sem("c_clo_done")
        acc_loaded = sem("c_acc_loaded")
        xin_loaded = [sem(f"c_xin_loaded{i}") for i in range(2)]
        gate_done = sem("c_gate_done")
        att_done = sem("c_att_done")
        y_done = sem("c_y_done")
        y_stored = sem("c_y_stored")

        x_v = x.rearrange("(b t p) d -> b p t d", p=P, t=TT)
        acc_v = acc_rows[0:T, :].rearrange("(b t p) d -> b p t d", p=P, t=TT)
        out_v = out.rearrange("(b t p) d -> b p t d", p=P, t=TT)

        def rows(h, part):
            part = 2 - part if h % 2 else part
            return slice(part * HD, (part + 1) * HD)

        def extra(b, j):
            if j % 2:
                return not (isinstance(b, int) and b == B - 1 and j == 3)
            return j == 0 and not (isinstance(b, int) and b == 0)

        def last_step(b, j):
            return isinstance(b, int) and b == B - 1 and j == G - 1

        def aux_before(b, j):
            if j == 0:
                return 8 if isinstance(b, int) and b == 0 else 28 * b + 4
            return 28 * b + (12, 20, 24)[j - 1] - (1 if last_step(b, j) else 0)

        def high_before(b, j):
            return 4 * (G * b + j) + 4 - (1 if last_step(b, j) else 0)

        def follows(b, j, ahead):
            return not isinstance(b, int) or G * b + j + ahead < G * B

        def over_groups(engine, step):
            step(0, 0)
            with engine.Fori(0, B - 1) as b:
                for j in (1, 2, 3):
                    step(b, j)
                step(b + 1, 0)
            for j in (1, 2, 3):
                step(B - 1, j)

        block = ctx.enter_context(nc.Block())

        @block.sync
        def _(sp):
            def stack_up(a, item, g2, heads):
                sp.wait_ge(aux_read, item + 1)
                for h in heads:
                    rows = slice(h * HD, (h + 1) * HD)
                    parts = (qk_hi, qk_lo, qk_hi) if a == 0 else (qk_hi, qk_hi, qk_lo)
                    for n, part in enumerate(parts):
                        sp.dma_start(stack[a][g2][n * HD:(n + 1) * HD, h, :].bitcast(F32),
                                     part[a][rows, :].bitcast(F32)).then_inc(stacked[h // 2], 16)

            def stack_max(pair, item, g2):
                sp.wait_ge(aux_read, item + 1)
                for n, part in enumerate((neg_hi, neg_lo)):
                    sp.dma_start(stack[0][g2][K3 + n:K3 + n + 1, 2 * pair:2 * pair + 2, :].bitcast(F32)
                                 .rearrange("o h (t s) -> o (h t) s", s=P), part[pair][:].bitcast(F32)
                                 ).then_inc(neg_stacked[pair], 16)

            def load_late(b):
                for tt in range(2, TT):
                    sp.wait_ge(y_done, TT * b + tt - 1)
                    sp.dma_start(xin[tt % 2][:], x_v[b, :, tt]).then_inc(xin_loaded[tt % 2], 16)

            for n in range(2):
                sp.dma_start(qk_bias[:, n, :], qkv_b[n * D:(n + 1) * D].rearrange("(c p) -> p c", p=P), allow_slow_non_contiguous=True
                             ).then_inc(bias_loaded, 16)
            sp.dma_start(v_bias[:], qkv_b[2 * D:3 * D].rearrange("(a e) -> a e", a=1).to_broadcast([P, D])
                         ).then_inc(bias_loaded, 16)
            sp.dma_start(o_bias[:], out_b.rearrange("(a e) -> a e", a=1).to_broadcast([P, D])
                         ).then_inc(bias_loaded, 16)
            stack_up(0, 0, 0, range(GH))
            stack_up(1, 1, 0, range(GH))
            stack_max(0, 6, 0)
            stack_up(0, 7, 1, range(GH))

            def step(b, j):
                g = G * b + j
                base = aux_before(b, j)
                more = 4 if extra(b, j) else 0
                stack_max(1, base, j % 2)
                if follows(b, j, 1):
                    stack_up(1, base + 1, (j + 1) % 2, range(GH))
                if j == 1:
                    sp.wait_ge(y_stored, 16 * b)
                    sp.dma_start(gate[:], acc_v[b]).then_inc(acc_loaded, 16)
                    for tt in range(2):
                        sp.dma_start(xin[tt][:], x_v[b, :, tt]).then_inc(xin_loaded[tt], 16)
                if j == 2 and follows(b, j, 2):
                    sp.dma_start(xT_hi[:].bitcast(F32), xT[b + 1, 0].rearrange("p (k s) -> p k s", k=KT)
                                 ).then_inc(x_turned, 16)
                    sp.dma_start(xT_lo[:].bitcast(F32), xT[b + 1, 1].rearrange("p (k s) -> p k s", k=KT)
                                 ).then_inc(x_turned, 16)
                if follows(b, j, 1):
                    stack_max(0, base + 2 + more // 2, (j + 1) % 2)
                if j == 0 and more:
                    load_late(b - 1)
                if follows(b, j, 2):
                    stack_up(0, base + 3 + more, j % 2, range(GH))
                if j == 0 and more:
                    sp.wait_ge(y_done, TT * b)
                    sp.dma_start(out_v[b - 1], gate[:]).then_inc(y_stored, 16)

            over_groups(sp, step)
            load_late(B - 1)
            sp.wait_ge(y_done, TT * B)
            sp.dma_start(out_v[B - 1], gate[:]).then_inc(y_stored, 16)
            sp.wait_ge(y_stored, 16 * B)

        @block.scalar
        def _(act):
            nc.scalar.preload_act_table_set("natural_log_exp_and_others")

            def qk_high(a, item, high, g, c):
                act.wait_ge(aux_done, item + 1)
                for pair in range(2):
                    act.wait_ge(stacked[pair], 16 * 2 * K3 // HD * 2 * g)
                act.activation(qk_hi[a][:], aux[:], ACT.Identity, bias=qk_bias[:, a, c:c + 1]).then_inc(aux_high, 1)

            def max_high(pair, item, g):
                act.wait_ge(aux_done, item + 1)
                act.wait_ge(neg_stacked[pair], 32 * g)
                act.activation(neg_hi[pair][:], aux[0:2 * TT, 0:P], ACT.Copy).then_inc(aux_high, 1)

            def v_split(item, c, s):
                act.wait_ge(aux_read, item + 1)
                act.activation(v_cols[c][:, s, :, 0:VB:VB - 1, :],
                               v_sum[:].rearrange("p (h o d) -> p h o d", h=GH, o=2), ACT.Copy).then_inc(v_high, 1)

            def exponentials(unit, pair):
                act.wait_ge(sc_done, 2 * unit + pair + 1)
                if not isinstance(unit, int) or unit > 0:
                    act.wait_ge(plo_done, 2 * unit + pair - 1)
                act.activation(probs[pair][:], sc[pair][:], ACT.Exp, scale=SCALE).then_inc(exp_done, 1)

            def head_out(unit, g, h):
                act.wait_ge(pv_done, 2 * unit + 2)
                if h == 0:
                    act.wait_ge(clo_done, g)
                act.activation(norm[h * HD:(h + 1) * HD, :], pv[rows(h, 2), :], ACT.Ln).then_inc(log_done, 1)
                act.wait_ge(ctx_added, unit)
                act.activation(ctx_low[:], pv[rows(h, 1), :], ACT.Copy).then_inc(low_copied, 1)

            def invert(g):
                act.wait_ge(log_done, GH * (g + 1))
                act.activation(norm[:], norm[:], ACT.Exp, scale=-1.0).then_inc(inv_done, 1)

            def ctx_high(g, c):
                act.wait_ge(nrm_done, g + 1)
                act.activation(ctx_hi[:, c, :], norm[:], ACT.Copy).then_inc(chi_done, 1)

            act.wait_ge(bias_loaded, 64)
            qk_high(0, 0, 0, 0, 0)
            qk_high(1, 1, 1, 0, 0)
            for s in range(TT):
                v_split(2 + s, 0, s)
            max_high(0, 6, 0)
            qk_high(0, 7, 3, 1, 1)

            def step(b, j):
                g = G * b + j
                base = aux_before(b, j)
                more = 4 if extra(b, j) else 0
                first = isinstance(b, int) and g == 0
                for h in range(GH):
                    unit = GH * g + h
                    if h == 0:
                        max_high(1, base, g)
                    if h >= 2 or not first:
                        head_out(unit - 2, g if h >= 2 else g - 1, (h - 2) % GH)
                    if h == 1 and not first:
                        invert(g - 1)
                    exponentials(unit, 0)
                    if h == 0 and follows(b, j, 1):
                        qk_high(1, base + 1, None, g + 1, (j + 1) % G)
                    if h == 1 and not first:
                        ctx_high(g - 1, (j - 1) % G)
                    if h == 3 and follows(b, j, 1):
                        max_high(0, base + 2 + more // 2, g + 1)
                    if j % 2 and more and h >= 1:
                        v_split(base + (2, 3, 5)[h - 1], (j + 1) // 2 % 2, h - 1)
                    exponentials(unit, 1)
                    if j % 2 and more and h == 3:
                        v_split(base + 6, (j + 1) // 2 % 2, 3)
                    if h == 3 and follows(b, j, 2):
                        qk_high(0, base + 3 + more, None, g + 2, (j + 2) % G)
                if j == 3:
                    act.wait_ge(acc_loaded, 16 * (b + 1))
                    act.activation(gate[:], gate[:], ACT.Silu).then_inc(gate_done, 1)
                    nc.scalar.preload_act_table_set("natural_log_exp_and_others")

            over_groups(act, step)
            head_out(UNITS - 2, G * B - 1, 2)
            head_out(UNITS - 1, G * B - 1, 3)
            invert(G * B - 1)
            ctx_high(G * B - 1, G - 1)

        @block.vector
        def _(dve):
            def qk_low(a, item, high, c):
                dve.wait_ge(aux_high, high + 1)
                dve.scalar_tensor_tensor(qk_lo[a][:], aux[:], qk_bias[:, a, c:c + 1], qk_hi[a][:].bitcast(F32),
                                         ALU.add, ALU.subtract).then_inc(aux_read, 1)

            def max_low(pair, item, high):
                dve.wait_ge(aux_high, high + 1)
                dve.tensor_tensor(neg_lo[pair][:], aux[0:2 * TT, 0:P], neg_hi[pair][:].bitcast(F32), ALU.subtract
                                  ).then_inc(aux_read, 1)

            def v_make(n, item, half):
                dve.wait_ge(aux_done, item + 1)
                dve.wait_ge(v_low, n)
                dve.tensor_tensor(v_sum[:], aux[:, 0:2 * P], v_bias[:, half * 2 * P:(half + 1) * 2 * P], ALU.add
                                  ).then_inc(aux_read, 1)

            def v_make_low(n, c, s):
                dve.wait_ge(v_high, n + 1)
                dve.tensor_tensor(v_cols[c][:, s, :, 1:VB - 1:2, :],
                                  v_sum[:].rearrange("p (h o d) -> p h o d", h=GH, o=2),
                                  v_cols[c][:, s, :, 0:VB:VB - 1, :].bitcast(F32), ALU.subtract).then_inc(v_low, 1)

            def maxima(index, pair, h, tp):
                dve.wait_ge(mx_done, index + 1)
                dve.tensor_reduce(neg_max[pair][:, h % 2, 2 * tp:2 * tp + 2], mx[:], AX.X, ALU.max, negate=True
                                  ).then_inc(mx_read, 1)

            def head_maxima(g, h):
                for tp in range(NP):
                    maxima(2 * GH * g + 2 * h + tp, h // 2, h, tp)

            def high_probs(unit, pair):
                dve.wait_ge(exp_done, 2 * unit + pair + 1)
                if not isinstance(unit, int) or unit > 0:
                    dve.wait_ge(pv_done, 2 * unit + pair - 1)
                dve.tensor_copy(p_hi[pair][:], probs[pair][:]).then_inc(phi_done, 1)

            def head_out(unit, g, h):
                dve.wait_ge(low_copied, unit + 1)
                if h == 0:
                    dve.wait_ge(nrm_done, g)
                dve.tensor_tensor(ctx_sum[h * HD:(h + 1) * HD, :], pv[rows(h, 0), :], ctx_low[:], ALU.add
                                  ).then_inc(ctx_added, 1)

            def normalise(g):
                dve.wait_ge(inv_done, g + 1)
                dve.wait_ge(ctx_added, GH * (g + 1))
                dve.tensor_tensor(norm[:], norm[:], ctx_sum[:], ALU.mult).then_inc(nrm_done, 1)

            def ctx_low_part(g, c):
                dve.wait_ge(chi_done, g + 1)
                dve.tensor_tensor(ctx_lo[:, c, :], norm[:], ctx_hi[:, c, :].bitcast(F32), ALU.subtract
                                  ).then_inc(clo_done, 1)

            def output(b, tt, item):
                dve.wait_ge(aux_done, item + 1)
                dve.wait_ge(att_done, TT * b + tt)
                dve.tensor_tensor(att[:], aux[:], o_bias[:], ALU.add).then_inc(aux_read, 1)
                if tt == 0:
                    dve.wait_ge(gate_done, b + 1)
                dve.wait_ge(aux_read, item + 1)
                dve.tensor_tensor(gate[:, tt, :], att[:], gate[:, tt, :], ALU.mult).then_inc(att_done, 1)

            dve.wait_ge(bias_loaded, 64)
            qk_low(0, 0, 0, 0)
            qk_low(1, 1, 1, 0)
            for s in range(TT):
                v_make(s, 2 + s, 0)
                v_make_low(s, 0, s)
            for h in range(GH):
                head_maxima(0, h)
            max_low(0, 6, 2)
            qk_low(0, 7, 3, 1)

            def step(b, j):
                g = G * b + j
                base = aux_before(b, j)
                high = high_before(b, j)
                more = 4 if extra(b, j) else 0
                first = isinstance(b, int) and g == 0
                vn = 4 + 8 * b + (0 if j == 1 else 4)
                vc = (j + 1) // 2 % 2

                def v_tile(s, item):
                    v_make(vn + s, item, vc)
                    v_make_low(vn + s, vc, s)

                for h in range(GH):
                    unit = GH * g + h
                    if h == 0:
                        max_low(1, base, high)
                    if h >= 2 or not first:
                        head_out(unit - 2, g if h >= 2 else g - 1, (h - 2) % GH)
                    if h == 1 and not first:
                        normalise(g - 1)
                    if h == 0 and follows(b, j, 1):
                        qk_low(1, base + 1, high + 1, (j + 1) % G)
                    if h == 1 and not first:
                        ctx_low_part(g - 1, (j - 1) % G)
                    if h == 3 and follows(b, j, 1):
                        max_low(0, base + 2 + more // 2, high + 2)
                    if h >= 2 and follows(b, j, 1):
                        head_maxima(g + 1, 2 * (h - 2))
                    if j % 2 and more and h >= 1:
                        v_tile(h - 1, base + (2, 3, 5)[h - 1])
                    if j == 0 and more and h >= 2:
                        output(b - 1, 2 * (h - 2), base + (2, 5)[h - 2])
                    high_probs(unit, 0)
                    if j % 2 and more and h == 3:
                        v_tile(3, base + 6)
                    if j == 0 and more and h >= 2:
                        output(b - 1, 2 * (h - 2) + 1, base + (3, 6)[h - 2])
                    if h >= 2 and follows(b, j, 1):
                        head_maxima(g + 1, 2 * (h - 2) + 1)
                    if h == 3 and follows(b, j, 2):
                        qk_low(0, base + 3 + more, high + 3, (j + 2) % G)
                    high_probs(unit, 1)

            over_groups(dve, step)
            head_out(UNITS - 2, G * B - 1, 2)
            head_out(UNITS - 1, G * B - 1, 3)
            normalise(G * B - 1)
            ctx_low_part(G * B - 1, G - 1)
            for tt in range(TT):
                output(B - 1, tt, aux_before(B - 1, 3) + 1 + tt)

        @block.gpsimd
        def _(pool):
            for i in range(2):
                pool.memset(stack[1][i][K3:K5, :, :].bitcast(F32), 1.0).then_inc(ones_set, 1)
                pool.wait_ge(ones_set, 2 * i + 1)
                pool.memset(v_cols[i][:, :, :, 2, :].bitcast(F32), 1.0).then_inc(ones_set, 1)
                pool.wait_ge(ones_set, 2 * i + 2)

            def low_probs(unit, pair):
                pool.wait_ge(phi_done, 2 * unit + pair + 1)
                pool.tensor_tensor(p_lo[pair][:], probs[pair][:], p_hi[pair][:].bitcast(F32), ALU.subtract
                                   ).then_inc(plo_done, 1)

            def result(b, tt):
                pool.wait_ge(att_done, TT * b + tt + 1)
                pool.wait_ge(xin_loaded[tt % 2], 16 * (2 * b + tt // 2 + 1))
                pool.tensor_tensor(gate[:, tt, :], gate[:, tt, :], xin[tt % 2][:], ALU.add).then_inc(y_done, 1)

            def step(b, j):
                g = G * b + j
                for h in range(GH):
                    unit = GH * g + h
                    low_probs(unit, 0)
                    if j == 0 and extra(b, j) and h == 3:
                        result(b - 1, 1)
                    low_probs(unit, 1)
                    if j == 0 and extra(b, j) and h == 2:
                        result(b - 1, 0)
                    if j == 0 and extra(b, j) and h == 3:
                        result(b - 1, 2)
                        result(b - 1, 3)

            over_groups(pool, step)
            for tt in range(TT):
                result(B - 1, tt)

        @block.tensor
        def _(pe):
            def aux_free(item):
                if not isinstance(item, int) or item > 0:
                    pe.wait_ge(aux_read, item)

            def turned_product(a, c, item):
                aux_free(item)
                cols = slice(a * D + c * P, a * D + (c + 1) * P)
                for k in range(KT):
                    for q, (w, xt) in enumerate(((w_hi, xT_hi), (w_lo, xT_hi), (w_hi, xT_lo))):
                        last = pe.matmul(aux[:], w[:, k, cols], xt[:, k, :],
                                         start=(k == 0 and q == 0), stop=(k == KT - 1 and q == 2))
                last.then_inc(aux_done, 1)

            def v_product(half, s, item):
                aux_free(item)
                cols = slice(2 * D + half * 2 * P, 2 * D + (half + 1) * 2 * P)
                for k in range(KT):
                    for q, (xt, w) in enumerate(((xT_hi, w_hi), (xT_lo, w_hi), (xT_hi, w_lo))):
                        last = pe.matmul(aux[:, 0:2 * P], xt[:, k, s * P:(s + 1) * P], w[:, k, cols],
                                         start=(k == 0 and q == 0), stop=(k == KT - 1 and q == 2))
                last.then_inc(aux_done, 1)

            def turn_maxima(g, pair, item):
                aux_free(item)
                pe.wait_ge(mx_read, 2 * GH * g + GH * (pair + 1))
                pe.transpose(aux[0:2 * TT, 0:P], neg_max[pair][:].rearrange("p h t -> p (h t)"), ident[:]
                             ).then_inc(aux_done, 1)

            def scores_for_max(g, g2, h):
                if h % 2 == 0:
                    pe.wait_ge(stacked[h // 2], 16 * 4 * K3 // HD * (g + 1))
                for tp in range(NP):
                    index = 2 * GH * g + 2 * h + tp
                    if not isinstance(index, int) or index > 0:
                        pe.wait_ge(mx_read, index)
                    for n in range(2):
                        at = slice((2 * tp + n) * P, (2 * tp + n + 1) * P)
                        last = pe.matmul(mx[:, n, :], stack[0][g2][0:K3, h, at], stack[1][g2][0:K3, h, :],
                                         start=True, stop=True)
                    last.then_inc(mx_done, 1)

            def scores(unit, g, g2, h, pair):
                if pair == 0 and h % 2 == 0:
                    pe.wait_ge(neg_stacked[h // 2], 32 * (g + 1))
                if not isinstance(unit, int) or unit > 0:
                    pe.wait_ge(exp_done, 2 * unit + pair - 1)
                for n in range(2):
                    at = slice((2 * pair + n) * P, (2 * pair + n + 1) * P)
                    last = pe.matmul(sc[pair][:, n, :], stack[1][g2][:, h, at], stack[0][g2][:, h, :],
                                     start=True, stop=True)
                last.then_inc(sc_done, 1)

            def weigh_values(unit, c, h, pair):
                pe.wait_ge(plo_done, 2 * unit + pair + 1)
                if pair == 0:
                    pe.wait_ge(ctx_added, unit)
                first = 2 * (h % 2)
                for n in range(2):
                    for q, part in enumerate((p_hi, p_lo)):
                        last = pe.matmul(pv[0:VW, :], v_cols[c // 2][:, 2 * pair + n, (c % 2) * 2 + h // 2, first:first + 3, :]
                                         .rearrange("p b d -> p (b d)"),
                                         part[pair][:, n, :], start=(pair == 0 and n == 0 and q == 0),
                                         stop=(pair == 1 and n == 1 and q == 1))
                last.then_inc(pv_done, 1)

            def out_product(b, tt, item):
                aux_free(item)
                if tt == 0:
                    pe.wait_ge(clo_done, G * (b + 1))
                for k in range(KT):
                    for q, (cp, w) in enumerate(((ctx_hi, w_hi), (ctx_lo, w_hi), (ctx_hi, w_lo))):
                        last = pe.matmul(aux[:], cp[:, k, tt * P:(tt + 1) * P], w[:, k, 3 * D:4 * D],
                                         start=(k == 0 and q == 0), stop=(k == KT - 1 and q == 2))
                last.then_inc(aux_done, 1)

            pe.wait_ge(ones_set, 4)
            turned_product(0, 0, 0)
            turned_product(1, 0, 1)
            for s in range(TT):
                v_product(0, s, 2 + s)
            for h in range(GH):
                scores_for_max(0, 0, h)
            turn_maxima(0, 0, 6)
            turned_product(0, 1, 7)

            def step(b, j):
                g = G * b + j
                base = aux_before(b, j)
                more = 4 if extra(b, j) else 0
                first = isinstance(b, int) and g == 0
                vc = (j + 1) // 2 % 2
                for h in range(GH):
                    unit = GH * g + h
                    if h == 0:
                        turn_maxima(g, 1, base)
                    scores(unit, g, j % 2, h, 0)
                    if h == 0 and follows(b, j, 1):
                        turned_product(1, (j + 1) % G, base + 1)
                    if h == 3 and follows(b, j, 1):
                        turn_maxima(g + 1, 0, base + 2 + more // 2)
                    if h >= 2 and follows(b, j, 1):
                        scores_for_max(g + 1, (j + 1) % 2, 2 * (h - 2))
                    if j % 2 and more and h >= 1:
                        if h == 1:
                            if j == 3:
                                pe.wait_ge(x_turned, 32 * (b + 1))
                        v_product(vc, h - 1, base + (2, 3, 5)[h - 1])
                    if j == 0 and more and h >= 2:
                        out_product(b - 1, 2 * (h - 2), base + (2, 5)[h - 2])
                    if h > 0 or not first:
                        weigh_values(unit - 1, j if h > 0 else (j - 1) % G, (h - 1) % GH, 0)
                    scores(unit, g, j % 2, h, 1)
                    if j % 2 and more and h == 3:
                        v_product(vc, 3, base + 6)
                    if j == 0 and more and h >= 2:
                        out_product(b - 1, 2 * (h - 2) + 1, base + (3, 6)[h - 2])
                    if h >= 2 and follows(b, j, 1):
                        scores_for_max(g + 1, (j + 1) % 2, 2 * (h - 2) + 1)
                    if h == 3 and follows(b, j, 2):
                        if j == 2:
                            pe.wait_ge(x_turned, 32 * (b + 1))
                        turned_product(0, (j + 2) % G, base + 3 + more)
                    if h > 0 or not first:
                        weigh_values(unit - 1, j if h > 0 else (j - 1) % G, (h - 1) % GH, 1)

            over_groups(pe, step)
            for pair in range(NP):
                weigh_values(UNITS - 1, G - 1, GH - 1, pair)
            for tt in range(TT):
                out_product(B - 1, tt, aux_before(B - 1, 3) + 1 + tt)


def recurrent_moe_attention_kernel(nc: bass.Bass, x: bass.AP, qkv_wT: bass.AP, qkv_b: bass.AP, out_wT: bass.AP,
                                   out_b: bass.AP, router_wT: bass.AP, e_bias: bass.AP, W_gate: bass.AP,
                                   W_up: bass.AP, W_down: bass.AP, gateT: bass.AP, upT: bass.AP, downT: bass.AP,
                                   out: bass.AP):
    def scratch(name, shape, dt=F32):
        return nc.dram_tensor(name, shape, dt, kind="Internal").ap()

    xn_rows = scratch("xn_rows", [ROWS, D])
    acc_rows = scratch("acc_rows", [ROWS, D])
    table = scratch("slot_table", [SLOTS, 2], I32)
    wb_hi = scratch("wb_hi", [D, 4 * D])
    wb_lo = scratch("wb_lo", [D, 4 * D])
    xT = scratch("xT", [B, 2, P, KT * S])

    with ExitStack() as ctx:
        ident = ctx.enter_context(nc.sbuf_tensor("ident", [P, P], F32))
        tokens_phase(nc, (ident,), x, router_wT, e_bias, gateT, upT, downT, qkv_wT, out_wT,
                     xn_rows, acc_rows, table, wb_hi, wb_lo, xT)

        w_hi = ctx.enter_context(nc.sbuf_tensor("w_hi", [P, KT, 4 * D], F32R))
        w_lo = ctx.enter_context(nc.sbuf_tensor("w_lo", [P, KT, 4 * D], F32R))
        xT_hi = ctx.enter_context(nc.sbuf_tensor("xT_hi", [P, KT, S], F32R))
        xT_lo = ctx.enter_context(nc.sbuf_tensor("xT_lo", [P, KT, S], F32R))
        next_loaded = ctx.enter_context(nc.semaphore("next_loaded"))

        def load_next(sp):
            for tile, rows in ((w_hi, wb_hi), (w_lo, wb_lo)):
                sp.dma_start(tile[:].bitcast(F32), rows.rearrange("(k p) n -> p k n", p=P)).then_inc(next_loaded, 16)
            for part, tile in enumerate((xT_hi, xT_lo)):
                sp.dma_start(tile[:].bitcast(F32), xT[0, part].rearrange("p (k s) -> p k s", k=KT)
                             ).then_inc(next_loaded, 16)

        def wait_next(sp):
            sp.wait_ge(next_loaded, 64)

        experts_phase(nc, (ident,), W_gate, W_up, W_down, xn_rows, acc_rows, table, load_next, wait_next)
        attention_phase(nc, (ident,), w_hi, w_lo, xT_hi, xT_lo, xT, x, acc_rows, qkv_b, out_b, out)


def kernel(**inputs):
    import numpy as _np
    import concourse.bacc as _bacc
    from concourse import mybir as _mybir
    from concourse.bass_utils import run_bass_kernel_spmd as _run

    attn = {n: inputs["L0_attn_" + n] for n in ("hidden_states", "Wqkv_w", "Wqkv_b", "out_w", "out_b")}
    ffn = {n: inputs["L0_ffn_" + n] for n in ("router_w", "e_bias", "W_gate", "W_up", "W_down",
                                              "shared_gate", "shared_up", "shared_down")}
    laid_out = (
        ("x", attn["hidden_states"].reshape(T, D)),
        ("qkv_wT", attn["Wqkv_w"].T), ("qkv_b", attn["Wqkv_b"]),
        ("out_wT", attn["out_w"].T), ("out_b", attn["out_b"]),
        ("router_wT", ffn["router_w"].T), ("e_bias", ffn["e_bias"]),
        ("W_gate", ffn["W_gate"]), ("W_up", ffn["W_up"]), ("W_down", ffn["W_down"]),
        ("gateT", ffn["shared_gate"].T), ("upT", ffn["shared_up"].T), ("downT", ffn["shared_down"].T),
    )
    nc = _bacc.Bacc("TRN2", target_bir_lowering=False, num_devices=1)
    arrays, args = {}, []
    for name, a in laid_out:
        a = _np.ascontiguousarray(a)
        arrays[f"in_{name}_dram"] = a
        args.append(nc.dram_tensor(f"in_{name}_dram", a.shape, _mybir.dt.from_np(a.dtype), kind="ExternalInput").ap())
    args.append(nc.dram_tensor("out_0_dram", (T, D), _mybir.dt.from_np(_np.dtype("float32")), kind="ExternalOutput").ap())
    recurrent_moe_attention_kernel(nc, *args)
    r = _run(nc, [arrays], core_ids=[0])
    return r.results[0]["out_0_dram"].reshape(B, S, D)
```

```python
import concourse.bass as bass
from concourse import mybir
from contextlib import ExitStack

F32 = mybir.dt.float32
F32R = mybir.dt.float32r
BF16 = mybir.dt.bfloat16
I32 = mybir.dt.int32
U32 = mybir.dt.uint32
ALU = mybir.AluOpType
ACT = mybir.ActivationFunctionType
AX = mybir.AxisListType

P = 128
D = 512
KT = D // P
B, S = 8, 512
T = B * S
TT = S // P
H, HD = 16, 32
GH = P // HD
G = H // GH
E, K, NG, TKG = 32, 4, 8, 3
EG = E // NG
I = 256
IT = I // P
IS = 512
MT = IS // P
ROUTE_SCALE = 2.5
CAP = -(-5 * T // (4 * E))
HALF = CAP // 2
SLOTS = E * CAP
EPS = 1e-5
SENTINEL = 1.0e6
ROWS = T + CAP




def tokens_phase(nc, consts, x, router_wT, e_bias, gateT, upT, downT, qkvT, outT,
                 xn_rows, acc_rows, table, wb_hi, wb_lo, xT):
    ident, = consts
    KC = 29

    with ExitStack() as ctx:
        def sb(name, shape, dt=F32):
            return ctx.enter_context(nc.sbuf_tensor(name, shape, dt))

        def pb(name, shape):
            return ctx.enter_context(nc.psum_tensor(name, shape, F32))

        def sem(name):
            return ctx.enter_context(nc.semaphore(name))

        before = sb("before", [P, P], BF16)
        ones = sb("ones", [P, P], BF16)
        bias_row = sb("bias_row", [P, E])
        slot_base = sb("slot_base", [P, E])
        expert_no = sb("expert_no", [P, E])
        lower_no = sb("lower_no", [P, NG, NG])
        empty = sb("empty", [E, CAP, 2], I32)
        zero_rows = sb("zero_rows", [P, D])
        carrier = sb("carrier", [P, 2])
        rw_raw = sb("rw_raw", [P, KT, E])
        rw_hi = sb("rw_hi", [P, KT, E], F32R)
        rw_lo = sb("rw_lo", [P, KT, E], F32R)
        sw_raw = sb("sw_raw", [P, 2, 3 * IS])
        sw_hi = sb("sw_hi", [P, KT, 3 * IS], F32R)
        sw_lo = sb("sw_lo", [P, KT, 3 * IS], F32R)
        wb_raw = sb("wb_raw", [P, 1024])
        wb_h = sb("wb_h", [P, 1024], F32R)
        wb_l = sb("wb_l", [P, 1024], F32R)
        xin = [sb(f"xin{i}", [P, TT, D]) for i in range(2)]
        xn = [sb(f"xn{i}", [P, TT, D]) for i in range(2)]
        xT_hi = [sb(f"xT_hi{i}", [P, KT, S], F32R) for i in range(2)]
        xT_lo = [sb(f"xT_lo{i}", [P, KT, S], F32R) for i in range(2)]
        stats = sb("stats", [P, TT, 6])
        mv = sb("mv", [P, TT, 2])
        var_eps = sb("var_eps", [P, TT])
        std = sb("std", [P, TT])
        rstd = sb("rstd", [P, TT])
        silu_g = sb("silu_g", [P, 2, S])
        hid = sb("hid", [P, 2, S])
        hid_hi = sb("hid_hi", [P, MT, S], F32R)
        hid_lo = sb("hid_lo", [P, MT, S], F32R)
        ybuf = sb("ybuf", [P, TT, D])
        score = sb("score", [P, TT, E])
        biased = sb("biased", [P, TT, E])
        pair_hi = sb("pair_hi", [P, TT * NG, 2])
        pair_lo = sb("pair_lo", [P, TT * NG, 2])
        top1 = sb("top1", [P, TT * NG])
        low1 = sb("low1", [P, TT * NG])
        low2 = sb("low2", [P, TT * NG])
        top2 = sb("top2", [P, TT * NG])
        gscore = sb("gscore", [P, TT, NG])
        above = sb("above", [P, TT, NG, NG])
        equal = sb("equal", [P, TT, NG, NG])
        rank = sb("rank", [P, TT, NG])
        gmask = sb("gmask", [P, TT, NG])
        masked0 = sb("masked0", [P, TT, E])
        masked = sb("masked", [P, TT, E])
        best = sb("best", [P, TT, 8])
        best_no = sb("best_no", [P, TT, 8], U32)
        best_f = sb("best_f", [P, TT, K])
        onehot = sb("onehot", [P, TT * K, E])
        chosen = sb("chosen", [P, TT, E], BF16)
        onehot_x = sb("onehot_x", [P, TT * K, E])
        weight = sb("weight", [P, TT, K])
        wsum = sb("wsum", [P, TT])
        wsum1 = sb("wsum1", [P, TT])
        wrec = sb("wrec", [P, TT])
        wnorm = sb("wnorm", [P, TT, K])
        carry = sb("carry", [P, E])
        place = sb("place", [P, TT, E])
        over = sb("over", [P, TT, E])
        slot0 = sb("slot0", [P, TT, E])
        slot = sb("slot", [P, TT, E])
        slot_x = sb("slot_x", [P, TT * K, E])
        slot_f = sb("slot_f", [P, TT * K])
        slot_no = sb("slot_no", [P, TT * K], U32)
        token_f = sb("token_f", [P, TT])
        entry = sb("entry", [P, TT, K, 2], I32)

        gu = [pb(f"gu{i}", [P, 2, S]) for i in range(2)]
        tp = pb("tp", [P, 2, S])
        lg = pb("lg", [P, TT, E])
        px = pb("px", [P, TT + 1, E])

        consts_done = sem("a_consts")
        table_set = sem("a_table_set")
        x_loaded = [sem(f"a_x_loaded{i}") for i in range(2)]
        xn_stored = [sem(f"a_xn_stored{i}") for i in range(2)]
        xT_stored = [sem(f"a_xT_stored{i}") for i in range(2)]
        y_stored = sem("a_y_stored")
        sw_loaded = [sem(f"a_sw_loaded{i}") for i in range(2)]
        rw_loaded = sem("a_rw_loaded")
        split_hi = sem("a_split_hi")
        split_lo = sem("a_split_lo")
        wb_loaded = sem("a_wb_loaded")
        wb_split = sem("a_wb_split")
        wb_own = sem("a_wb_own")
        wb_stored = sem("a_wb_stored")
        stat_step = sem("a_stat_step")
        var_ready = sem("a_var_ready")
        std_ready = sem("a_std_ready")
        ln_done = sem("a_ln_done")
        tr_done = sem("a_tr_done")
        xhi_done = sem("a_xhi_done")
        xlo_done = sem("a_xlo_done")
        logits_done = sem("a_logits_done")
        score_done = sem("a_score_done")
        route_step = sem("a_route_step")
        chosen_done = sem("a_chosen_done")
        prefix_done = sem("a_prefix_done")
        entry_done = sem("a_entry_done")
        scattered = sem("a_scattered")
        gu_done = sem("a_gu_done")
        silu_done = sem("a_silu_done")
        hid_done = sem("a_hid_done")
        hhi_done = sem("a_hhi_done")
        hlo_done = sem("a_hlo_done")
        down_done = sem("a_down_done")
        y_copied = sem("a_y_copied")

        x_v = x.rearrange("(b t p) d -> b p t d", p=P, t=TT)
        xn_v = xn_rows[0:T, :].rearrange("(b t p) d -> b p t d", p=P, t=TT)
        acc_v = acc_rows[0:T, :].rearrange("(b t p) d -> b p t d", p=P, t=TT)

        block = ctx.enter_context(nc.Block())

        @block.sync
        def _(sp):
            sp.dma_start(xin[0][:], x_v[0]).then_inc(x_loaded[0], 16)
            sp.dma_start(rw_raw[:], router_wT.rearrange("(k p) e -> p k e", p=P)).then_inc(rw_loaded, 16)
            sp.dma_start(bias_row[:], e_bias.rearrange("(a e) -> a e", a=1).to_broadcast([P, E])
                         ).then_inc(rw_loaded, 16)
            for k in range(KT):
                if k >= 2:
                    sp.wait_ge(split_lo, k)
                for j, w in enumerate((gateT, upT, downT)):
                    sp.dma_start(sw_raw[:, k % 2, j * IS:(j + 1) * IS], w[k * P:(k + 1) * P, :]
                                 ).then_inc(sw_loaded[k % 2], 16)
            sp.dma_start(xin[1][:], x_v[1]).then_inc(x_loaded[1], 16)
            with sp.Fori(0, B // 2) as i:
                for u in range(2):
                    n = 2 * i + u
                    c, d = u, 1 - u
                    sp.wait_ge(wb_stored, 32 * n)
                    if u == 0:
                        sp.dma_start(wb_raw[:], qkvT[bass.ts(i, P), 0:1024]).then_inc(wb_loaded, 32)
                    else:
                        sp.dma_start(wb_raw[:, 0:512], qkvT[bass.ts(i, P), 1024:1536]).then_inc(wb_loaded, 16)
                        sp.dma_start(wb_raw[:, 512:1024], outT[bass.ts(i, P), :]).then_inc(wb_loaded, 16)
                    sp.wait_ge(ln_done, n + 1)
                    sp.dma_start(xin[c][:], x_v[(n + 2) % B]).then_inc(x_loaded[c], 16)
                    sp.dma_start(xn_v[n], xn[c][:]).then_inc(xn_stored[c], 16)
                    sp.wait_ge(wb_split, n + 1)
                    sp.dma_start(wb_hi[bass.ts(i, P), u * 1024:(u + 1) * 1024], wb_h[:].bitcast(F32)).then_inc(wb_stored, 16)
                    sp.dma_start(wb_lo[bass.ts(i, P), u * 1024:(u + 1) * 1024], wb_l[:].bitcast(F32)).then_inc(wb_stored, 16)
                    sp.wait_ge(xlo_done, 2 * n + 2)
                    for part, xt in enumerate((xT_hi[c], xT_lo[c])):
                        sp.dma_start(xT[n, part].rearrange("p (k s) -> p k s", k=KT), xt[:].bitcast(F32)
                                     ).then_inc(xT_stored[c], 16)
                    sp.wait_ge(y_copied, TT * (n + 1))
                    sp.dma_start(acc_v[n], ybuf[:]).then_inc(y_stored, 16)
            sp.wait_ge(y_stored, 16 * B)
            sp.wait_ge(wb_stored, 32 * B)
            for c in range(2):
                sp.wait_ge(xn_stored[c], 16 * (B // 2))
                sp.wait_ge(xT_stored[c], 32 * (B // 2))
                sp.wait_ge(x_loaded[c], 16 * (B // 2 + 1))

        @block.gpsimd
        def _(pool):
            pool.memset(ident[:], 0.0).then_inc(wb_own, 1)
            pool.memset(before[:], 0.0).then_inc(wb_own, 1)
            pool.memset(lower_no[:], 0.0).then_inc(wb_own, 1)
            pool.memset(ones[:], 1.0).then_inc(consts_done, 1)
            pool.memset(zero_rows[:], 0.0).then_inc(consts_done, 1)
            pool.memset(carry[:], 0.0).then_inc(consts_done, 1)
            pool.memset(empty[:], 0).then_inc(wb_own, 1)
            pool.wait_ge(wb_own, 4)
            pool.affine_select(out=ident[:], in_=ident[:], compare_op=ALU.not_equal, fill=1.0, base=0,
                               pattern=[[-1, P]], channel_multiplier=1).then_inc(consts_done, 1)
            pool.affine_select(out=before[:], in_=before[:], compare_op=ALU.is_ge, fill=1.0, base=0,
                               pattern=[[-1, P]], channel_multiplier=1).then_inc(consts_done, 1)
            pool.affine_select(out=lower_no[:], in_=lower_no[:], compare_op=ALU.is_ge, fill=1.0, base=0,
                               pattern=[[-1, NG], [1, NG]], channel_multiplier=0).then_inc(consts_done, 1)
            pool.iota(slot_base[:], [[CAP, E]], base=0, channel_multiplier=0,
                      allow_small_or_imprecise_dtypes=True).then_inc(consts_done, 1)
            pool.iota(expert_no[:], [[1, E]], base=0, channel_multiplier=0,
                      allow_small_or_imprecise_dtypes=True).then_inc(consts_done, 1)
            pool.iota(token_f[:], [[P, TT]], base=0, channel_multiplier=1,
                      allow_small_or_imprecise_dtypes=True).then_inc(consts_done, 1)
            pool.iota(empty[:, :, 0], [[1, CAP]], base=T, channel_multiplier=0).then_inc(consts_done, 1)
            pool.wait_ge(consts_done, 10)
            pool.dma_start(table.rearrange("(e s) c -> e s c", e=E), empty[:]).then_inc(table_set, 16)
            for rows in (xn_rows, acc_rows):
                pool.dma_start(rows[T:T + P, :], zero_rows[:]).then_inc(table_set, 16)
                pool.dma_start(rows[T + P:ROWS, :], zero_rows[0:CAP - P, :]).then_inc(table_set, 16)
            pool.wait_ge(table_set, 16 * 5)
            with pool.Fori(0, B) as n:
                pool.wait_ge(wb_loaded, 32 * n + 32)
                pool.tensor_tensor(wb_h[:], wb_raw[:], zero_rows[:, 0:1].to_broadcast([P, 1024]), ALU.add
                                   ).then_inc(wb_own, 1)
                pool.wait_ge(wb_own, n + 5)
                pool.tensor_tensor(wb_l[:], wb_raw[:], wb_h[:].bitcast(F32), ALU.subtract).then_inc(wb_split, 1)
                pool.wait_ge(entry_done, 2 * n + 2)
                pool.tensor_tensor(carrier[:, 0:1], zero_rows[:, 0:1], zero_rows[:, 1:2], ALU.add)
                for t in range(TT):
                    for k in range(K):
                        j = t * K + k
                        pool.indirect_dma_start(
                            out=table, out_offset=bass.IndirectOffsetOnAxis(ap=slot_no[:, j:j + 1], axis=0),
                            in_=entry[:, t, k, :], in_offset=None, bounds_check=SLOTS - 1, oob_is_err=False,
                        ).then_inc(scattered, 16)
            pool.wait_ge(scattered, 16 * TT * K * B)

        @block.scalar
        def _(act):
            def std_of(m):
                act.wait_ge(var_ready, m + 1)
                act.activation(std[:], var_eps[:], ACT.Sqrt).then_inc(std_ready, 1)

            def xhi(m, buf, pair):
                act.wait_ge(tr_done, 2 * m + pair + 1)
                act.activation(xT_hi[buf][:, 2 * pair:2 * pair + 2, :], tp[:], ACT.Copy).then_inc(xhi_done, 1)

            std_of(0)
            act.wait_ge(rw_loaded, 32)
            act.activation(rw_hi[:], rw_raw[:], ACT.Copy).then_inc(split_hi, 1)
            for k in range(KT):
                act.wait_ge(sw_loaded[k % 2], 48 * (k // 2 + 1))
                act.activation(sw_hi[:, k, :], sw_raw[:, k % 2, :], ACT.Copy).then_inc(split_hi, 1)
            for pair in range(2):
                xhi(0, 0, pair)
            with act.Fori(0, B // 2) as i:
                for u in range(2):
                    n = 2 * i + u
                    c, d = u, 1 - u

                    def silu(mt):
                        act.wait_ge(gu_done, MT * n + mt + 1)
                        act.activation(silu_g[:, mt % 2, :], gu[mt % 2][:, 0, :], ACT.Silu).then_inc(silu_done, 1)

                    def hid_high(mt):
                        if mt == 0:
                            act.wait_ge(down_done, TT * n)
                        act.wait_ge(hid_done, MT * n + mt + 1)
                        act.activation(hid_hi[:, mt, :], hid[:, mt % 2, :], ACT.Copy).then_inc(hhi_done, 1)

                    std_of(n + 1)
                    act.wait_ge(logits_done, n + 1)
                    act.activation(score[:], lg[:], ACT.Sigmoid).then_inc(score_done, 1)
                    silu(0)
                    hid_high(0)
                    silu(1)
                    hid_high(1)
                    act.wait_ge(xT_stored[d], 32 * (i + u))
                    xhi(n + 1, d, 0)
                    silu(2)
                    hid_high(2)
                    xhi(n + 1, d, 1)
                    silu(3)
                    hid_high(3)
                    act.wait_ge(y_stored, 16 * n)
                    for t in range(TT):
                        act.wait_ge(down_done, TT * n + t + 1)
                        act.activation(ybuf[:, t, :], tp[:, t % 2, :], ACT.Copy).then_inc(y_copied, 1)

        @block.vector
        def _(dve):
            def normalise(m, buf, loads, stores):
                dve.wait_ge(x_loaded[buf], 16 * loads)
                for t in range(TT):
                    last = dve.bn_stats(stats[:, t, :], xin[buf][:, t, :])
                last.then_inc(stat_step, 1)
                dve.wait_ge(stat_step, 3 * m + 1)
                dve.memset(carrier[:, 1:2], 0.0)
                for t in range(TT):
                    last = dve.bn_aggr(mv[:, t, :], stats[:, t, :])
                last.then_inc(stat_step, 1)
                dve.wait_ge(stat_step, 3 * m + 2)
                dve.tensor_scalar(var_eps[:], mv[:, :, 1], EPS, None, ALU.add).then_inc(var_ready, 1)
                dve.wait_ge(std_ready, m + 1)
                dve.reciprocal(rstd[:], std[:]).then_inc(stat_step, 1)
                dve.wait_ge(stat_step, 3 * m + 3)
                dve.wait_ge(xn_stored[buf], 16 * stores)
                for t in range(TT):
                    last = dve.tensor_scalar(xn[buf][:, t, :], xin[buf][:, t, :], mv[:, t, 0:1], rstd[:, t:t + 1],
                                             ALU.subtract, ALU.mult)
                last.then_inc(ln_done, 1)

            def xlo(m, buf, pair):
                dve.wait_ge(xhi_done, 2 * m + pair + 1)
                dve.tensor_tensor(xT_lo[buf][:, 2 * pair:2 * pair + 2, :], tp[:],
                                  xT_hi[buf][:, 2 * pair:2 * pair + 2, :].bitcast(F32), ALU.subtract
                                  ).then_inc(xlo_done, 1)

            normalise(0, 0, 1, 0)
            dve.wait_ge(split_hi, 1)
            dve.tensor_tensor(rw_lo[:], rw_raw[:], rw_hi[:].bitcast(F32), ALU.subtract).then_inc(split_lo, 1)
            for k in range(KT):
                dve.wait_ge(split_hi, k + 2)
                dve.tensor_tensor(sw_lo[:, k, :], sw_raw[:, k % 2, :], sw_hi[:, k, :].bitcast(F32), ALU.subtract
                                  ).then_inc(split_lo, 1)
            for pair in range(2):
                xlo(0, 0, pair)
            dve.wait_ge(consts_done, 10)
            with dve.Fori(0, B // 2) as i:
                for u in range(2):
                    n = 2 * i + u
                    c, d = u, 1 - u
                    steps = [0]

                    def step(ins):
                        steps[0] += 1
                        ins.then_inc(route_step, 1)
                        dve.wait_ge(route_step, KC * n + steps[0])

                    def hidden(mt):
                        dve.wait_ge(silu_done, MT * n + mt + 1)
                        dve.tensor_tensor(hid[:, mt % 2, :], silu_g[:, mt % 2, :], gu[mt % 2][:, 1, :], ALU.mult
                                          ).then_inc(hid_done, 1)

                    def hid_low(mt):
                        dve.wait_ge(hhi_done, MT * n + mt + 1)
                        dve.tensor_tensor(hid_lo[:, mt, :], hid[:, mt % 2, :], hid_hi[:, mt, :].bitcast(F32),
                                          ALU.subtract).then_inc(hlo_done, 1)

                    def pick_groups():
                        dve.wait_ge(score_done, n + 1)
                        step(dve.tensor_tensor(biased[:], score[:], bias_row[:].unsqueeze(1).to_broadcast([P, TT, E]),
                                               ALU.add))
                        four = biased[:].rearrange("p t (g a b) -> p (t g) a b", a=2, b=2)
                        dve.tensor_tensor(pair_hi[:], four[:, :, :, 0], four[:, :, :, 1], ALU.max)
                        step(dve.tensor_tensor(pair_lo[:], four[:, :, :, 0], four[:, :, :, 1], ALU.min))
                        dve.tensor_tensor(top1[:], pair_hi[:, :, 0], pair_hi[:, :, 1], ALU.max)
                        dve.tensor_tensor(low1[:], pair_hi[:, :, 0], pair_hi[:, :, 1], ALU.min)
                        step(dve.tensor_tensor(low2[:], pair_lo[:, :, 0], pair_lo[:, :, 1], ALU.max))
                        step(dve.tensor_tensor(top2[:], low1[:], low2[:], ALU.max))
                        step(dve.tensor_tensor(gscore[:].rearrange("p t g -> p (t g)"), top1[:], top2[:], ALU.add))
                        other = gscore[:].unsqueeze(2).to_broadcast([P, TT, NG, NG])
                        own = gscore[:].unsqueeze(3).to_broadcast([P, TT, NG, NG])
                        dve.tensor_tensor(above[:], other, own, ALU.is_gt)
                        step(dve.tensor_tensor(equal[:], other, own, ALU.is_equal))
                        step(dve.tensor_tensor(equal[:], equal[:],
                                               lower_no[:].unsqueeze(1).to_broadcast([P, TT, NG, NG]), ALU.mult))
                        step(dve.tensor_tensor(above[:], above[:], equal[:], ALU.add))
                        step(dve.tensor_reduce(rank[:], above[:], AX.X, ALU.add))
                        step(dve.tensor_scalar(gmask[:], rank[:], TKG - 0.5, None, ALU.is_lt))
                        step(dve.tensor_tensor(masked0[:].rearrange("p t (g a) -> p (t g) a", a=EG),
                                               biased[:].rearrange("p t (g a) -> p (t g) a", a=EG),
                                               gmask[:].rearrange("p t g -> p (t g)").unsqueeze(2)
                                               .to_broadcast([P, TT * NG, EG]), ALU.mult))
                        step(dve.tensor_scalar(masked[:], masked0[:], 0.0, None, ALU.add))

                    def pick_experts():
                        for t in range(TT):
                            last = dve.max(best[:, t, :], masked[:, t, :])
                        step(last)
                        dve.memset(carrier[:, 1:2], 0.0)
                        for t in range(TT):
                            last = dve.max_index(best_no[:, t, :], best[:, t, :], masked[:, t, :])
                        step(last)
                        step(dve.tensor_copy(best_f[:], best_no[:, :, 0:K]))
                        step(dve.tensor_tensor(
                            onehot[:], best_f[:].rearrange("p t k -> p (t k)").unsqueeze(2).to_broadcast([P, TT * K, E]),
                            expert_no[:].unsqueeze(1).to_broadcast([P, TT * K, E]), ALU.is_equal))
                        with nc.allow_low_precision(reason="0 or 1"):
                            dve.tensor_reduce(chosen[:], onehot[:].rearrange("p (t k) e -> p t e k", k=K), AX.X, ALU.add
                                              ).then_inc(chosen_done, 1)

                    def weigh():
                        for t in range(TT):
                            last = dve.tensor_tensor(onehot_x[:, t * K:(t + 1) * K, :], onehot[:, t * K:(t + 1) * K, :],
                                                     score[:, t, :].unsqueeze(1).to_broadcast([P, K, E]), ALU.mult)
                        step(last)
                        step(dve.tensor_reduce(weight[:].rearrange("p t k -> p (t k)"), onehot_x[:], AX.X, ALU.add))
                        step(dve.tensor_reduce(wsum[:], weight[:], AX.X, ALU.add))
                        step(dve.tensor_scalar(wsum1[:], wsum[:], 1e-20, None, ALU.add))
                        step(dve.reciprocal(wrec[:], wsum1[:]))
                        step(dve.tensor_tensor(wnorm[:], weight[:], wrec[:].unsqueeze(2).to_broadcast([P, TT, K]),
                                               ALU.mult))
                        dve.wait_ge(scattered, 16 * TT * K * n)
                        dve.tensor_scalar(entry[:, :, :, 1].bitcast(F32), wnorm[:], ROUTE_SCALE, None, ALU.mult
                                          ).then_inc(entry_done, 1)

                    def place_tokens():
                        dve.wait_ge(prefix_done, n + 1)
                        step(dve.tensor_tensor(place[:], px[:, 0:TT, :], carry[:].unsqueeze(1).to_broadcast([P, TT, E]),
                                               ALU.add))
                        dve.tensor_tensor(carry[:], px[:, TT, :], carry[:], ALU.add)
                        dve.tensor_scalar(over[:], place[:], CAP - 0.5, SENTINEL, ALU.is_gt, ALU.mult)
                        step(dve.tensor_tensor(slot0[:], place[:], slot_base[:].unsqueeze(1).to_broadcast([P, TT, E]),
                                               ALU.add))
                        step(dve.tensor_tensor(slot[:], slot0[:], over[:], ALU.add))
                        for t in range(TT):
                            last = dve.tensor_tensor(slot_x[:, t * K:(t + 1) * K, :], onehot[:, t * K:(t + 1) * K, :],
                                                     slot[:, t, :].unsqueeze(1).to_broadcast([P, K, E]), ALU.mult)
                        step(last)
                        step(dve.tensor_reduce(slot_f[:], slot_x[:], AX.X, ALU.add))
                        step(dve.tensor_copy(entry[:, :, :, 0], token_f[:].unsqueeze(2).to_broadcast([P, TT, K])))
                        dve.tensor_copy(slot_no[:], slot_f[:]).then_inc(entry_done, 1)
                        step(dve.tensor_scalar(token_f[:], token_f[:], float(S), None, ALU.add))

                    normalise(n + 1, d, i + 1 + u, i + u)
                    hidden(0)
                    pick_groups()
                    hid_low(0)
                    hidden(1)
                    pick_experts()
                    hid_low(1)
                    xlo(n + 1, d, 0)
                    hidden(2)
                    weigh()
                    hid_low(2)
                    xlo(n + 1, d, 1)
                    hidden(3)
                    hid_low(3)
                    place_tokens()
                    assert steps[0] == KC, steps

        @block.tensor
        def _(pe):
            def transposes(m, buf, pair):
                for k in range(2 * pair, 2 * pair + 2):
                    for t in range(TT):
                        last = pe.transpose(tp[:, k % 2, t * P:(t + 1) * P], xn[buf][:, t, k * P:(k + 1) * P], ident[:])
                last.then_inc(tr_done, 1)

            pe.wait_ge(consts_done, 10)
            pe.wait_ge(ln_done, 1)
            transposes(0, 0, 0)
            pe.wait_ge(xlo_done, 1)
            transposes(0, 0, 1)
            pe.wait_ge(split_lo, KT + 1)
            with pe.Fori(0, B // 2) as i:
                for u in range(2):
                    n = 2 * i + u
                    c, d = u, 1 - u
                    parts = ((xT_hi[c], 0), (xT_lo[c], 0), (xT_hi[c], 1))

                    def gate_up(mt):
                        for j in range(2):
                            at = j * IS + mt * P
                            for k in range(KT):
                                for q, (xt, low) in enumerate(parts):
                                    w = sw_lo if low else sw_hi
                                    last = pe.matmul(gu[mt % 2][:, j, :], w[:, k, at:at + P], xt[:, k, :],
                                                     start=(k == 0 and q == 0), stop=(k == KT - 1 and q == 2))
                        last.then_inc(gu_done, 1)

                    pe.wait_ge(xlo_done, 2 * n + 2)
                    pe.wait_ge(score_done, n)
                    for t in range(TT):
                        for k in range(KT):
                            for q, (xt, low) in enumerate(parts):
                                w = rw_lo if low else rw_hi
                                last = pe.matmul(lg[:, t, :], xt[:, k, t * P:(t + 1) * P], w[:, k, :],
                                                 start=(k == 0 and q == 0), stop=(k == KT - 1 and q == 2))
                    last.then_inc(logits_done, 1)
                    pe.wait_ge(hid_done, MT * n)
                    gate_up(0)
                    gate_up(1)
                    pe.wait_ge(ln_done, n + 2)
                    pe.wait_ge(y_copied, TT * n)
                    transposes(n + 1, d, 0)
                    pe.wait_ge(hid_done, MT * n + 1)
                    gate_up(2)
                    pe.wait_ge(xlo_done, 2 * n + 3)
                    transposes(n + 1, d, 1)
                    pe.wait_ge(hid_done, MT * n + 2)
                    gate_up(3)
                    pe.wait_ge(chosen_done, n + 1)
                    for t in range(TT + 1):
                        if t < TT:
                            pe.matmul(px[:, t, :], before[:], chosen[:, t, :], start=True, stop=(t == 0))
                        for j in range(t):
                            last = pe.matmul(px[:, t, :], ones[:], chosen[:, j, :], start=(t == TT and j == 0),
                                             stop=(j == t - 1))
                    last.then_inc(prefix_done, 1)
                    pe.wait_ge(xlo_done, 2 * n + 4)
                    for t in range(TT):
                        if t >= 2:
                            pe.wait_ge(y_copied, TT * n + t - 1)
                        for mt in range(MT):
                            if t == 0:
                                pe.wait_ge(hlo_done, MT * n + mt + 1)
                            for q, (hp, w) in enumerate(((hid_hi, sw_hi), (hid_lo, sw_hi), (hid_hi, sw_lo))):
                                last = pe.matmul(tp[:, t % 2, :], hp[:, mt, t * P:(t + 1) * P], w[:, mt, 2 * IS:3 * IS],
                                                 start=(mt == 0 and q == 0), stop=(mt == MT - 1 and q == 2))
                        last.then_inc(down_done, 1)


def experts_phase(nc, consts, W_gate, W_up, W_down, xn_rows, acc_rows, table, load_next, wait_next):
    ident, = consts
    C2 = 2 * CAP

    with ExitStack() as ctx:
        def sb(name, shape, dt=F32):
            return ctx.enter_context(nc.sbuf_tensor(name, shape, dt))

        def pb(name, shape):
            return ctx.enter_context(nc.psum_tensor(name, shape, F32))

        def sem(name):
            return ctx.enter_context(nc.semaphore(name))

        ids_g = [sb(f"ids_g{i}", [HALF, 2, 2], I32) for i in range(2)]
        ids_s = [sb(f"ids_s{i}", [HALF, 2, 2], I32) for i in range(2)]
        raw_gu = [sb(f"raw_gu{i}", [P, 2, KT, I]) for i in range(2)]
        gu_hi = [sb(f"gu_hi{i}", [P, 2, KT, I], F32R) for i in range(2)]
        gu_lo = [sb(f"gu_lo{i}", [P, 2, KT, I], F32R) for i in range(2)]
        raw_dn = [sb(f"raw_dn{i}", [P, IT, D]) for i in range(2)]
        dn_hi = [sb(f"dn_hi{i}", [P, IT, D], F32R) for i in range(2)]
        dn_lo = [sb(f"dn_lo{i}", [P, IT, D], F32R) for i in range(2)]
        xs = [sb(f"xs{i}", [HALF, 2, D]) for i in range(2)]
        xt = [sb(f"xt{i}", [P, KT, 2, CAP], F32R) for i in range(2)]
        gu_low = sb("gu_low", [P, IT, 2, CAP])
        gu_sum = sb("gu_sum", [P, IT, 2, CAP])
        silu_e = sb("silu_e", [P, IT, CAP])
        hid_e = sb("hid_e", [P, IT, CAP])
        he_hi = [sb(f"he_hi{i}", [P, IT, CAP], F32R) for i in range(2)]
        he_lo = [sb(f"he_lo{i}", [P, IT, CAP], F32R) for i in range(2)]
        ys = [sb(f"ys{i}", [HALF, 2, D]) for i in range(2)]
        carrier = sb("carrier_e", [P, 2])

        gup = [pb(f"gup{i}", [P, 2, 512]) for i in range(IT)]
        tpe = pb("tpe", [P, 2, 512])
        yp = pb("yp", [P, 2, D])

        zeroed = sem("e_zeroed")
        gu_loaded = [sem(f"e_gu_loaded{i}") for i in range(2)]
        dn_loaded = [sem(f"e_dn_loaded{i}") for i in range(2)]
        idg_loaded = [sem(f"e_idg_loaded{i}") for i in range(2)]
        ids_loaded = [sem(f"e_ids_loaded{i}") for i in range(2)]
        gathered = [sem(f"e_gathered{i}") for i in range(2)]
        scattered = sem("e_scattered")
        carried = sem("e_carried")
        gu_high = sem("e_gu_high")
        vector_low = sem("e_vector_low")
        pool_low = sem("e_pool_low")
        dn_high = sem("e_dn_high")
        dn_low = sem("e_dn_low")
        tr_done = sem("e_tr_done")
        xhi_done = sem("e_xhi_done")
        xlo_done = sem("e_xlo_done")
        gu_done = sem("e_gu_done")
        low_copied = sem("e_low_copied")
        summed = sem("e_summed")
        silu_done = sem("e_silu_done")
        hid_done = sem("e_hid_done")
        hhi_done = sem("e_hhi_done")
        hlo_done = sem("e_hlo_done")
        down_done = sem("e_down_done")
        y_done = sem("e_y_done")

        gate_v = W_gate.rearrange("e (p k) i -> e p k i", k=KT)
        up_v = W_up.rearrange("e (p k) i -> e p k i", k=KT)
        down_v = W_down.rearrange("e (p k) n -> e p k n", k=IT)
        table_v = table.rearrange("(e h p) c -> e p h c", e=E, h=2)

        VS = 5

        def slices(tile, first, end):
            return tile[:].rearrange("p j k i -> p (j k) i")[:, first:end]

        PEEL = 4

        def over_experts(engine, body):
            with engine.Fori(0, (E - PEEL) // 2) as i:
                for u in range(2):
                    body(2 * i + u, i, u)
            for e in range(E - PEEL, E):
                body(e, e // 2, e % 2)

        def exists(e, ahead):
            return not isinstance(e, int) or e + ahead < E

        block = ctx.enter_context(nc.Block())

        @block.sync
        def _(sp):
            def load_gu(e, c):
                sp.dma_start(raw_gu[c][:, 0], gate_v[e]).then_inc(gu_loaded[c], 16)
                sp.dma_start(raw_gu[c][:, 1], up_v[e]).then_inc(gu_loaded[c], 16)

            def load_dn(e, c):
                sp.dma_start(raw_dn[c][:], down_v[e]).then_inc(dn_loaded[c], 16)

            for e in range(2):
                sp.dma_start(ids_g[e][:], table_v[e]).then_inc(idg_loaded[e], 16)
                load_gu(e, e)
            load_dn(0, 0)
            sp.dma_start(ids_s[0][:], table_v[0]).then_inc(ids_loaded[0], 16)
            for e in (2, 3):
                sp.wait_ge(gathered[e - 2], 32)
                sp.dma_start(ids_g[e - 2][:], table_v[e]).then_inc(idg_loaded[e - 2], 16)
            load_dn(1, 1)
            sp.wait_ge(gu_high, 1)
            sp.wait_ge(vector_low, 1)
            sp.wait_ge(pool_low, 1)
            load_gu(2, 0)

            def body(e, i, u):
                c, d = u, 1 - u
                if exists(e, 3):
                    sp.wait_ge(gu_high, e + 2)
                    sp.wait_ge(vector_low, e + 2)
                    sp.wait_ge(pool_low, e + 2)
                    load_gu(e + 3, d)
                if exists(e, 2):
                    sp.wait_ge(dn_high, e + 1)
                    sp.wait_ge(dn_low, e + 1)
                    load_dn(e + 2, c)
                if exists(e, 1):
                    sp.wait_ge(scattered, 32 * e)
                    sp.dma_start(ids_s[d][:], table_v[e + 1]).then_inc(ids_loaded[d], 16)
                if exists(e, 4):
                    sp.wait_ge(gathered[c], 32 * (i + 2))
                    sp.dma_start(ids_g[c][:], table_v[e + 4]).then_inc(idg_loaded[c], 16)
                if isinstance(e, int) and e == E - PEEL:
                    load_next(sp)

            over_experts(sp, body)
            sp.wait_ge(scattered, 32 * E)
            wait_next(sp)

        @block.gpsimd
        def _(pool):
            pool.memset(carrier[:], 0.0).then_inc(zeroed, 1)
            pool.wait_ge(zeroed, 1)

            def carry(earlier):
                pool.wait_ge(carried, earlier)
                pool.tensor_tensor(carrier[:, 0:1], carrier[:, 1:2], carrier[:, 1:2], ALU.add).then_inc(carried, 1)

            def gather(c, uses, earlier):
                pool.wait_ge(idg_loaded[c], 16 * uses)
                carry(earlier)
                for h in range(2):
                    pool.indirect_dma_start(
                        out=xs[c][:, h, :], out_offset=None, in_=xn_rows,
                        in_offset=bass.IndirectOffsetOnAxis(ap=ids_g[c][:, h, 0:1].bitcast(U32), axis=0),
                        bounds_check=ROWS - 1, oob_is_err=True).then_inc(gathered[c], 16)

            def pool_part(e, c):
                pool.wait_ge(gu_high, e + 1)
                pool.tensor_tensor(slices(gu_lo[c], VS, 2 * KT), slices(raw_gu[c], VS, 2 * KT),
                                   slices(gu_hi[c], VS, 2 * KT).bitcast(F32), ALU.subtract).then_inc(pool_low, 1)

            gather(0, 1, 0)
            gather(1, 1, 1)
            pool_part(0, 0)
            pool_part(1, 1)
            pool.wait_ge(tr_done, 1)
            gather(0, 2, 2)

            def body(e, i, u):
                c, d = u, 1 - u
                if exists(e, 3):
                    pool.wait_ge(tr_done, e + 2)
                    gather(d, i + 2 + u, 3 + 2 * e)
                if exists(e, 2):
                    pool_part(e + 2, c)
                pool.wait_ge(scattered, 32 * e)
                pool.wait_ge(y_done, 2 * e + 2)
                carry(4 + 2 * e if exists(e, 3) else 3 + (E - 3) + e)
                for h in range(2):
                    pool.indirect_dma_start(
                        out=acc_rows, in_=ys[c][:, h, :], in_offset=None,
                        out_offset=bass.IndirectOffsetOnAxis(ap=ids_s[c][:, h, 0:1].bitcast(U32), axis=0),
                        bounds_check=ROWS - 1, oob_is_err=True, compute_op=ALU.add).then_inc(scattered, 16)

            over_experts(pool, body)

        @block.scalar
        def _(act):
            def split_gu(e, c, uses):
                act.wait_ge(gu_loaded[c], 32 * uses)
                act.activation(gu_hi[c][:], raw_gu[c][:], ACT.Copy).then_inc(gu_high, 1)

            def split_dn(c, uses):
                act.wait_ge(dn_loaded[c], 16 * uses)
                act.activation(dn_hi[c][:], raw_dn[c][:], ACT.Copy).then_inc(dn_high, 1)

            def xhi(e, c):
                act.wait_ge(tr_done, e + 1)
                act.activation(xt[c][:, :, 0, :].rearrange("p (a b) s -> p a b s", b=2),
                               tpe[:, :, 0:C2].rearrange("p a (b s) -> p a b s", b=2), ACT.Copy
                               ).then_inc(xhi_done, 1)

            def low(e, it):
                act.wait_ge(gu_done, 2 * e + it + 1)
                act.activation(gu_low[:, it], gup[it][:, :, CAP:C2], ACT.Copy).then_inc(low_copied, 1)

            def silu(e, it):
                act.wait_ge(summed, 2 * e + it + 1)
                act.activation(silu_e[:, it], gu_sum[:, it, 0], ACT.Silu).then_inc(silu_done, 1)

            def hid_high(e, c, it):
                act.wait_ge(hid_done, 2 * e + it + 1)
                act.activation(he_hi[c][:, it], hid_e[:, it], ACT.Copy).then_inc(hhi_done, 1)

            def hidden(e, c):
                for it in range(IT):
                    silu(e, it)
                for it in range(IT):
                    hid_high(e, c, it)

            split_gu(0, 0, 1)
            split_gu(1, 1, 1)
            xhi(0, 0)
            for it in range(IT):
                low(0, it)
            xhi(1, 1)
            hidden(0, 0)
            split_dn(0, 1)

            def body(e, i, u):
                c, d = u, 1 - u
                if exists(e, 2):
                    act.wait_ge(gu_done, 2 * e + 2)
                    split_gu(e + 2, c, i + 2)
                if exists(e, 1):
                    low(e + 1, 0)
                if exists(e, 2):
                    xhi(e + 2, c)
                if exists(e, 1):
                    act.wait_ge(down_done, 2 * e)
                    split_dn(d, i + 1 + u)
                    low(e + 1, 1)
                    hidden(e + 1, d)
                act.wait_ge(ids_loaded[c], 16 * (i + 1))
                for h in range(2):
                    act.wait_ge(down_done, 2 * e + h + 1)
                    act.activation(ys[c][:, h, :], yp[0:HALF, h, :], ACT.Copy,
                                   scale=ids_s[c][:, h, 1:2].bitcast(F32)).then_inc(y_done, 1)

            over_experts(act, body)

        @block.vector
        def _(dve):
            def vector_part(e, c):
                dve.wait_ge(gu_high, e + 1)
                dve.tensor_tensor(slices(gu_lo[c], 0, VS), slices(raw_gu[c], 0, VS),
                                  slices(gu_hi[c], 0, VS).bitcast(F32), ALU.subtract).then_inc(vector_low, 1)

            def dn_part(e, c):
                dve.wait_ge(dn_high, e + 1)
                dve.tensor_tensor(dn_lo[c][:], raw_dn[c][:], dn_hi[c][:].bitcast(F32), ALU.subtract
                                  ).then_inc(dn_low, 1)

            def xlo(e, c):
                dve.wait_ge(xhi_done, e + 1)
                dve.tensor_tensor(xt[c][:, :, 1, :].rearrange("p (a b) s -> p a b s", b=2),
                                  tpe[:, :, 0:C2].rearrange("p a (b s) -> p a b s", b=2),
                                  xt[c][:, :, 0, :].bitcast(F32).rearrange("p (a b) s -> p a b s", b=2), ALU.subtract
                                  ).then_inc(xlo_done, 1)

            def add(e, it):
                dve.wait_ge(low_copied, 2 * e + it + 1)
                dve.tensor_tensor(gu_sum[:, it], gup[it][:, :, 0:CAP], gu_low[:, it], ALU.add).then_inc(summed, 1)

            def hidden(e, c):
                for it in range(IT):
                    dve.wait_ge(silu_done, 2 * e + it + 1)
                    dve.tensor_tensor(hid_e[:, it], silu_e[:, it], gu_sum[:, it, 1], ALU.mult).then_inc(hid_done, 1)
                for it in range(IT):
                    dve.wait_ge(hhi_done, 2 * e + it + 1)
                    dve.tensor_tensor(he_lo[c][:, it], hid_e[:, it], he_hi[c][:, it].bitcast(F32), ALU.subtract
                                      ).then_inc(hlo_done, 1)

            vector_part(0, 0)
            vector_part(1, 1)
            xlo(0, 0)
            for it in range(IT):
                add(0, it)
            xlo(1, 1)
            hidden(0, 0)
            dn_part(0, 0)

            def body(e, i, u):
                c, d = u, 1 - u
                if exists(e, 2):
                    vector_part(e + 2, c)
                if exists(e, 1):
                    add(e + 1, 0)
                if exists(e, 2):
                    xlo(e + 2, c)
                if exists(e, 1):
                    add(e + 1, 1)
                    hidden(e + 1, d)
                    dn_part(e + 1, d)

            over_experts(dve, body)

        @block.tensor
        def _(pe):
            def turn(e, c, uses):
                pe.wait_ge(gathered[c], 32 * uses)
                for k in range(KT):
                    for h in range(2):
                        at = (k % 2) * CAP + h * HALF
                        last = pe.transpose(tpe[:, k // 2, at:at + HALF], xs[c][:, h, k:D:KT], ident[0:HALF, 0:HALF])
                last.then_inc(tr_done, 1)

            def gate_up(e, c, it):
                for j in range(2):
                    for k in range(KT):
                        at = slice(it, I, IT)
                        pe.matmul(gup[it][:, j, 0:C2], gu_hi[c][:, j, k, at], xt[c][:, k].rearrange("p a s -> p (a s)"),
                                  start=(k == 0), stop=False, skip_group_check=True)
                        last = pe.matmul(gup[it][:, j, 0:CAP], gu_lo[c][:, j, k, at], xt[c][:, k, 0],
                                         start=False, stop=(k == KT - 1), skip_group_check=True)
                last.then_inc(gu_done, 1)

            def down(c):
                for h in range(2):
                    at = slice(h * HALF, (h + 1) * HALF)
                    for it in range(IT):
                        for q, (hp, w) in enumerate(((he_hi, dn_hi), (he_lo, dn_hi), (he_hi, dn_lo))):
                            last = pe.matmul(yp[0:HALF, h, :], hp[c][:, it, at], w[c][:, it, :],
                                             start=(it == 0 and q == 0), stop=(it == IT - 1 and q == 2))
                    last.then_inc(down_done, 1)

            def gu_ready(e):
                pe.wait_ge(xlo_done, e + 1)
                pe.wait_ge(vector_low, e + 1)
                pe.wait_ge(pool_low, e + 1)

            turn(0, 0, 1)
            gu_ready(0)
            for it in range(IT):
                gate_up(0, 0, it)
            turn(1, 1, 1)

            def body(e, i, u):
                c, d = u, 1 - u
                if exists(e, 1):
                    gu_ready(e + 1)
                    pe.wait_ge(summed, 2 * e + 1)
                    gate_up(e + 1, d, 0)
                if exists(e, 2):
                    turn(e + 2, c, i + 2)
                if exists(e, 1):
                    pe.wait_ge(summed, 2 * e + 2)
                    gate_up(e + 1, d, 1)
                pe.wait_ge(hlo_done, 2 * e + 2)
                pe.wait_ge(dn_low, e + 1)
                pe.wait_ge(y_done, 2 * e)
                down(c)

            over_experts(pe, body)


def attention_phase(nc, consts, w_hi, w_lo, xT_hi, xT_lo, xT, x, acc_rows, qkv_b, out_b, out):
    ident, = consts
    K3 = 3 * HD
    K5 = K3 + 2
    NP = TT // 2
    UNITS = B * H
    VW = 3 * HD
    VB = 5
    SCALE = 1.0 / float(HD) ** 0.5

    with ExitStack() as ctx:
        def sb(name, shape, dt=F32):
            return ctx.enter_context(nc.sbuf_tensor(name, shape, dt))

        def pb(name, shape):
            return ctx.enter_context(nc.psum_tensor(name, shape, F32))

        def sem(name):
            return ctx.enter_context(nc.semaphore(name))

        qk_bias = sb("qk_bias", [P, 2, G])
        v_bias = sb("v_bias", [P, D])
        o_bias = sb("o_bias", [P, D])
        qk_hi = [sb(f"{a}_hi", [P, S], F32R) for a in "qk"]
        qk_lo = [sb(f"{a}_lo", [P, S]) for a in "qk"]
        stack = [[sb(f"{a}_stack{i}", [K5, GH, S], F32R) for i in range(2)] for a in "qk"]
        v_sum = sb("v_sum", [P, 2 * P])
        v_cols = [sb(f"v_cols{i}", [P, TT, GH, VB, HD], F32R) for i in range(2)]
        neg_max = [sb(f"neg_max{i}", [P, 2, TT]) for i in range(2)]
        neg_hi = [sb(f"neg_hi{i}", [2 * TT, P], F32R) for i in range(2)]
        neg_lo = [sb(f"neg_lo{i}", [2 * TT, P], F32R) for i in range(2)]
        probs = [sb(f"probs{i}", [P, 2, S]) for i in range(NP)]
        p_hi = [sb(f"p_hi{i}", [P, 2, S], F32R) for i in range(NP)]
        p_lo = [sb(f"p_lo{i}", [P, 2, S], F32R) for i in range(NP)]
        ctx_low = sb("ctx_low", [HD, S])
        ctx_sum = sb("ctx_sum", [P, S])
        norm = sb("norm", [P, S])
        ctx_hi = sb("ctx_hi", [P, G, S], F32R)
        ctx_lo = sb("ctx_lo", [P, G, S], F32R)
        gate = sb("gate", [P, TT, D])
        att = sb("att", [P, D])
        xin = [sb(f"x_in{i}", [P, D]) for i in range(2)]

        sc = pb("sc", [P, 2, S])
        mx = pb("mx", [P, 2, S])
        pv = [pb(f"pv{i}", [P, S]) for i in range(2)]
        aux = [pb(f"aux{i}", [P, S]) for i in range(2)]

        bias_loaded = sem("c_bias_loaded")
        ones_set = sem("c_ones_set")
        x_turned = sem("c_x_turned")
        aux_done = sem("c_aux_done")
        aux_read = [sem(f"c_aux_read{i}") for i in range(2)]
        max_high_done = sem("c_max_high_done")
        qk_high_done = sem("c_qk_high_done")
        qk_low_done = sem("c_qk_low_done")
        v_high = sem("c_v_high")
        v_low = sem("c_v_low")
        stacked = [sem(f"c_stacked{i}") for i in range(2)]
        neg_stacked = [sem(f"c_neg_stacked{i}") for i in range(2)]
        mx_done = sem("c_mx_done")
        mx_read = sem("c_mx_read")
        sc_done = sem("c_sc_done")
        exp_done = sem("c_exp_done")
        phi_done = sem("c_phi_done")
        plo_done = sem("c_plo_done")
        pv_done = sem("c_pv_done")
        log_done = sem("c_log_done")
        low_copied = sem("c_low_copied")
        ctx_added = sem("c_ctx_added")
        inv_done = sem("c_inv_done")
        nrm_done = sem("c_nrm_done")
        chi_done = sem("c_chi_done")
        clo_done = sem("c_clo_done")
        acc_loaded = sem("c_acc_loaded")
        xin_loaded = [sem(f"c_xin_loaded{i}") for i in range(2)]
        gate_done = sem("c_gate_done")
        att_done = sem("c_att_done")
        y_done = sem("c_y_done")
        y_stored = sem("c_y_stored")

        x_v = x.rearrange("(b t p) d -> b p t d", p=P, t=TT)
        acc_v = acc_rows[0:T, :].rearrange("(b t p) d -> b p t d", p=P, t=TT)
        out_v = out.rearrange("(b t p) d -> b p t d", p=P, t=TT)

        def rows(h, part):
            part = 2 - part if h % 2 else part
            return slice(part * HD, (part + 1) * HD)

        def uses(b, j):
            last = isinstance(b, int) and b == B - 1
            if j == 0:
                outs = () if isinstance(b, int) and b == 0 else ("out0", "out1", "out2", "out3")
                return ("max1", "q", "k", "max0") + outs
            if j == 2:
                return ("max1", "max0") if last else ("max1", "q", "k", "max0")
            if j == 3 and last:
                return ("max1",)
            return ("v0", "max1", "v1", "q", "k", "v2", "max0", "v3")

        def use_no(b, j, use):
            last = isinstance(b, int) and b == B - 1 and j == G - 1
            if j == 0:
                before = 9 if isinstance(b, int) and b == 0 else 5
            else:
                before = (13, 21, 25)[j - 1] - (2 if last else 0)
            return b, before + uses(b, j).index(use)

        def number(use, later=0):
            return 28 * use[0] + use[1] + later

        def buf(use):
            return use[1] % 2

        def turn(use):
            return 14 * use[0] + use[1] // 2

        def follows(b, j, ahead):
            return not isinstance(b, int) or G * b + j + ahead < G * B

        def over_groups(engine, step):
            step(0, 0)
            with engine.Fori(0, B - 1) as b:
                for j in (1, 2, 3):
                    step(b, j)
                step(b + 1, 0)
            for j in (1, 2, 3):
                step(B - 1, j)

        block = ctx.enter_context(nc.Block())

        @block.sync
        def _(sp):
            def stack_rows(a, g2, pair):
                parts = (qk_hi, qk_lo, qk_hi) if a == 0 else (qk_hi, qk_hi, qk_lo)
                for n, part in enumerate(parts):
                    sp.dma_start(stack[a][g2][n * HD:(n + 1) * HD, 2 * pair:2 * pair + 2, :].bitcast(F32),
                                 part[a][pair * 2 * HD:(pair + 1) * 2 * HD, :].bitcast(F32)
                                 ).then_inc(stacked[pair], 16)

            def stack_up(a, g, g2, pair):
                sp.wait_ge(qk_low_done, 2 * g + a + 1)
                stack_rows(a, g2, pair)

            def stack_max(pair, use, g2):
                sp.wait_ge(aux_read[buf(use)], turn(use) + 1)
                for n, part in enumerate((neg_hi, neg_lo)):
                    sp.dma_start(stack[0][g2][K3 + n:K3 + n + 1, 2 * pair:2 * pair + 2, :].bitcast(F32)
                                 .rearrange("o h (t s) -> o (h t) s", s=P), part[pair][:].bitcast(F32)
                                 ).then_inc(neg_stacked[pair], 16)

            def load_late(b):
                for tt in range(2, TT):
                    sp.wait_ge(y_done, TT * b + tt - 1)
                    sp.dma_start(xin[tt % 2][:], x_v[b, :, tt]).then_inc(xin_loaded[tt % 2], 16)

            for n in range(2):
                sp.dma_start(qk_bias[:, n, :], qkv_b[n * D:(n + 1) * D].rearrange("(c p) -> p c", p=P), allow_slow_non_contiguous=True
                             ).then_inc(bias_loaded, 16)
            sp.dma_start(v_bias[:], qkv_b[2 * D:3 * D].rearrange("(a e) -> a e", a=1).to_broadcast([P, D])
                         ).then_inc(bias_loaded, 16)
            sp.dma_start(o_bias[:], out_b.rearrange("(a e) -> a e", a=1).to_broadcast([P, D])
                         ).then_inc(bias_loaded, 16)
            for pair in range(2):
                stack_up(0, 0, 0, pair)
            for pair in range(2):
                stack_up(1, 0, 0, pair)
            stack_max(0, (0, 6), 0)
            stack_up(0, 1, 1, 0)
            stack_up(1, 1, 1, 0)

            def step(b, j):
                g = G * b + j
                if follows(b, j, 1):
                    sp.wait_ge(sc_done, 2 * GH * g)
                    for a in range(2):
                        stack_rows(a, (j + 1) % 2, 1)
                stack_max(1, use_no(b, j, "max1"), j % 2)
                if j == 1:
                    sp.wait_ge(y_stored, 16 * b)
                    sp.dma_start(gate[:], acc_v[b]).then_inc(acc_loaded, 16)
                    for tt in range(2):
                        sp.dma_start(xin[tt][:], x_v[b, :, tt]).then_inc(xin_loaded[tt], 16)
                if follows(b, j, 2):
                    stack_up(0, g + 2, j % 2, 0)
                    stack_up(1, g + 2, j % 2, 0)
                if follows(b, j, 1):
                    stack_max(0, use_no(b, j, "max0"), (j + 1) % 2)
                if j == 1 and follows(b, j, G - 1):
                    sp.wait_ge(aux_done, number(use_no(b, j, "v3"), 1))
                    for part, tile in enumerate((xT_hi, xT_lo)):
                        sp.dma_start(tile[:].bitcast(F32), xT[b + 1, part].rearrange("p (k s) -> p k s", k=KT)
                                     ).then_inc(x_turned, 16)
                if "out0" in uses(b, j):
                    load_late(b - 1)
                    sp.wait_ge(y_done, TT * b)
                    sp.dma_start(out_v[b - 1], gate[:]).then_inc(y_stored, 16)

            over_groups(sp, step)
            load_late(B - 1)
            sp.wait_ge(y_done, TT * B)
            sp.dma_start(out_v[B - 1], gate[:]).then_inc(y_stored, 16)
            sp.wait_ge(y_stored, 16 * B)

        @block.scalar
        def _(act):
            nc.scalar.preload_act_table_set("natural_log_exp_and_others")

            def qk_high(a, use, g, c):
                act.wait_ge(aux_done, number(use, 1))
                for pair in range(2):
                    act.wait_ge(stacked[pair], 16 * 6 * g)
                act.activation(qk_lo[a][:], aux[buf(use)][:], ACT.Identity, bias=qk_bias[:, a, c:c + 1]
                               ).then_inc(aux_read[buf(use)], 1)
                act.wait_ge(aux_read[buf(use)], turn(use) + 1)
                act.activation(qk_hi[a][:], qk_lo[a][:], ACT.Copy).then_inc(qk_high_done, 1)

            def max_high(pair, use, g):
                act.wait_ge(aux_done, number(use, 1))
                act.wait_ge(neg_stacked[pair], 32 * g)
                act.activation(neg_hi[pair][:], aux[buf(use)][0:2 * TT, 0:P], ACT.Copy).then_inc(max_high_done, 1)

            def v_split(use, c, s):
                act.wait_ge(aux_read[buf(use)], turn(use) + 1)
                act.activation(v_cols[c][:, s, :, 0:VB:VB - 1, :],
                               v_sum[:].rearrange("p (h o d) -> p h o d", h=GH, o=2), ACT.Copy).then_inc(v_high, 1)

            def exponentials(unit, pair):
                act.wait_ge(sc_done, 2 * unit + pair + 1)
                if not isinstance(unit, int) or unit > 0:
                    act.wait_ge(plo_done, 2 * unit + pair - 1)
                act.activation(probs[pair][:], sc[:], ACT.Exp, scale=SCALE).then_inc(exp_done, 1)

            def head_out(unit, g, h):
                act.wait_ge(pv_done, 2 * unit + 2)
                if h == 0:
                    act.wait_ge(clo_done, g)
                act.activation(norm[h * HD:(h + 1) * HD, :], pv[h % 2][rows(h, 2), :], ACT.Ln).then_inc(log_done, 1)
                act.wait_ge(ctx_added, unit)
                act.activation(ctx_low[:], pv[h % 2][rows(h, 1), :], ACT.Copy).then_inc(low_copied, 1)

            def invert(g):
                act.wait_ge(log_done, GH * (g + 1))
                act.activation(norm[:], norm[:], ACT.Exp, scale=-1.0).then_inc(inv_done, 1)

            def ctx_high(g, c):
                act.wait_ge(nrm_done, g + 1)
                act.activation(ctx_hi[:, c, :], norm[:], ACT.Copy).then_inc(chi_done, 1)

            act.wait_ge(bias_loaded, 64)
            qk_high(0, (0, 0), 0, 0)
            qk_high(1, (0, 1), 0, 0)
            for s in range(TT):
                v_split((0, 2 + s), 0, s)
            max_high(0, (0, 6), 0)
            qk_high(0, (0, 7), 1, 1)
            qk_high(1, (0, 8), 1, 1)

            def open_gate(b):
                act.wait_ge(acc_loaded, 16 * (b + 1))
                act.activation(gate[:], gate[:], ACT.Silu).then_inc(gate_done, 1)
                nc.scalar.preload_act_table_set("natural_log_exp_and_others")

            def step(b, j):
                g = G * b + j
                first = isinstance(b, int) and g == 0
                for h in range(GH):
                    unit = GH * g + h
                    exponentials(unit, 0)
                    if f"v{h}" in uses(b, j) and h != 2:
                        v_split(use_no(b, j, f"v{h}"), (j + 1) // 2 % 2, h)
                    if h == 2 and follows(b, j, 2):
                        qk_high(1, use_no(b, j, "k"), g + 2, (j + 2) % G)
                    if h >= 2 or not first:
                        head_out(unit - 2, g if h >= 2 else g - 1, (h - 2) % GH)
                    exponentials(unit, 1)
                    if h == 1 and not first:
                        invert(g - 1)
                    if h == 1 and follows(b, j, 2):
                        qk_high(0, use_no(b, j, "q"), g + 2, (j + 2) % G)
                    if h == 1 and not first:
                        ctx_high(g - 1, (j - 1) % G)
                    if h == 2 and "v2" in uses(b, j):
                        v_split(use_no(b, j, "v2"), (j + 1) // 2 % 2, 2)
                    if h == 0:
                        max_high(1, use_no(b, j, "max1"), g)
                    if h == 2 and follows(b, j, 1):
                        max_high(0, use_no(b, j, "max0"), g + 1)
                    if h == 2 and "out0" in uses(b, j):
                        open_gate(b - 1)

            over_groups(act, step)
            open_gate(B - 1)
            head_out(UNITS - 2, G * B - 1, 2)
            head_out(UNITS - 1, G * B - 1, 3)
            invert(G * B - 1)
            ctx_high(G * B - 1, G - 1)

        @block.vector
        def _(dve):
            def qk_low(a, g):
                dve.wait_ge(qk_high_done, 2 * g + a + 1)
                dve.tensor_tensor(qk_lo[a][:], qk_lo[a][:], qk_hi[a][:].bitcast(F32), ALU.subtract
                                  ).then_inc(qk_low_done, 1)

            def max_low(pair, use, g):
                dve.wait_ge(max_high_done, 2 * g + pair + 1)
                dve.tensor_tensor(neg_lo[pair][:], aux[buf(use)][0:2 * TT, 0:P], neg_hi[pair][:].bitcast(F32),
                                  ALU.subtract).then_inc(aux_read[buf(use)], 1)

            def v_make(n, use, half):
                dve.wait_ge(aux_done, number(use, 1))
                dve.wait_ge(v_low, n)
                dve.tensor_tensor(v_sum[:], aux[buf(use)][:, 0:2 * P], v_bias[:, half * 2 * P:(half + 1) * 2 * P],
                                  ALU.add).then_inc(aux_read[buf(use)], 1)

            def v_make_low(n, c, s):
                dve.wait_ge(v_high, n + 1)
                dve.tensor_tensor(v_cols[c][:, s, :, 1:VB - 1:2, :],
                                  v_sum[:].rearrange("p (h o d) -> p h o d", h=GH, o=2),
                                  v_cols[c][:, s, :, 0:VB:VB - 1, :].bitcast(F32), ALU.subtract).then_inc(v_low, 1)

            def maxima(g, h, tp):
                dve.wait_ge(mx_done, 2 * GH * g + 2 * h + tp + 1)
                dve.tensor_reduce(neg_max[h // 2][:, h % 2, 2 * tp:2 * tp + 2], mx[:], AX.X, ALU.max, negate=True
                                  ).then_inc(mx_read, 1)

            def high_probs(unit, pair):
                dve.wait_ge(exp_done, 2 * unit + pair + 1)
                if not isinstance(unit, int) or unit > 0:
                    dve.wait_ge(pv_done, 2 * unit + pair - 1)
                dve.tensor_copy(p_hi[pair][:], probs[pair][:]).then_inc(phi_done, 1)

            def head_out(unit, g, h):
                dve.wait_ge(low_copied, unit + 1)
                if h == 0:
                    dve.wait_ge(nrm_done, g)
                dve.tensor_tensor(ctx_sum[h * HD:(h + 1) * HD, :], pv[h % 2][rows(h, 0), :], ctx_low[:], ALU.add
                                  ).then_inc(ctx_added, 1)

            def normalise(g):
                dve.wait_ge(inv_done, g + 1)
                dve.wait_ge(ctx_added, GH * (g + 1))
                dve.tensor_tensor(norm[:], norm[:], ctx_sum[:], ALU.mult).then_inc(nrm_done, 1)

            def ctx_low_part(g, c):
                dve.wait_ge(chi_done, g + 1)
                dve.tensor_tensor(ctx_lo[:, c, :], norm[:], ctx_hi[:, c, :].bitcast(F32), ALU.subtract
                                  ).then_inc(clo_done, 1)

            def output(b, tt, use):
                dve.wait_ge(aux_done, number(use, 1))
                dve.wait_ge(att_done, TT * b + tt)
                dve.tensor_tensor(att[:], aux[buf(use)][:], o_bias[:], ALU.add).then_inc(aux_read[buf(use)], 1)

            def times_gate(b, tt, use):
                if tt == 0:
                    dve.wait_ge(gate_done, b + 1)
                dve.wait_ge(aux_read[buf(use)], turn(use) + 1)
                dve.tensor_tensor(gate[:, tt, :], att[:], gate[:, tt, :], ALU.mult).then_inc(att_done, 1)

            dve.wait_ge(bias_loaded, 64)
            for a in range(2):
                qk_low(a, 0)
            for s in range(TT):
                v_make(s, (0, 2 + s), 0)
                v_make_low(s, 0, s)
            for h in range(GH):
                for tp in range(NP if h < GH - 1 else 1):
                    maxima(0, h, tp)
            max_low(0, (0, 6), 0)
            for a in range(2):
                qk_low(a, 1)

            def step(b, j):
                g = G * b + j
                first = isinstance(b, int) and g == 0
                vn = 4 + 8 * b + (0 if j == 1 else 4)
                vc = (j + 1) // 2 % 2

                def rows_out(tt, step_of=output):
                    if f"out{tt}" in uses(b, j):
                        step_of(b - 1, tt, use_no(b, j, f"out{tt}"))

                for h in range(GH):
                    unit = GH * g + h
                    if f"v{h}" in uses(b, j) and h != 2:
                        v_make(vn + h, use_no(b, j, f"v{h}"), vc)
                        v_make_low(vn + h, vc, h)
                    if h == 3:
                        rows_out(1)
                        rows_out(1, times_gate)
                    high_probs(unit, 0)
                    if h == 2 and follows(b, j, 2):
                        qk_low(1, g + 2)
                    if h == 0:
                        maxima(g, GH - 1, 1)
                    elif follows(b, j, 1):
                        maxima(g + 1, h - 1, 1)
                    if h >= 2 or not first:
                        head_out(unit - 2, g if h >= 2 else g - 1, (h - 2) % GH)
                    if h == 1 and not first:
                        normalise(g - 1)
                    if h == 3:
                        rows_out(2)
                        rows_out(2, times_gate)
                    if h == 2 and "v2" in uses(b, j):
                        v_make(vn + 2, use_no(b, j, "v2"), vc)
                        v_make_low(vn + 2, vc, 2)
                    high_probs(unit, 1)
                    if follows(b, j, 1):
                        maxima(g + 1, h, 0)
                    if h == 1 and follows(b, j, 2):
                        qk_low(0, g + 2)
                    if h == 1 and not first:
                        ctx_low_part(g - 1, (j - 1) % G)
                    if h == 0:
                        max_low(1, use_no(b, j, "max1"), g)
                    if h == 2 and follows(b, j, 1):
                        max_low(0, use_no(b, j, "max0"), g + 1)
                    if h == 2:
                        rows_out(0)
                        rows_out(0, times_gate)
                    if h == 3:
                        rows_out(3)
                        rows_out(3, times_gate)

            over_groups(dve, step)
            head_out(UNITS - 2, G * B - 1, 2)
            head_out(UNITS - 1, G * B - 1, 3)
            normalise(G * B - 1)
            ctx_low_part(G * B - 1, G - 1)
            for tt in range(TT):
                for part in (output, times_gate):
                    part(B - 1, tt, (B - 1, use_no(B - 1, 3, "max1")[1] + 1 + tt))

        @block.gpsimd
        def _(pool):
            for i in range(2):
                pool.memset(stack[1][i][K3:K5, :, :].bitcast(F32), 1.0).then_inc(ones_set, 1)
                pool.wait_ge(ones_set, 2 * i + 1)
                pool.memset(v_cols[i][:, :, :, 2, :].bitcast(F32), 1.0).then_inc(ones_set, 1)
                pool.wait_ge(ones_set, 2 * i + 2)

            def low_probs(unit, pair):
                pool.wait_ge(phi_done, 2 * unit + pair + 1)
                pool.tensor_tensor(p_lo[pair][:], probs[pair][:], p_hi[pair][:].bitcast(F32), ALU.subtract
                                   ).then_inc(plo_done, 1)

            def result(b, tt):
                pool.wait_ge(att_done, TT * b + tt + 1)
                pool.wait_ge(xin_loaded[tt % 2], 16 * (2 * b + tt // 2 + 1))
                pool.tensor_tensor(gate[:, tt, :], gate[:, tt, :], xin[tt % 2][:], ALU.add).then_inc(y_done, 1)

            def step(b, j):
                g = G * b + j
                for h in range(GH):
                    unit = GH * g + h
                    low_probs(unit, 0)
                    if h == 3 and "out0" in uses(b, j):
                        result(b - 1, 0)
                        result(b - 1, 1)
                    low_probs(unit, 1)
                    if h == 3 and "out0" in uses(b, j):
                        result(b - 1, 2)
                        result(b - 1, 3)

            over_groups(pool, step)
            for tt in range(TT):
                result(B - 1, tt)

        @block.tensor
        def _(pe):
            def aux_free(use):
                pe.wait_ge(aux_read[buf(use)], turn(use))

            def turned_product(a, c, use):
                aux_free(use)
                cols = slice(a * D + c * P, a * D + (c + 1) * P)
                for k in range(KT):
                    for q, (w, xt) in enumerate(((w_hi, xT_hi), (w_lo, xT_hi), (w_hi, xT_lo))):
                        last = pe.matmul(aux[buf(use)][:], w[:, k, cols], xt[:, k, :],
                                         start=(k == 0 and q == 0), stop=(k == KT - 1 and q == 2))
                last.then_inc(aux_done, 1)

            def v_product(half, s, use):
                aux_free(use)
                cols = slice(2 * D + half * 2 * P, 2 * D + (half + 1) * 2 * P)
                for k in range(KT):
                    for q, (xt, w) in enumerate(((xT_hi, w_hi), (xT_lo, w_hi), (xT_hi, w_lo))):
                        last = pe.matmul(aux[buf(use)][:, 0:2 * P], xt[:, k, s * P:(s + 1) * P], w[:, k, cols],
                                         start=(k == 0 and q == 0), stop=(k == KT - 1 and q == 2))
                last.then_inc(aux_done, 1)

            def turn_maxima(g, pair, use):
                aux_free(use)
                pe.wait_ge(mx_read, 2 * GH * g + GH * (pair + 1))
                pe.transpose(aux[buf(use)][0:2 * TT, 0:P], neg_max[pair][:].rearrange("p h t -> p (h t)"), ident[:]
                             ).then_inc(aux_done, 1)

            def scores_for_max(g, g2, h, tp):
                if h % 2 == 0 and tp == 0:
                    pe.wait_ge(stacked[h // 2], 16 * 6 * (g + 1))
                index = 2 * GH * g + 2 * h + tp
                if not isinstance(index, int) or index > 0:
                    pe.wait_ge(mx_read, index)
                for n in range(2):
                    at = slice((2 * tp + n) * P, (2 * tp + n + 1) * P)
                    last = pe.matmul(mx[:, n, :], stack[0][g2][0:K3, h, at], stack[1][g2][0:K3, h, :],
                                     start=True, stop=True)
                last.then_inc(mx_done, 1)

            def scores(unit, g, g2, h, pair):
                if pair == 0 and h % 2 == 0:
                    pe.wait_ge(neg_stacked[h // 2], 32 * (g + 1))
                if not isinstance(unit, int) or unit > 0 or pair > 0:
                    pe.wait_ge(exp_done, 2 * unit + pair)
                for n in range(2):
                    at = slice((2 * pair + n) * P, (2 * pair + n + 1) * P)
                    last = pe.matmul(sc[:, n, :], stack[1][g2][:, h, at], stack[0][g2][:, h, :],
                                     start=True, stop=True)
                last.then_inc(sc_done, 1)

            def weigh_values(unit, c, h, pair):
                pe.wait_ge(plo_done, 2 * unit + pair + 1)
                if pair == 0 and (not isinstance(unit, int) or unit > 0):
                    pe.wait_ge(ctx_added, unit - 1)
                first = 2 * (h % 2)
                for n in range(2):
                    for q, part in enumerate((p_hi, p_lo)):
                        last = pe.matmul(pv[h % 2][0:VW, :], v_cols[c // 2][:, 2 * pair + n, (c % 2) * 2 + h // 2, first:first + 3, :]
                                         .rearrange("p b d -> p (b d)"),
                                         part[pair][:, n, :], start=(pair == 0 and n == 0 and q == 0),
                                         stop=(pair == 1 and n == 1 and q == 1))
                last.then_inc(pv_done, 1)

            def out_product(b, tt, use):
                aux_free(use)
                if tt == 0:
                    pe.wait_ge(clo_done, G * (b + 1))
                for k in range(KT):
                    for q, (cp, w) in enumerate(((ctx_hi, w_hi), (ctx_lo, w_hi), (ctx_hi, w_lo))):
                        last = pe.matmul(aux[buf(use)][:], cp[:, k, tt * P:(tt + 1) * P], w[:, k, 3 * D:4 * D],
                                         start=(k == 0 and q == 0), stop=(k == KT - 1 and q == 2))
                last.then_inc(aux_done, 1)

            turned_product(0, 0, (0, 0))
            turned_product(1, 0, (0, 1))
            for s in range(TT):
                v_product(0, s, (0, 2 + s))
            for h in range(GH):
                for tp in range(NP if h < GH - 1 else 1):
                    scores_for_max(0, 0, h, tp)
            turn_maxima(0, 0, (0, 6))
            pe.wait_ge(ones_set, 4)
            turned_product(0, 1, (0, 7))
            turned_product(1, 1, (0, 8))

            def step(b, j):
                g = G * b + j
                first = isinstance(b, int) and g == 0

                def rows_out(tt):
                    if f"out{tt}" in uses(b, j):
                        out_product(b - 1, tt, use_no(b, j, f"out{tt}"))

                for h in range(GH):
                    unit = GH * g + h
                    scores(unit, g, j % 2, h, 0)
                    if f"v{h}" in uses(b, j) and h != 2:
                        v_product((j + 1) // 2 % 2, h, use_no(b, j, f"v{h}"))
                    if h == 2 and follows(b, j, 2):
                        turned_product(1, (j + 2) % G, use_no(b, j, "k"))
                    if h == 3:
                        rows_out(1)
                    if h > 0 or not first:
                        weigh_values(unit - 1, j if h > 0 else (j - 1) % G, (h - 1) % GH, 0)
                    if h == 0:
                        scores_for_max(g, j % 2, GH - 1, 1)
                    elif follows(b, j, 1):
                        scores_for_max(g + 1, (j + 1) % 2, h - 1, 1)
                    scores(unit, g, j % 2, h, 1)
                    if h == 1 and follows(b, j, 2):
                        if j == 2:
                            pe.wait_ge(x_turned, 32 * (b + 1))
                        turned_product(0, (j + 2) % G, use_no(b, j, "q"))
                    if h == 2 and "v2" in uses(b, j):
                        v_product((j + 1) // 2 % 2, 2, use_no(b, j, "v2"))
                    if h == 3:
                        rows_out(2)
                    if h > 0 or not first:
                        weigh_values(unit - 1, j if h > 0 else (j - 1) % G, (h - 1) % GH, 1)
                    if follows(b, j, 1):
                        scores_for_max(g + 1, (j + 1) % 2, h, 0)
                    if h == 0:
                        turn_maxima(g, 1, use_no(b, j, "max1"))
                    if h == 2 and follows(b, j, 1):
                        turn_maxima(g + 1, 0, use_no(b, j, "max0"))
                    if h == 2:
                        rows_out(0)
                    if h == 3:
                        rows_out(3)

            over_groups(pe, step)
            for pair in range(NP):
                weigh_values(UNITS - 1, G - 1, GH - 1, pair)
            for tt in range(TT):
                out_product(B - 1, tt, (B - 1, use_no(B - 1, 3, "max1")[1] + 1 + tt))


def recurrent_moe_attention_kernel(nc: bass.Bass, x: bass.AP, qkv_wT: bass.AP, qkv_b: bass.AP, out_wT: bass.AP,
                                   out_b: bass.AP, router_wT: bass.AP, e_bias: bass.AP, W_gate: bass.AP,
                                   W_up: bass.AP, W_down: bass.AP, gateT: bass.AP, upT: bass.AP, downT: bass.AP,
                                   out: bass.AP):
    def scratch(name, shape, dt=F32):
        return nc.dram_tensor(name, shape, dt, kind="Internal").ap()

    xn_rows = scratch("xn_rows", [ROWS, D])
    acc_rows = scratch("acc_rows", [ROWS, D])
    table = scratch("slot_table", [SLOTS, 2], I32)
    wb_hi = scratch("wb_hi", [D, 4 * D])
    wb_lo = scratch("wb_lo", [D, 4 * D])
    xT = scratch("xT", [B, 2, P, KT * S])

    with ExitStack() as ctx:
        ident = ctx.enter_context(nc.sbuf_tensor("ident", [P, P], F32))
        tokens_phase(nc, (ident,), x, router_wT, e_bias, gateT, upT, downT, qkv_wT, out_wT,
                     xn_rows, acc_rows, table, wb_hi, wb_lo, xT)

        w_hi = ctx.enter_context(nc.sbuf_tensor("w_hi", [P, KT, 4 * D], F32R))
        w_lo = ctx.enter_context(nc.sbuf_tensor("w_lo", [P, KT, 4 * D], F32R))
        xT_hi = ctx.enter_context(nc.sbuf_tensor("xT_hi", [P, KT, S], F32R))
        xT_lo = ctx.enter_context(nc.sbuf_tensor("xT_lo", [P, KT, S], F32R))
        next_loaded = ctx.enter_context(nc.semaphore("next_loaded"))

        def load_next(sp):
            for tile, rows in ((w_hi, wb_hi), (w_lo, wb_lo)):
                sp.dma_start(tile[:].bitcast(F32), rows.rearrange("(k p) n -> p k n", p=P)).then_inc(next_loaded, 16)
            for part, tile in enumerate((xT_hi, xT_lo)):
                sp.dma_start(tile[:].bitcast(F32), xT[0, part].rearrange("p (k s) -> p k s", k=KT)
                             ).then_inc(next_loaded, 16)

        def wait_next(sp):
            sp.wait_ge(next_loaded, 64)

        experts_phase(nc, (ident,), W_gate, W_up, W_down, xn_rows, acc_rows, table, load_next, wait_next)
        attention_phase(nc, (ident,), w_hi, w_lo, xT_hi, xT_lo, xT, x, acc_rows, qkv_b, out_b, out)


def kernel(**inputs):
    import numpy as _np
    import concourse.bacc as _bacc
    from concourse import mybir as _mybir
    from concourse.bass_utils import run_bass_kernel_spmd as _run

    attn = {n: inputs["L0_attn_" + n] for n in ("hidden_states", "Wqkv_w", "Wqkv_b", "out_w", "out_b")}
    ffn = {n: inputs["L0_ffn_" + n] for n in ("router_w", "e_bias", "W_gate", "W_up", "W_down",
                                              "shared_gate", "shared_up", "shared_down")}

    def qk_order(a):
        qk = a[:2 * D].reshape(2 * G, 2, GH // 2, HD, -1).transpose(0, 1, 3, 2, 4)
        return _np.concatenate([qk.reshape(2 * D, -1), a[2 * D:].reshape(D, -1)]).reshape(a.shape)

    laid_out = (
        ("x", attn["hidden_states"].reshape(T, D)),
        ("qkv_wT", qk_order(_np.asarray(attn["Wqkv_w"])).T), ("qkv_b", qk_order(_np.asarray(attn["Wqkv_b"]))),
        ("out_wT", attn["out_w"].T), ("out_b", attn["out_b"]),
        ("router_wT", ffn["router_w"].T), ("e_bias", ffn["e_bias"]),
        ("W_gate", ffn["W_gate"]), ("W_up", ffn["W_up"]), ("W_down", ffn["W_down"]),
        ("gateT", ffn["shared_gate"].T), ("upT", ffn["shared_up"].T), ("downT", ffn["shared_down"].T),
    )
    nc = _bacc.Bacc("TRN2", target_bir_lowering=False, num_devices=1)
    arrays, args = {}, []
    for name, a in laid_out:
        a = _np.ascontiguousarray(a)
        arrays[f"in_{name}_dram"] = a
        args.append(nc.dram_tensor(f"in_{name}_dram", a.shape, _mybir.dt.from_np(a.dtype), kind="ExternalInput").ap())
    args.append(nc.dram_tensor("out_0_dram", (T, D), _mybir.dt.from_np(_np.dtype("float32")), kind="ExternalOutput").ap())
    recurrent_moe_attention_kernel(nc, *args)
    r = _run(nc, [arrays], core_ids=[0])
    return r.results[0]["out_0_dram"].reshape(B, S, D)
```

```python
import concourse.bass as bass
from concourse import mybir
from contextlib import ExitStack

F32 = mybir.dt.float32
F32R = mybir.dt.float32r
BF16 = mybir.dt.bfloat16
I32 = mybir.dt.int32
U32 = mybir.dt.uint32
ALU = mybir.AluOpType
ACT = mybir.ActivationFunctionType
AX = mybir.AxisListType

P = 128
D = 512
KT = D // P
B, S = 8, 512
T = B * S
TT = S // P
H, HD = 16, 32
GH = P // HD
G = H // GH
E, K, NG, TKG = 32, 4, 8, 3
EG = E // NG
I = 256
IT = I // P
IS = 512
MT = IS // P
ROUTE_SCALE = 2.5
CAP = -(-5 * T // (4 * E))
HALF = CAP // 2
SLOTS = E * CAP
EPS = 1e-5
SENTINEL = 1.0e6
ROWS = T + CAP




def tokens_phase(nc, consts, x, router_wT, e_bias, gateT, upT, downT, qkvT, outT,
                 xn_rows, acc_rows, table, wb_hi, wb_lo, xT):
    ident, = consts
    KC = 29

    with ExitStack() as ctx:
        def sb(name, shape, dt=F32):
            return ctx.enter_context(nc.sbuf_tensor(name, shape, dt))

        def pb(name, shape):
            return ctx.enter_context(nc.psum_tensor(name, shape, F32))

        def sem(name):
            return ctx.enter_context(nc.semaphore(name))

        before = sb("before", [P, P], BF16)
        ones = sb("ones", [P, P], BF16)
        bias_row = sb("bias_row", [P, E])
        slot_base = sb("slot_base", [P, E])
        expert_no = sb("expert_no", [P, E])
        lower_no = sb("lower_no", [P, NG, NG])
        empty = sb("empty", [E, CAP, 2], I32)
        zero_rows = sb("zero_rows", [P, D])
        carrier = sb("carrier", [P, 2])
        rw_raw = sb("rw_raw", [P, KT, E])
        rw_both = sb("rw_both", [P, KT, 3 * E], F32R)
        lg_low = sb("lg_low", [E, S])
        lg_sum = sb("lg_sum", [E, S])
        sw_raw = sb("sw_raw", [P, 2, 3 * IS])
        sw_hi = sb("sw_hi", [P, KT, 3 * IS], F32R)
        sw_lo = sb("sw_lo", [P, KT, 3 * IS], F32R)
        wb_raw = sb("wb_raw", [P, 1024])
        wb_h = sb("wb_h", [P, 1024], F32R)
        wb_l = sb("wb_l", [P, 1024], F32R)
        xin = [sb(f"xin{i}", [P, TT, D]) for i in range(2)]
        xn = [sb(f"xn{i}", [P, TT, D]) for i in range(2)]
        xT_hi = [sb(f"xT_hi{i}", [P, KT, S], F32R) for i in range(2)]
        xT_lo = [sb(f"xT_lo{i}", [P, KT, S], F32R) for i in range(2)]
        stats = sb("stats", [P, TT, 6])
        mv = sb("mv", [P, TT, 2])
        var_eps = sb("var_eps", [P, TT])
        std = sb("std", [P, TT])
        rstd = sb("rstd", [P, TT])
        silu_g = sb("silu_g", [P, 2, S])
        hid = sb("hid", [P, 2, S])
        hid_hi = sb("hid_hi", [P, MT, S], F32R)
        hid_lo = sb("hid_lo", [P, MT, S], F32R)
        ybuf = sb("ybuf", [P, TT, D])
        score = sb("score", [P, TT, E])
        biased = sb("biased", [P, TT, E])
        pair_hi = sb("pair_hi", [P, TT * NG, 2])
        pair_lo = sb("pair_lo", [P, TT * NG, 2])
        top1 = sb("top1", [P, TT * NG])
        low1 = sb("low1", [P, TT * NG])
        low2 = sb("low2", [P, TT * NG])
        top2 = sb("top2", [P, TT * NG])
        gscore = sb("gscore", [P, TT, NG])
        above = sb("above", [P, TT, NG, NG])
        equal = sb("equal", [P, TT, NG, NG])
        rank = sb("rank", [P, TT, NG])
        gmask = sb("gmask", [P, TT, NG])
        masked0 = sb("masked0", [P, TT, E])
        masked = sb("masked", [P, TT, E])
        best = sb("best", [P, TT, 8])
        best_no = sb("best_no", [P, TT, 8], U32)
        best_f = sb("best_f", [P, TT, K])
        onehot = sb("onehot", [P, TT * K, E])
        chosen = sb("chosen", [P, TT, E], BF16)
        onehot_x = sb("onehot_x", [P, TT * K, E])
        weight = sb("weight", [P, TT, K])
        wsum = sb("wsum", [P, TT])
        wsum1 = sb("wsum1", [P, TT])
        wrec = sb("wrec", [P, TT])
        wnorm = sb("wnorm", [P, TT, K])
        carry = sb("carry", [P, E])
        place = sb("place", [P, TT, E])
        over = sb("over", [P, TT, E])
        slot0 = sb("slot0", [P, TT, E])
        slot = sb("slot", [P, TT, E])
        slot_x = sb("slot_x", [P, TT * K, E])
        slot_f = sb("slot_f", [P, TT * K])
        slot_no = sb("slot_no", [P, TT * K], U32)
        token_f = sb("token_f", [P, TT])
        entry = sb("entry", [P, TT, K, 2], I32)

        gu = [pb(f"gu{i}", [P, 2, S]) for i in range(2)]
        tp = pb("tp", [P, 2, S])
        lgT = pb("lgT", [P, S])
        lgpx = pb("lgpx", [P, 2 * TT + 1, E])
        lg = lgpx[:, 0:TT, :]
        px = lgpx[:, TT:2 * TT + 1, :]

        consts_done = sem("a_consts")
        table_set = sem("a_table_set")
        x_loaded = [sem(f"a_x_loaded{i}") for i in range(2)]
        xn_stored = [sem(f"a_xn_stored{i}") for i in range(2)]
        xT_stored = [sem(f"a_xT_stored{i}") for i in range(2)]
        y_stored = sem("a_y_stored")
        sw_loaded = [sem(f"a_sw_loaded{i}") for i in range(2)]
        dn_loaded = [sem(f"a_dn_loaded{i}") for i in range(2)]
        rw_loaded = sem("a_rw_loaded")
        split_hi = sem("a_split_hi")
        split_lo = sem("a_split_lo")
        wb_loaded = sem("a_wb_loaded")
        wb_split = sem("a_wb_split")
        wb_own = sem("a_wb_own")
        wb_stored = sem("a_wb_stored")
        stat_step = sem("a_stat_step")
        var_ready = sem("a_var_ready")
        std_ready = sem("a_std_ready")
        ln_done = sem("a_ln_done")
        tr_done = sem("a_tr_done")
        xhi_done = sem("a_xhi_done")
        xlo_done = sem("a_xlo_done")
        lgT_done = sem("a_lgT_done")
        lg_low_copied = sem("a_lg_low_copied")
        lg_summed = sem("a_lg_summed")
        logits_done = sem("a_logits_done")
        score_done = sem("a_score_done")
        route_step = sem("a_route_step")
        chosen_done = sem("a_chosen_done")
        prefix_done = sem("a_prefix_done")
        entry_done = sem("a_entry_done")
        scattered = sem("a_scattered")
        gu_done = sem("a_gu_done")
        silu_done = sem("a_silu_done")
        hid_done = sem("a_hid_done")
        hhi_done = sem("a_hhi_done")
        hlo_done = sem("a_hlo_done")
        down_done = sem("a_down_done")
        y_copied = sem("a_y_copied")

        x_v = x.rearrange("(b t p) d -> b p t d", p=P, t=TT)
        xn_v = xn_rows[0:T, :].rearrange("(b t p) d -> b p t d", p=P, t=TT)
        acc_v = acc_rows[0:T, :].rearrange("(b t p) d -> b p t d", p=P, t=TT)

        block = ctx.enter_context(nc.Block())

        @block.sync
        def _(sp):
            sp.dma_start(xin[0][:], x_v[0]).then_inc(x_loaded[0], 16)
            sp.dma_start(rw_raw[:], router_wT.rearrange("(k p) e -> p k e", p=P)).then_inc(rw_loaded, 16)
            sp.dma_start(bias_row[:], e_bias.rearrange("(a e) -> a e", a=1).to_broadcast([P, E])
                         ).then_inc(rw_loaded, 16)
            for k in range(KT):
                if k >= 2:
                    sp.wait_ge(split_lo, k)
                for j, w in enumerate((gateT, upT)):
                    sp.dma_start(sw_raw[:, k % 2, j * IS:(j + 1) * IS], w[k * P:(k + 1) * P, :]
                                 ).then_inc(sw_loaded[k % 2], 16)
            for k in range(KT):
                if k >= 2:
                    sp.wait_ge(split_lo, KT + k)
                sp.dma_start(sw_raw[:, k % 2, 2 * IS:3 * IS], downT[k * P:(k + 1) * P, :]
                             ).then_inc(dn_loaded[k % 2], 16)
                if k == 1:
                    sp.dma_start(xin[1][:], x_v[1]).then_inc(x_loaded[1], 16)
            def two_batches(i):
                for u in range(2):
                    n = 2 * i + u
                    c, d = u, 1 - u
                    sp.wait_ge(wb_stored, 32 * n)
                    if u == 0:
                        sp.dma_start(wb_raw[:], qkvT[bass.ts(i, P), 0:1024]).then_inc(wb_loaded, 32)
                    else:
                        sp.dma_start(wb_raw[:, 0:512], qkvT[bass.ts(i, P), 1024:1536]).then_inc(wb_loaded, 16)
                        sp.dma_start(wb_raw[:, 512:1024], outT[bass.ts(i, P), :]).then_inc(wb_loaded, 16)
                    sp.wait_ge(ln_done, n + 1)
                    sp.dma_start(xin[c][:], x_v[(n + 2) % B]).then_inc(x_loaded[c], 16)
                    sp.dma_start(xn_v[n], xn[c][:]).then_inc(xn_stored[c], 16)
                    sp.wait_ge(wb_split, n + 1)
                    sp.dma_start(wb_hi[bass.ts(i, P), u * 1024:(u + 1) * 1024], wb_h[:].bitcast(F32)).then_inc(wb_stored, 16)
                    sp.dma_start(wb_lo[bass.ts(i, P), u * 1024:(u + 1) * 1024], wb_l[:].bitcast(F32)).then_inc(wb_stored, 16)
                    sp.wait_ge(xlo_done, 2 * n + 2)
                    for part, xt in enumerate((xT_hi[c], xT_lo[c])):
                        sp.dma_start(xT[n, part].rearrange("p (k s) -> p k s", k=KT), xt[:].bitcast(F32)
                                     ).then_inc(xT_stored[c], 16)
                    sp.wait_ge(y_copied, TT * (n + 1))
                    sp.dma_start(acc_v[n], ybuf[:]).then_inc(y_stored, 16)

            two_batches(0)
            with sp.Fori(1, B // 2) as i:
                two_batches(i)
            sp.wait_ge(y_stored, 16 * B)
            sp.wait_ge(wb_stored, 32 * B)
            for c in range(2):
                sp.wait_ge(xn_stored[c], 16 * (B // 2))
                sp.wait_ge(xT_stored[c], 32 * (B // 2))
                sp.wait_ge(x_loaded[c], 16 * (B // 2 + 1))

        @block.gpsimd
        def _(pool):
            pool.memset(ident[:], 0.0).then_inc(wb_own, 1)
            pool.memset(before[:], 0.0).then_inc(wb_own, 1)
            pool.memset(lower_no[:], 0.0).then_inc(wb_own, 1)
            pool.memset(ones[:], 1.0).then_inc(consts_done, 1)
            pool.memset(zero_rows[:], 0.0).then_inc(consts_done, 1)
            pool.memset(carry[:], 0.0).then_inc(consts_done, 1)
            pool.memset(empty[:], 0).then_inc(wb_own, 1)
            pool.wait_ge(wb_own, 4)
            pool.affine_select(out=ident[:], in_=ident[:], compare_op=ALU.not_equal, fill=1.0, base=0,
                               pattern=[[-1, P]], channel_multiplier=1).then_inc(consts_done, 1)
            pool.affine_select(out=before[:], in_=before[:], compare_op=ALU.is_ge, fill=1.0, base=0,
                               pattern=[[-1, P]], channel_multiplier=1).then_inc(consts_done, 1)
            pool.affine_select(out=lower_no[:], in_=lower_no[:], compare_op=ALU.is_ge, fill=1.0, base=0,
                               pattern=[[-1, NG], [1, NG]], channel_multiplier=0).then_inc(consts_done, 1)
            pool.iota(slot_base[:], [[CAP, E]], base=0, channel_multiplier=0,
                      allow_small_or_imprecise_dtypes=True).then_inc(consts_done, 1)
            pool.iota(expert_no[:], [[1, E]], base=0, channel_multiplier=0,
                      allow_small_or_imprecise_dtypes=True).then_inc(consts_done, 1)
            pool.iota(token_f[:], [[P, TT]], base=0, channel_multiplier=1,
                      allow_small_or_imprecise_dtypes=True).then_inc(consts_done, 1)
            pool.iota(empty[:, :, 0], [[1, CAP]], base=T, channel_multiplier=0).then_inc(consts_done, 1)
            pool.wait_ge(consts_done, 10)
            pool.dma_start(table.rearrange("(e s) c -> e s c", e=E), empty[:]).then_inc(table_set, 16)
            for rows in (xn_rows, acc_rows):
                pool.dma_start(rows[T:T + P, :], zero_rows[:]).then_inc(table_set, 16)
                pool.dma_start(rows[T + P:ROWS, :], zero_rows[0:CAP - P, :]).then_inc(table_set, 16)
            pool.wait_ge(table_set, 16 * 5)
            def batch(n):
                pool.wait_ge(wb_loaded, 32 * n + 32)
                pool.tensor_tensor(wb_h[:], wb_raw[:], zero_rows[:, 0:1].to_broadcast([P, 1024]), ALU.add
                                   ).then_inc(wb_own, 1)
                pool.wait_ge(wb_own, n + 5)
                pool.tensor_tensor(wb_l[:], wb_raw[:], wb_h[:].bitcast(F32), ALU.subtract).then_inc(wb_split, 1)
                pool.wait_ge(entry_done, 2 * n + 2)
                pool.tensor_tensor(carrier[:, 0:1], zero_rows[:, 0:1], zero_rows[:, 1:2], ALU.add)
                for t in range(TT):
                    for k in range(K):
                        j = t * K + k
                        pool.indirect_dma_start(
                            out=table, out_offset=bass.IndirectOffsetOnAxis(ap=slot_no[:, j:j + 1], axis=0),
                            in_=entry[:, t, k, :], in_offset=None, bounds_check=SLOTS - 1, oob_is_err=False,
                        ).then_inc(scattered, 16)

            batch(0)
            with pool.Fori(1, B) as n:
                batch(n)
            pool.wait_ge(scattered, 16 * TT * K * B)

        @block.scalar
        def _(act):
            def std_of(m):
                act.wait_ge(var_ready, m + 1)
                act.activation(std[:], var_eps[:], ACT.Sqrt).then_inc(std_ready, 1)

            def xhi(m, buf, pair):
                act.wait_ge(tr_done, 2 * m + pair + 1)
                act.activation(xT_hi[buf][:, 2 * pair:2 * pair + 2, :], tp[:], ACT.Copy).then_inc(xhi_done, 1)

            std_of(0)
            act.wait_ge(rw_loaded, 32)
            act.activation(rw_both[:, :, 0:E], rw_raw[:], ACT.Copy).then_inc(split_hi, 1)
            act.activation(rw_both[:, :, 2 * E:3 * E], rw_raw[:], ACT.Copy)
            for k in range(KT):
                act.wait_ge(sw_loaded[k % 2], 32 * (k // 2 + 1))
                act.activation(sw_hi[:, k, 0:2 * IS], sw_raw[:, k % 2, 0:2 * IS], ACT.Copy).then_inc(split_hi, 1)
            for pair in range(2):
                xhi(0, 0, pair)
            for k in range(KT):
                act.wait_ge(dn_loaded[k % 2], 16 * (k // 2 + 1))
                act.activation(sw_hi[:, k, 2 * IS:3 * IS], sw_raw[:, k % 2, 2 * IS:3 * IS], ACT.Copy
                               ).then_inc(split_hi, 1)
            std_of(1)
            def two_batches(i):
                for u in range(2):
                    n = 2 * i + u
                    c, d = u, 1 - u

                    def silu(mt):
                        act.wait_ge(gu_done, MT * n + mt + 1)
                        act.activation(silu_g[:, mt % 2, :], gu[mt % 2][:, 0, :], ACT.Silu).then_inc(silu_done, 1)

                    def hid_high(mt):
                        if mt == 0:
                            act.wait_ge(down_done, TT * n)
                        act.wait_ge(hid_done, MT * n + mt + 1)
                        act.activation(hid_hi[:, mt, :], hid[:, mt % 2, :], ACT.Copy).then_inc(hhi_done, 1)

                    act.wait_ge(lgT_done, n + 1)
                    act.wait_ge(lg_summed, n)
                    act.activation(lg_low[:], lgT[E:2 * E, :], ACT.Copy).then_inc(lg_low_copied, 1)
                    act.wait_ge(logits_done, n + 1)
                    act.activation(score[:], lg, ACT.Sigmoid).then_inc(score_done, 1)
                    silu(0)
                    hid_high(0)
                    silu(1)
                    hid_high(1)
                    act.wait_ge(xT_stored[d], 32 * (i + u))
                    xhi(n + 1, d, 0)
                    silu(2)
                    hid_high(2)
                    xhi(n + 1, d, 1)
                    silu(3)
                    hid_high(3)
                    act.wait_ge(y_stored, 16 * n)
                    for t in range(TT):
                        act.wait_ge(down_done, TT * n + t + 1)
                        act.activation(ybuf[:, t, :], tp[:, t % 2, :], ACT.Copy).then_inc(y_copied, 1)
                    std_of(n + 2)

            two_batches(0)
            with act.Fori(1, B // 2) as i:
                two_batches(i)

        @block.vector
        def _(dve):
            def statistics(m, buf, loads):
                dve.wait_ge(x_loaded[buf], 16 * loads)
                for t in range(TT):
                    last = dve.bn_stats(stats[:, t, :], xin[buf][:, t, :])
                last.then_inc(stat_step, 1)
                dve.wait_ge(stat_step, 3 * m + 1)
                dve.memset(carrier[:, 1:2], 0.0)
                for t in range(TT):
                    last = dve.bn_aggr(mv[:, t, :], stats[:, t, :])
                last.then_inc(stat_step, 1)
                dve.wait_ge(stat_step, 3 * m + 2)
                dve.tensor_scalar(var_eps[:], mv[:, :, 1], EPS, None, ALU.add).then_inc(var_ready, 1)

            def normalise(m, buf, stores):
                dve.wait_ge(std_ready, m + 1)
                dve.reciprocal(rstd[:], std[:]).then_inc(stat_step, 1)
                dve.wait_ge(stat_step, 3 * m + 3)
                dve.wait_ge(xn_stored[buf], 16 * stores)
                for t in range(TT):
                    last = dve.tensor_scalar(xn[buf][:, t, :], xin[buf][:, t, :], mv[:, t, 0:1], rstd[:, t:t + 1],
                                             ALU.subtract, ALU.mult)
                last.then_inc(ln_done, 1)

            def xlo(m, buf, pair):
                dve.wait_ge(xhi_done, 2 * m + pair + 1)
                dve.tensor_tensor(xT_lo[buf][:, 2 * pair:2 * pair + 2, :], tp[:],
                                  xT_hi[buf][:, 2 * pair:2 * pair + 2, :].bitcast(F32), ALU.subtract
                                  ).then_inc(xlo_done, 1)

            statistics(0, 0, 1)
            normalise(0, 0, 0)
            dve.wait_ge(split_hi, 1)
            dve.tensor_tensor(rw_both[:, :, E:2 * E], rw_raw[:], rw_both[:, :, 0:E].bitcast(F32), ALU.subtract
                              ).then_inc(split_lo, 1)
            for k in range(KT):
                dve.wait_ge(split_hi, k + 2)
                dve.tensor_tensor(sw_lo[:, k, 0:2 * IS], sw_raw[:, k % 2, 0:2 * IS],
                                  sw_hi[:, k, 0:2 * IS].bitcast(F32), ALU.subtract).then_inc(split_lo, 1)
            for pair in range(2):
                xlo(0, 0, pair)
            for k in range(KT):
                dve.wait_ge(split_hi, KT + k + 2)
                dve.tensor_tensor(sw_lo[:, k, 2 * IS:3 * IS], sw_raw[:, k % 2, 2 * IS:3 * IS],
                                  sw_hi[:, k, 2 * IS:3 * IS].bitcast(F32), ALU.subtract).then_inc(split_lo, 1)
            statistics(1, 1, 1)
            dve.wait_ge(consts_done, 10)
            def two_batches(i):
                for u in range(2):
                    n = 2 * i + u
                    c, d = u, 1 - u
                    steps = [0]

                    def step(ins):
                        steps[0] += 1
                        ins.then_inc(route_step, 1)
                        dve.wait_ge(route_step, KC * n + steps[0])

                    def hidden(mt):
                        dve.wait_ge(silu_done, MT * n + mt + 1)
                        dve.tensor_tensor(hid[:, mt % 2, :], silu_g[:, mt % 2, :], gu[mt % 2][:, 1, :], ALU.mult
                                          ).then_inc(hid_done, 1)

                    def hid_low(mt):
                        dve.wait_ge(hhi_done, MT * n + mt + 1)
                        dve.tensor_tensor(hid_lo[:, mt, :], hid[:, mt % 2, :], hid_hi[:, mt, :].bitcast(F32),
                                          ALU.subtract).then_inc(hlo_done, 1)

                    def pick_groups():
                        dve.wait_ge(score_done, n + 1)
                        step(dve.tensor_tensor(biased[:], score[:], bias_row[:].unsqueeze(1).to_broadcast([P, TT, E]),
                                               ALU.add))
                        four = biased[:].rearrange("p t (g a b) -> p (t g) a b", a=2, b=2)
                        dve.tensor_tensor(pair_hi[:], four[:, :, :, 0], four[:, :, :, 1], ALU.max)
                        step(dve.tensor_tensor(pair_lo[:], four[:, :, :, 0], four[:, :, :, 1], ALU.min))
                        dve.tensor_tensor(top1[:], pair_hi[:, :, 0], pair_hi[:, :, 1], ALU.max)
                        dve.tensor_tensor(low1[:], pair_hi[:, :, 0], pair_hi[:, :, 1], ALU.min)
                        step(dve.tensor_tensor(low2[:], pair_lo[:, :, 0], pair_lo[:, :, 1], ALU.max))
                        step(dve.tensor_tensor(top2[:], low1[:], low2[:], ALU.max))
                        step(dve.tensor_tensor(gscore[:].rearrange("p t g -> p (t g)"), top1[:], top2[:], ALU.add))
                        other = gscore[:].unsqueeze(2).to_broadcast([P, TT, NG, NG])
                        own = gscore[:].unsqueeze(3).to_broadcast([P, TT, NG, NG])
                        dve.tensor_tensor(above[:], other, own, ALU.is_gt)
                        step(dve.tensor_tensor(equal[:], other, own, ALU.is_equal))
                        step(dve.tensor_tensor(equal[:], equal[:],
                                               lower_no[:].unsqueeze(1).to_broadcast([P, TT, NG, NG]), ALU.mult))
                        step(dve.tensor_tensor(above[:], above[:], equal[:], ALU.add))
                        step(dve.tensor_reduce(rank[:], above[:], AX.X, ALU.add))
                        step(dve.tensor_scalar(gmask[:], rank[:], TKG - 0.5, None, ALU.is_lt))
                        step(dve.tensor_tensor(masked0[:].rearrange("p t (g a) -> p (t g) a", a=EG),
                                               biased[:].rearrange("p t (g a) -> p (t g) a", a=EG),
                                               gmask[:].rearrange("p t g -> p (t g)").unsqueeze(2)
                                               .to_broadcast([P, TT * NG, EG]), ALU.mult))
                        step(dve.tensor_scalar(masked[:], masked0[:], 0.0, None, ALU.add))

                    def pick_experts():
                        for t in range(TT):
                            last = dve.max(best[:, t, :], masked[:, t, :])
                        step(last)
                        dve.memset(carrier[:, 1:2], 0.0)
                        for t in range(TT):
                            last = dve.max_index(best_no[:, t, :], best[:, t, :], masked[:, t, :])
                        step(last)
                        step(dve.tensor_copy(best_f[:], best_no[:, :, 0:K]))
                        step(dve.tensor_tensor(
                            onehot[:], best_f[:].rearrange("p t k -> p (t k)").unsqueeze(2).to_broadcast([P, TT * K, E]),
                            expert_no[:].unsqueeze(1).to_broadcast([P, TT * K, E]), ALU.is_equal))
                        with nc.allow_low_precision(reason="0 or 1"):
                            dve.tensor_reduce(chosen[:], onehot[:].rearrange("p (t k) e -> p t e k", k=K), AX.X, ALU.add
                                              ).then_inc(chosen_done, 1)

                    def weigh():
                        for t in range(TT):
                            last = dve.tensor_tensor(onehot_x[:, t * K:(t + 1) * K, :], onehot[:, t * K:(t + 1) * K, :],
                                                     score[:, t, :].unsqueeze(1).to_broadcast([P, K, E]), ALU.mult)
                        step(last)
                        step(dve.tensor_reduce(weight[:].rearrange("p t k -> p (t k)"), onehot_x[:], AX.X, ALU.add))
                        step(dve.tensor_reduce(wsum[:], weight[:], AX.X, ALU.add))
                        step(dve.tensor_scalar(wsum1[:], wsum[:], 1e-20, None, ALU.add))
                        step(dve.reciprocal(wrec[:], wsum1[:]))
                        step(dve.tensor_tensor(wnorm[:], weight[:], wrec[:].unsqueeze(2).to_broadcast([P, TT, K]),
                                               ALU.mult))
                        dve.wait_ge(scattered, 16 * TT * K * n)
                        dve.tensor_scalar(entry[:, :, :, 1].bitcast(F32), wnorm[:], ROUTE_SCALE, None, ALU.mult
                                          ).then_inc(entry_done, 1)

                    def place_tokens():
                        dve.wait_ge(prefix_done, n + 1)
                        step(dve.tensor_tensor(place[:], px[:, 0:TT, :], carry[:].unsqueeze(1).to_broadcast([P, TT, E]),
                                               ALU.add))
                        dve.tensor_tensor(carry[:], px[:, TT, :], carry[:], ALU.add)
                        dve.tensor_scalar(over[:], place[:], CAP - 0.5, SENTINEL, ALU.is_gt, ALU.mult)
                        step(dve.tensor_tensor(slot0[:], place[:], slot_base[:].unsqueeze(1).to_broadcast([P, TT, E]),
                                               ALU.add))
                        step(dve.tensor_tensor(slot[:], slot0[:], over[:], ALU.add))
                        for t in range(TT):
                            last = dve.tensor_tensor(slot_x[:, t * K:(t + 1) * K, :], onehot[:, t * K:(t + 1) * K, :],
                                                     slot[:, t, :].unsqueeze(1).to_broadcast([P, K, E]), ALU.mult)
                        step(last)
                        step(dve.tensor_reduce(slot_f[:], slot_x[:], AX.X, ALU.add))
                        step(dve.tensor_copy(entry[:, :, :, 0], token_f[:].unsqueeze(2).to_broadcast([P, TT, K])))
                        dve.tensor_copy(slot_no[:], slot_f[:]).then_inc(entry_done, 1)
                        step(dve.tensor_scalar(token_f[:], token_f[:], float(S), None, ALU.add))

                    normalise(n + 1, d, i + u)
                    dve.wait_ge(lg_low_copied, n + 1)
                    dve.tensor_tensor(lg_sum[:], lgT[0:E, :], lg_low[:], ALU.add).then_inc(lg_summed, 1)
                    hidden(0)
                    pick_groups()
                    hid_low(0)
                    hidden(1)
                    pick_experts()
                    hid_low(1)
                    xlo(n + 1, d, 0)
                    hidden(2)
                    weigh()
                    hid_low(2)
                    xlo(n + 1, d, 1)
                    place_tokens()
                    hidden(3)
                    hid_low(3)
                    statistics(n + 2, c, i + 2)
                    assert steps[0] == KC, steps

            two_batches(0)
            with dve.Fori(1, B // 2) as i:
                two_batches(i)

        @block.tensor
        def _(pe):
            def transposes(m, buf, pair):
                for k in range(2 * pair, 2 * pair + 2):
                    for t in range(TT):
                        last = pe.transpose(tp[:, k % 2, t * P:(t + 1) * P], xn[buf][:, t, k * P:(k + 1) * P], ident[:])
                last.then_inc(tr_done, 1)

            pe.wait_ge(consts_done, 10)
            pe.wait_ge(ln_done, 1)
            transposes(0, 0, 0)
            pe.wait_ge(xlo_done, 1)
            transposes(0, 0, 1)
            pe.wait_ge(split_lo, KT + 1)
            def two_batches(i):
                for u in range(2):
                    n = 2 * i + u
                    c, d = u, 1 - u
                    parts = ((xT_hi[c], 0), (xT_lo[c], 0), (xT_hi[c], 1))

                    def gate_up(mt):
                        for j in range(2):
                            if mt == 0 and j == 1:
                                pe.wait_ge(lg_summed, n + 1)
                                pe.wait_ge(score_done, n)
                            at = j * IS + mt * P
                            for k in range(KT):
                                for q, (xt, low) in enumerate(parts):
                                    w = sw_lo if low else sw_hi
                                    last = pe.matmul(gu[mt % 2][:, j, :], w[:, k, at:at + P], xt[:, k, :],
                                                     start=(k == 0 and q == 0), stop=(k == KT - 1 and q == 2))
                        last.then_inc(gu_done, 1)

                    pe.wait_ge(xlo_done, 2 * n + 2)
                    pe.wait_ge(lg_summed, n)
                    for k in range(KT):
                        for q, xt in enumerate((xT_hi[c], xT_lo[c])):
                            last = pe.matmul(lgT[0:3 * E, :], rw_both[:, k, :], xt[:, k, :],
                                             start=(k == 0 and q == 0), stop=(k == KT - 1 and q == 1))
                    last.then_inc(lgT_done, 1)
                    pe.wait_ge(hid_done, MT * n)
                    gate_up(0)
                    for t in range(TT):
                        last = pe.transpose(lg[:, t, :], lg_sum[:, t * P:(t + 1) * P], ident[0:E, 0:E])
                    last.then_inc(logits_done, 1)
                    gate_up(1)
                    pe.wait_ge(ln_done, n + 2)
                    pe.wait_ge(y_copied, TT * n)
                    transposes(n + 1, d, 0)
                    pe.wait_ge(hid_done, MT * n + 1)
                    gate_up(2)
                    pe.wait_ge(xlo_done, 2 * n + 3)
                    transposes(n + 1, d, 1)
                    pe.wait_ge(chosen_done, n + 1)
                    for t in range(TT + 1):
                        if t < TT:
                            pe.matmul(px[:, t, :], before[:], chosen[:, t, :], start=True, stop=(t == 0))
                        for j in range(t):
                            last = pe.matmul(px[:, t, :], ones[:], chosen[:, j, :], start=(t == TT and j == 0),
                                             stop=(j == t - 1))
                    last.then_inc(prefix_done, 1)
                    pe.wait_ge(hid_done, MT * n + 2)
                    gate_up(3)
                    pe.wait_ge(xlo_done, 2 * n + 4)
                    pe.wait_ge(split_lo, 2 * KT + 1)

                    def down(t, slices):
                        for mt in slices:
                            for q, (hp, w) in enumerate(((hid_hi, sw_hi), (hid_lo, sw_hi), (hid_hi, sw_lo))):
                                last = pe.matmul(tp[:, t % 2, :], hp[:, mt, t * P:(t + 1) * P], w[:, mt, 2 * IS:3 * IS],
                                                 start=(mt == 0 and q == 0), stop=(mt == MT - 1 and q == 2))
                        return last

                    pe.wait_ge(hlo_done, MT * n + MT - 1)
                    for t in range(2):
                        down(t, range(MT - 1))
                    pe.wait_ge(hlo_done, MT * n + MT)
                    for t in range(2):
                        down(t, (MT - 1,)).then_inc(down_done, 1)
                    for t in range(2, TT):
                        pe.wait_ge(y_copied, TT * n + t - 1)
                        down(t, range(MT)).then_inc(down_done, 1)

            two_batches(0)
            with pe.Fori(1, B // 2) as i:
                two_batches(i)


def experts_phase(nc, consts, W_gate, W_up, W_down, xn_rows, acc_rows, table, load_next, wait_next):
    ident, = consts
    C2 = 2 * CAP

    with ExitStack() as ctx:
        def sb(name, shape, dt=F32):
            return ctx.enter_context(nc.sbuf_tensor(name, shape, dt))

        def pb(name, shape):
            return ctx.enter_context(nc.psum_tensor(name, shape, F32))

        def sem(name):
            return ctx.enter_context(nc.semaphore(name))

        ids_g = [sb(f"ids_g{i}", [HALF, 2, 2], I32) for i in range(2)]
        ids_s = [sb(f"ids_s{i}", [HALF, 2, 2], I32) for i in range(2)]
        raw_gu = [sb(f"raw_gu{i}", [P, 2, KT, I]) for i in range(2)]
        gu_hi = [sb(f"gu_hi{i}", [P, 2, KT, I], F32R) for i in range(2)]
        gu_lo = [sb(f"gu_lo{i}", [P, 2, KT, I], F32R) for i in range(2)]
        raw_dn = [sb(f"raw_dn{i}", [P, IT, D]) for i in range(2)]
        dn_hi = [sb(f"dn_hi{i}", [P, IT, D], F32R) for i in range(2)]
        dn_lo = [sb(f"dn_lo{i}", [P, IT, D], F32R) for i in range(2)]
        xs = [sb(f"xs{i}", [HALF, 2, D]) for i in range(2)]
        xt = [sb(f"xt{i}", [P, KT, 2, CAP], F32R) for i in range(2)]
        gu_low = sb("gu_low", [P, IT, 2, CAP])
        gu_sum = sb("gu_sum", [P, IT, 2, CAP])
        silu_e = sb("silu_e", [P, IT, CAP])
        hid_e = sb("hid_e", [P, IT, CAP])
        he_hi = [sb(f"he_hi{i}", [P, IT, CAP], F32R) for i in range(2)]
        he_lo = [sb(f"he_lo{i}", [P, IT, CAP], F32R) for i in range(2)]
        ys = [sb(f"ys{i}", [HALF, 2, D]) for i in range(2)]
        carrier = sb("carrier_e", [P, 2])

        gup = [pb(f"gup{i}", [P, 2, 512]) for i in range(IT)]
        tpe = pb("tpe", [P, 2, 512])
        yp = pb("yp", [P, 2, D])

        zeroed = sem("e_zeroed")
        gu_loaded = [sem(f"e_gu_loaded{i}") for i in range(2)]
        dn_loaded = [sem(f"e_dn_loaded{i}") for i in range(2)]
        idg_loaded = [sem(f"e_idg_loaded{i}") for i in range(2)]
        ids_loaded = [sem(f"e_ids_loaded{i}") for i in range(2)]
        gathered = [sem(f"e_gathered{i}") for i in range(2)]
        scattered = sem("e_scattered")
        carried = sem("e_carried")
        gu_high = sem("e_gu_high")
        vector_low = sem("e_vector_low")
        pool_low = sem("e_pool_low")
        dn_high = sem("e_dn_high")
        dn_low = sem("e_dn_low")
        tr_done = sem("e_tr_done")
        xhi_done = sem("e_xhi_done")
        xlo_done = sem("e_xlo_done")
        gu_done = sem("e_gu_done")
        low_copied = sem("e_low_copied")
        summed = sem("e_summed")
        silu_done = sem("e_silu_done")
        hid_done = sem("e_hid_done")
        hhi_done = sem("e_hhi_done")
        hlo_done = sem("e_hlo_done")
        down_done = sem("e_down_done")
        y_done = sem("e_y_done")

        gate_v = W_gate.rearrange("e (p k) i -> e p k i", k=KT)
        up_v = W_up.rearrange("e (p k) i -> e p k i", k=KT)
        down_v = W_down.rearrange("e (p k) n -> e p k n", k=IT)
        table_v = table.rearrange("(e h p) c -> e p h c", e=E, h=2)

        VS = 5

        def slices(tile, first, end):
            return tile[:].rearrange("p j k i -> p (j k) i")[:, first:end]

        PEEL = 6

        def over_experts(engine, body):
            for e in range(2):
                body(e, 0, e)
            with engine.Fori(1, (E - PEEL) // 2) as i:
                for u in range(2):
                    body(2 * i + u, i, u)
            for e in range(E - PEEL, E):
                body(e, e // 2, e % 2)

        def exists(e, ahead):
            return not isinstance(e, int) or e + ahead < E

        block = ctx.enter_context(nc.Block())

        @block.sync
        def _(sp):
            def load_gu(e, c):
                sp.dma_start(raw_gu[c][:, 0], gate_v[e]).then_inc(gu_loaded[c], 16)
                sp.dma_start(raw_gu[c][:, 1], up_v[e]).then_inc(gu_loaded[c], 16)

            def load_dn(e, c):
                sp.dma_start(raw_dn[c][:], down_v[e]).then_inc(dn_loaded[c], 16)

            for e in range(2):
                sp.dma_start(ids_g[e][:], table_v[e]).then_inc(idg_loaded[e], 16)
                load_gu(e, e)
            load_dn(0, 0)
            sp.dma_start(ids_s[0][:], table_v[0]).then_inc(ids_loaded[0], 16)
            for e in (2, 3):
                sp.wait_ge(gathered[e - 2], 32)
                sp.dma_start(ids_g[e - 2][:], table_v[e]).then_inc(idg_loaded[e - 2], 16)
            load_dn(1, 1)
            sp.wait_ge(gu_high, 1)
            sp.wait_ge(vector_low, 1)
            sp.wait_ge(pool_low, 1)
            load_gu(2, 0)
            load_next(sp, 0)

            def body(e, i, u):
                c, d = u, 1 - u
                if exists(e, 3):
                    sp.wait_ge(gu_high, e + 2)
                    sp.wait_ge(vector_low, e + 2)
                    sp.wait_ge(pool_low, e + 2)
                    load_gu(e + 3, d)
                if exists(e, 2):
                    sp.wait_ge(dn_high, e + 1)
                    sp.wait_ge(dn_low, e + 1)
                    load_dn(e + 2, c)
                if exists(e, 1):
                    sp.wait_ge(scattered, 32 * e)
                    sp.dma_start(ids_s[d][:], table_v[e + 1]).then_inc(ids_loaded[d], 16)
                if exists(e, 4):
                    sp.wait_ge(gathered[c], 32 * (i + 2))
                    sp.dma_start(ids_g[c][:], table_v[e + 4]).then_inc(idg_loaded[c], 16)
                if isinstance(e, int) and e >= E - PEEL:
                    load_next(sp, e - (E - PEEL) + 1)

            over_experts(sp, body)
            sp.wait_ge(scattered, 32 * E)
            wait_next(sp)

        @block.gpsimd
        def _(pool):
            pool.memset(carrier[:], 0.0).then_inc(zeroed, 1)
            pool.wait_ge(zeroed, 1)

            def carry(earlier):
                pool.wait_ge(carried, earlier)
                pool.tensor_tensor(carrier[:, 0:1], carrier[:, 1:2], carrier[:, 1:2], ALU.add).then_inc(carried, 1)

            def gather(c, uses, earlier):
                pool.wait_ge(idg_loaded[c], 16 * uses)
                carry(earlier)
                for h in range(2):
                    pool.indirect_dma_start(
                        out=xs[c][:, h, :], out_offset=None, in_=xn_rows,
                        in_offset=bass.IndirectOffsetOnAxis(ap=ids_g[c][:, h, 0:1].bitcast(U32), axis=0),
                        bounds_check=ROWS - 1, oob_is_err=True).then_inc(gathered[c], 16)

            def pool_part(e, c):
                pool.wait_ge(gu_high, e + 1)
                pool.tensor_tensor(slices(gu_lo[c], VS, 2 * KT), slices(raw_gu[c], VS, 2 * KT),
                                   slices(gu_hi[c], VS, 2 * KT).bitcast(F32), ALU.subtract).then_inc(pool_low, 1)

            gather(0, 1, 0)
            gather(1, 1, 1)
            pool_part(0, 0)
            pool_part(1, 1)
            pool.wait_ge(tr_done, 1)
            gather(0, 2, 2)

            def body(e, i, u):
                c, d = u, 1 - u
                if exists(e, 3):
                    pool.wait_ge(tr_done, e + 2)
                    gather(d, i + 2 + u, 3 + 2 * e)
                if exists(e, 2):
                    pool_part(e + 2, c)
                pool.wait_ge(scattered, 32 * e)
                pool.wait_ge(y_done, 2 * e + 2)
                carry(4 + 2 * e if exists(e, 3) else 3 + (E - 3) + e)
                for h in range(2):
                    pool.indirect_dma_start(
                        out=acc_rows, in_=ys[c][:, h, :], in_offset=None,
                        out_offset=bass.IndirectOffsetOnAxis(ap=ids_s[c][:, h, 0:1].bitcast(U32), axis=0),
                        bounds_check=ROWS - 1, oob_is_err=True, compute_op=ALU.add).then_inc(scattered, 16)

            over_experts(pool, body)

        @block.scalar
        def _(act):
            def split_gu(e, c, uses):
                act.wait_ge(gu_loaded[c], 32 * uses)
                act.activation(gu_hi[c][:], raw_gu[c][:], ACT.Copy).then_inc(gu_high, 1)

            def split_dn(c, uses):
                act.wait_ge(dn_loaded[c], 16 * uses)
                act.activation(dn_hi[c][:], raw_dn[c][:], ACT.Copy).then_inc(dn_high, 1)

            def xhi(e, c):
                act.wait_ge(tr_done, e + 1)
                act.activation(xt[c][:, :, 0, :].rearrange("p (a b) s -> p a b s", b=2),
                               tpe[:, :, 0:C2].rearrange("p a (b s) -> p a b s", b=2), ACT.Copy
                               ).then_inc(xhi_done, 1)

            def low(e, it):
                act.wait_ge(gu_done, 2 * e + it + 1)
                act.activation(gu_low[:, it], gup[it][:, :, CAP:C2], ACT.Copy).then_inc(low_copied, 1)

            def silu(e, it):
                act.wait_ge(summed, 2 * e + it + 1)
                act.activation(silu_e[:, it], gu_sum[:, it, 0], ACT.Silu).then_inc(silu_done, 1)

            def hid_high(e, c, it):
                act.wait_ge(hid_done, 2 * e + it + 1)
                act.activation(he_hi[c][:, it], hid_e[:, it], ACT.Copy).then_inc(hhi_done, 1)

            def hidden(e, c):
                for it in range(IT):
                    silu(e, it)
                for it in range(IT):
                    hid_high(e, c, it)

            split_gu(0, 0, 1)
            split_gu(1, 1, 1)
            xhi(0, 0)
            for it in range(IT):
                low(0, it)
            xhi(1, 1)
            hidden(0, 0)
            split_dn(0, 1)

            def body(e, i, u):
                c, d = u, 1 - u
                if exists(e, 2):
                    act.wait_ge(gu_done, 2 * e + 2)
                    split_gu(e + 2, c, i + 2)
                if exists(e, 1):
                    low(e + 1, 0)
                if exists(e, 2):
                    xhi(e + 2, c)
                if exists(e, 1):
                    act.wait_ge(down_done, 2 * e)
                    split_dn(d, i + 1 + u)
                    low(e + 1, 1)
                    hidden(e + 1, d)
                act.wait_ge(ids_loaded[c], 16 * (i + 1))
                for h in range(2):
                    act.wait_ge(down_done, 2 * e + h + 1)
                    act.activation(ys[c][:, h, :], yp[0:HALF, h, :], ACT.Copy,
                                   scale=ids_s[c][:, h, 1:2].bitcast(F32)).then_inc(y_done, 1)

            over_experts(act, body)

        @block.vector
        def _(dve):
            def vector_part(e, c):
                dve.wait_ge(gu_high, e + 1)
                dve.tensor_tensor(slices(gu_lo[c], 0, VS), slices(raw_gu[c], 0, VS),
                                  slices(gu_hi[c], 0, VS).bitcast(F32), ALU.subtract).then_inc(vector_low, 1)

            def dn_part(e, c):
                dve.wait_ge(dn_high, e + 1)
                dve.tensor_tensor(dn_lo[c][:], raw_dn[c][:], dn_hi[c][:].bitcast(F32), ALU.subtract
                                  ).then_inc(dn_low, 1)

            def xlo(e, c):
                dve.wait_ge(xhi_done, e + 1)
                dve.tensor_tensor(xt[c][:, :, 1, :].rearrange("p (a b) s -> p a b s", b=2),
                                  tpe[:, :, 0:C2].rearrange("p a (b s) -> p a b s", b=2),
                                  xt[c][:, :, 0, :].bitcast(F32).rearrange("p (a b) s -> p a b s", b=2), ALU.subtract
                                  ).then_inc(xlo_done, 1)

            def add(e, it):
                dve.wait_ge(low_copied, 2 * e + it + 1)
                dve.tensor_tensor(gu_sum[:, it], gup[it][:, :, 0:CAP], gu_low[:, it], ALU.add).then_inc(summed, 1)

            def hidden(e, c):
                for it in range(IT):
                    dve.wait_ge(silu_done, 2 * e + it + 1)
                    dve.tensor_tensor(hid_e[:, it], silu_e[:, it], gu_sum[:, it, 1], ALU.mult).then_inc(hid_done, 1)
                for it in range(IT):
                    dve.wait_ge(hhi_done, 2 * e + it + 1)
                    dve.tensor_tensor(he_lo[c][:, it], hid_e[:, it], he_hi[c][:, it].bitcast(F32), ALU.subtract
                                      ).then_inc(hlo_done, 1)

            vector_part(0, 0)
            vector_part(1, 1)
            xlo(0, 0)
            for it in range(IT):
                add(0, it)
            xlo(1, 1)
            hidden(0, 0)
            dn_part(0, 0)

            def body(e, i, u):
                c, d = u, 1 - u
                if exists(e, 2):
                    vector_part(e + 2, c)
                if exists(e, 1):
                    add(e + 1, 0)
                if exists(e, 2):
                    xlo(e + 2, c)
                if exists(e, 1):
                    add(e + 1, 1)
                    hidden(e + 1, d)
                    dn_part(e + 1, d)

            over_experts(dve, body)

        @block.tensor
        def _(pe):
            def turn(e, c, uses):
                pe.wait_ge(gathered[c], 32 * uses)
                for k in range(KT):
                    for h in range(2):
                        at = (k % 2) * CAP + h * HALF
                        last = pe.transpose(tpe[:, k // 2, at:at + HALF], xs[c][:, h, k:D:KT], ident[0:HALF, 0:HALF])
                last.then_inc(tr_done, 1)

            def gate_up(e, c, it):
                for j in range(2):
                    for k in range(KT):
                        at = slice(it, I, IT)
                        pe.matmul(gup[it][:, j, 0:C2], gu_hi[c][:, j, k, at], xt[c][:, k].rearrange("p a s -> p (a s)"),
                                  start=(k == 0), stop=False, skip_group_check=True)
                        last = pe.matmul(gup[it][:, j, 0:CAP], gu_lo[c][:, j, k, at], xt[c][:, k, 0],
                                         start=False, stop=(k == KT - 1), skip_group_check=True)
                last.then_inc(gu_done, 1)

            def down(c):
                for h in range(2):
                    at = slice(h * HALF, (h + 1) * HALF)
                    for it in range(IT):
                        for q, (hp, w) in enumerate(((he_hi, dn_hi), (he_lo, dn_hi), (he_hi, dn_lo))):
                            last = pe.matmul(yp[0:HALF, h, :], hp[c][:, it, at], w[c][:, it, :],
                                             start=(it == 0 and q == 0), stop=(it == IT - 1 and q == 2))
                    last.then_inc(down_done, 1)

            def gu_ready(e):
                pe.wait_ge(xlo_done, e + 1)
                pe.wait_ge(vector_low, e + 1)
                pe.wait_ge(pool_low, e + 1)

            turn(0, 0, 1)
            gu_ready(0)
            for it in range(IT):
                gate_up(0, 0, it)
            turn(1, 1, 1)

            def body(e, i, u):
                c, d = u, 1 - u
                if exists(e, 1):
                    gu_ready(e + 1)
                    pe.wait_ge(summed, 2 * e + 1)
                    gate_up(e + 1, d, 0)
                if exists(e, 2):
                    turn(e + 2, c, i + 2)
                if exists(e, 1):
                    pe.wait_ge(summed, 2 * e + 2)
                    gate_up(e + 1, d, 1)
                pe.wait_ge(hlo_done, 2 * e + 2)
                pe.wait_ge(dn_low, e + 1)
                pe.wait_ge(y_done, 2 * e)
                down(c)

            over_experts(pe, body)


def attention_phase(nc, consts, w_hi, w_lo, xT_hi, xT_lo, qk_bias, v_bias, o_bias, xT, x, acc_rows, out):
    ident, = consts
    K3 = 3 * HD
    K5 = K3 + 2
    NP = TT // 2
    UNITS = B * H
    VW = 3 * HD
    VB = 5
    SCALE = 1.0 / float(HD) ** 0.5

    with ExitStack() as ctx:
        def sb(name, shape, dt=F32):
            return ctx.enter_context(nc.sbuf_tensor(name, shape, dt))

        def pb(name, shape):
            return ctx.enter_context(nc.psum_tensor(name, shape, F32))

        def sem(name):
            return ctx.enter_context(nc.semaphore(name))

        qk_hi = [sb(f"{a}_hi", [P, S], F32R) for a in "qk"]
        qk_lo = [sb(f"{a}_lo", [P, S]) for a in "qk"]
        stack = [[sb(f"{a}_stack{i}", [K5, GH, S], F32R) for i in range(2)] for a in "qk"]
        v_sum = sb("v_sum", [P, 2 * P])
        v_cols = [sb(f"v_cols{i}", [P, TT, GH, VB, HD], F32R) for i in range(2)]
        neg_max = [sb(f"neg_max{i}", [P, 2, TT]) for i in range(2)]
        neg_hi = [sb(f"neg_hi{i}", [2 * TT, P], F32R) for i in range(2)]
        neg_lo = [sb(f"neg_lo{i}", [2 * TT, P], F32R) for i in range(2)]
        probs = [sb(f"probs{i}", [P, 2, S]) for i in range(NP)]
        p_hi = [sb(f"p_hi{i}", [P, 2, S], F32R) for i in range(NP)]
        p_lo = [sb(f"p_lo{i}", [P, 2, S], F32R) for i in range(NP)]
        ctx_low = sb("ctx_low", [HD, S])
        ctx_sum = sb("ctx_sum", [P, S])
        norm = sb("norm", [P, S])
        ctx_hi = sb("ctx_hi", [P, G, S], F32R)
        ctx_lo = sb("ctx_lo", [P, G, S], F32R)
        gate = sb("gate", [P, TT, D])
        att = sb("att", [P, D])
        xin = [sb(f"x_in{i}", [P, D]) for i in range(2)]

        sc = pb("sc", [P, 2, S])
        mx = pb("mx", [P, 2, S])
        pv = [pb(f"pv{i}", [P, S]) for i in range(2)]
        aux = [pb(f"aux{i}", [P, S]) for i in range(2)]

        ones_set = sem("c_ones_set")
        x_turned = sem("c_x_turned")
        aux_done = sem("c_aux_done")
        aux_read = [sem(f"c_aux_read{i}") for i in range(2)]
        max_high_done = sem("c_max_high_done")
        qk_high_done = sem("c_qk_high_done")
        qk_low_done = sem("c_qk_low_done")
        v_high = sem("c_v_high")
        v_low = sem("c_v_low")
        stacked = [sem(f"c_stacked{i}") for i in range(2)]
        neg_stacked = [sem(f"c_neg_stacked{i}") for i in range(2)]
        mx_done = sem("c_mx_done")
        mx_read = sem("c_mx_read")
        sc_done = sem("c_sc_done")
        exp_done = sem("c_exp_done")
        phi_done = sem("c_phi_done")
        plo_done = sem("c_plo_done")
        pv_done = sem("c_pv_done")
        log_done = sem("c_log_done")
        low_copied = sem("c_low_copied")
        ctx_added = sem("c_ctx_added")
        inv_done = sem("c_inv_done")
        nrm_done = sem("c_nrm_done")
        chi_done = sem("c_chi_done")
        clo_done = sem("c_clo_done")
        acc_loaded = sem("c_acc_loaded")
        xin_loaded = [sem(f"c_xin_loaded{i}") for i in range(2)]
        gate_done = sem("c_gate_done")
        att_done = sem("c_att_done")
        y_done = sem("c_y_done")
        y_stored = sem("c_y_stored")

        x_v = x.rearrange("(b t p) d -> b p t d", p=P, t=TT)
        acc_v = acc_rows[0:T, :].rearrange("(b t p) d -> b p t d", p=P, t=TT)
        out_v = out.rearrange("(b t p) d -> b p t d", p=P, t=TT)

        def rows(h, part):
            part = 2 - part if h % 2 else part
            return slice(part * HD, (part + 1) * HD)

        def uses(b, j):
            last = isinstance(b, int) and b == B - 1
            if j == 0:
                return ("max1", "q", "k", "max0") if isinstance(b, int) and b == 0 else (
                    "v3", "max1", "q", "k", "max0", "out0", "out1")
            if j == 1:
                outs = () if isinstance(b, int) and b == 0 else ("out2", "out3")
                return outs + ("max1", "v0", "q", "k", "v1", "max0", "v2", "v3")
            if j == 2:
                return ("max1", "max0") if last else ("max1", "q", "k", "max0", "v0")
            return ("max1",) if last else ("v1", "max1", "q", "k", "max0", "v2")

        places = (
            {(0, "A"): ("v3",), (2, "C"): ("out0",), (3, "A"): ("out1",)},
            {(0, "A"): ("out2",), (0, "B"): ("out3",), (1, "A"): ("v0",), (2, "B"): ("v1",), (3, "A"): ("v2",),
             (3, "B"): ("v3",)},
            {(3, "A"): ("v0",)},
            {(0, "A"): ("v1",), (3, "A"): ("v2",)},
        )

        def at(b, j, h, place, kind):
            return [(int(use[-1]), use_no(b, j, use)) for use in places[j].get((h, place), ())
                    if use in uses(b, j) and use.startswith(kind)]

        def v_no(b, j, s):
            return 8 * b + s + (0, 4, 8, 8)[j]

        def v_half(j):
            return 1 if j == 1 else 0

        def use_no(b, j, use):
            first = isinstance(b, int) and b == 0
            last = isinstance(b, int) and b == B - 1
            before = (9 if first else 4, 13 if first else 11, 21, 23 if last else 26)[j]
            return b, before + uses(b, j).index(use)

        def number(use, later=0):
            return 28 * use[0] + use[1] + later

        def buf(use):
            return use[1] % 2

        def turn(use):
            return 14 * use[0] + use[1] // 2

        def follows(b, j, ahead):
            return not isinstance(b, int) or G * b + j + ahead < G * B

        def over_groups(engine, step):
            for b, j in ((0, 0), (0, 1), (0, 2), (0, 3), (1, 0), (1, 1)):
                step(b, j)
            with engine.Fori(1, B - 1) as b:
                for j in (2, 3):
                    step(b, j)
                for j in (0, 1):
                    step(b + 1, j)
            for j in (2, 3):
                step(B - 1, j)

        block = ctx.enter_context(nc.Block())

        @block.sync
        def _(sp):
            def stack_rows(a, g2, pair):
                parts = (qk_hi, qk_lo, qk_hi) if a == 0 else (qk_hi, qk_hi, qk_lo)
                for n, part in enumerate(parts):
                    sp.dma_start(stack[a][g2][n * HD:(n + 1) * HD, 2 * pair:2 * pair + 2, :].bitcast(F32),
                                 part[a][pair * 2 * HD:(pair + 1) * 2 * HD, :].bitcast(F32)
                                 ).then_inc(stacked[pair], 16)

            def stack_up(a, g, g2, pair):
                sp.wait_ge(qk_low_done, 2 * g + a + 1)
                stack_rows(a, g2, pair)

            def stack_max(pair, use, g2):
                sp.wait_ge(aux_read[buf(use)], turn(use) + 1)
                for n, part in enumerate((neg_hi, neg_lo)):
                    sp.dma_start(stack[0][g2][K3 + n:K3 + n + 1, 2 * pair:2 * pair + 2, :].bitcast(F32)
                                 .rearrange("o h (t s) -> o (h t) s", s=P), part[pair][:].bitcast(F32)
                                 ).then_inc(neg_stacked[pair], 16)

            def load_late(b, tt):
                sp.wait_ge(y_done, TT * b + tt - 1)
                sp.dma_start(xin[tt % 2][:], x_v[b, :, tt]).then_inc(xin_loaded[tt % 2], 16)

            for pair in range(2):
                stack_up(0, 0, 0, pair)
            for pair in range(2):
                stack_up(1, 0, 0, pair)
            stack_max(0, (0, 6), 0)
            stack_up(0, 1, 1, 0)
            stack_up(1, 1, 1, 0)

            def step(b, j):
                g = G * b + j
                if j == 2 and follows(b, j, 2):
                    sp.wait_ge(aux_done, number(use_no(b, j, "max1")))
                    for part, tile in enumerate((xT_hi, xT_lo)):
                        sp.dma_start(tile[:].bitcast(F32), xT[b + 1, part].rearrange("p (k s) -> p k s", k=KT)
                                     ).then_inc(x_turned, 16)
                if follows(b, j, 1):
                    sp.wait_ge(sc_done, 2 * GH * g)
                    for a in range(2):
                        stack_rows(a, (j + 1) % 2, 1)
                if "out3" in uses(b, j):
                    load_late(b - 1, 3)
                stack_max(1, use_no(b, j, "max1"), j % 2)
                if j == 2:
                    sp.wait_ge(y_stored, 16 * b)
                    sp.dma_start(gate[:], acc_v[b]).then_inc(acc_loaded, 16)
                    for tt in range(2):
                        sp.dma_start(xin[tt][:], x_v[b, :, tt]).then_inc(xin_loaded[tt], 16)
                if follows(b, j, 2):
                    stack_up(0, g + 2, j % 2, 0)
                    stack_up(1, g + 2, j % 2, 0)
                if follows(b, j, 1):
                    stack_max(0, use_no(b, j, "max0"), (j + 1) % 2)
                if "out0" in uses(b, j):
                    load_late(b - 1, 2)
                if "out3" in uses(b, j):
                    sp.wait_ge(y_done, TT * b)
                    sp.dma_start(out_v[b - 1], gate[:]).then_inc(y_stored, 16)

            over_groups(sp, step)
            for tt in (2, 3):
                load_late(B - 1, tt)
            sp.wait_ge(y_done, TT * B)
            sp.dma_start(out_v[B - 1], gate[:]).then_inc(y_stored, 16)
            sp.wait_ge(y_stored, 16 * B)

        @block.scalar
        def _(act):
            nc.scalar.preload_act_table_set("natural_log_exp_and_others")

            def qk_high(a, use, g, c):
                act.wait_ge(aux_done, number(use, 1))
                for pair in range(2):
                    act.wait_ge(stacked[pair], 16 * 6 * g)
                act.activation(qk_lo[a][:], aux[buf(use)][:], ACT.Identity, bias=qk_bias[:, a, c:c + 1]
                               ).then_inc(aux_read[buf(use)], 1)
                act.wait_ge(aux_read[buf(use)], turn(use) + 1)
                act.activation(qk_hi[a][:], qk_lo[a][:], ACT.Copy).then_inc(qk_high_done, 1)

            def max_high(pair, use, g):
                act.wait_ge(aux_done, number(use, 1))
                act.wait_ge(neg_stacked[pair], 32 * g)
                act.activation(neg_hi[pair][:], aux[buf(use)][0:2 * TT, 0:P], ACT.Copy).then_inc(max_high_done, 1)

            def v_split(use, c, s):
                act.wait_ge(aux_read[buf(use)], turn(use) + 1)
                act.activation(v_cols[c][:, s, :, 0:VB:VB - 1, :],
                               v_sum[:].rearrange("p (h o d) -> p h o d", h=GH, o=2), ACT.Copy).then_inc(v_high, 1)

            def exponentials(unit, pair):
                act.wait_ge(sc_done, 2 * unit + pair + 1)
                if not isinstance(unit, int) or unit > 0:
                    act.wait_ge(plo_done, 2 * unit + pair - 1)
                act.activation(probs[pair][:], sc[:], ACT.Exp, scale=SCALE).then_inc(exp_done, 1)

            def head_out(unit, g, h):
                act.wait_ge(pv_done, 2 * unit + 2)
                if h == 0:
                    act.wait_ge(clo_done, g)
                act.activation(norm[h * HD:(h + 1) * HD, :], pv[h % 2][rows(h, 2), :], ACT.Ln).then_inc(log_done, 1)
                act.wait_ge(ctx_added, unit)
                act.activation(ctx_low[:], pv[h % 2][rows(h, 1), :], ACT.Copy).then_inc(low_copied, 1)

            def invert(g):
                act.wait_ge(log_done, GH * (g + 1))
                act.activation(norm[:], norm[:], ACT.Exp, scale=-1.0).then_inc(inv_done, 1)

            def ctx_high(g, c):
                act.wait_ge(nrm_done, g + 1)
                act.activation(ctx_hi[:, c, :], norm[:], ACT.Copy).then_inc(chi_done, 1)

            qk_high(0, (0, 0), 0, 0)
            qk_high(1, (0, 1), 0, 0)
            for s in range(TT):
                v_split((0, 2 + s), 0, s)
            max_high(0, (0, 6), 0)
            qk_high(0, (0, 7), 1, 1)
            qk_high(1, (0, 8), 1, 1)

            def open_gate(b):
                act.wait_ge(acc_loaded, 16 * (b + 1))
                act.activation(gate[:], gate[:], ACT.Silu).then_inc(gate_done, 1)
                nc.scalar.preload_act_table_set("natural_log_exp_and_others")

            def step(b, j):
                g = G * b + j
                first = isinstance(b, int) and g == 0
                for h in range(GH):
                    unit = GH * g + h
                    exponentials(unit, 0)
                    for t, use in at(b, j, h, "A", "v"):
                        v_split(use, v_half(j), t)
                    if h == 2 and follows(b, j, 2):
                        qk_high(1, use_no(b, j, "k"), g + 2, (j + 2) % G)
                    if h >= 2 or not first:
                        head_out(unit - 2, g if h >= 2 else g - 1, (h - 2) % GH)
                    exponentials(unit, 1)
                    if h == 1 and not first:
                        invert(g - 1)
                    if h == 1 and follows(b, j, 2):
                        qk_high(0, use_no(b, j, "q"), g + 2, (j + 2) % G)
                    if h == 1 and not first:
                        ctx_high(g - 1, (j - 1) % G)
                    for t, use in at(b, j, h, "B", "v"):
                        v_split(use, v_half(j), t)
                    if h == 0:
                        max_high(1, use_no(b, j, "max1"), g)
                    if h == 2 and follows(b, j, 1):
                        max_high(0, use_no(b, j, "max0"), g + 1)
                    if h == 2 and "out0" in uses(b, j):
                        open_gate(b - 1)

            over_groups(act, step)
            open_gate(B - 1)
            head_out(UNITS - 2, G * B - 1, 2)
            head_out(UNITS - 1, G * B - 1, 3)
            invert(G * B - 1)
            ctx_high(G * B - 1, G - 1)

        @block.vector
        def _(dve):
            def qk_low(a, g):
                dve.wait_ge(qk_high_done, 2 * g + a + 1)
                dve.tensor_tensor(qk_lo[a][:], qk_lo[a][:], qk_hi[a][:].bitcast(F32), ALU.subtract
                                  ).then_inc(qk_low_done, 1)

            def max_low(pair, use, g):
                dve.wait_ge(max_high_done, 2 * g + pair + 1)
                dve.tensor_tensor(neg_lo[pair][:], aux[buf(use)][0:2 * TT, 0:P], neg_hi[pair][:].bitcast(F32),
                                  ALU.subtract).then_inc(aux_read[buf(use)], 1)

            def v_make(n, use, half):
                dve.wait_ge(aux_done, number(use, 1))
                dve.wait_ge(v_low, n)
                dve.tensor_tensor(v_sum[:], aux[buf(use)][:, 0:2 * P], v_bias[:, half * 2 * P:(half + 1) * 2 * P],
                                  ALU.add).then_inc(aux_read[buf(use)], 1)

            def v_make_low(n, c, s):
                dve.wait_ge(v_high, n + 1)
                dve.tensor_tensor(v_cols[c][:, s, :, 1:VB - 1:2, :],
                                  v_sum[:].rearrange("p (h o d) -> p h o d", h=GH, o=2),
                                  v_cols[c][:, s, :, 0:VB:VB - 1, :].bitcast(F32), ALU.subtract).then_inc(v_low, 1)

            def maxima(g, h, tp):
                dve.wait_ge(mx_done, 2 * GH * g + 2 * h + tp + 1)
                dve.tensor_reduce(neg_max[h // 2][:, h % 2, 2 * tp:2 * tp + 2], mx[:], AX.X, ALU.max, negate=True
                                  ).then_inc(mx_read, 1)

            def high_probs(unit, pair):
                dve.wait_ge(exp_done, 2 * unit + pair + 1)
                if not isinstance(unit, int) or unit > 0:
                    dve.wait_ge(pv_done, 2 * unit + pair - 1)
                dve.tensor_copy(p_hi[pair][:], probs[pair][:]).then_inc(phi_done, 1)

            def head_out(unit, g, h):
                dve.wait_ge(low_copied, unit + 1)
                if h == 0:
                    dve.wait_ge(nrm_done, g)
                dve.tensor_tensor(ctx_sum[h * HD:(h + 1) * HD, :], pv[h % 2][rows(h, 0), :], ctx_low[:], ALU.add
                                  ).then_inc(ctx_added, 1)

            def normalise(g):
                dve.wait_ge(inv_done, g + 1)
                dve.wait_ge(ctx_added, GH * (g + 1))
                dve.tensor_tensor(norm[:], norm[:], ctx_sum[:], ALU.mult).then_inc(nrm_done, 1)

            def ctx_low_part(g, c):
                dve.wait_ge(chi_done, g + 1)
                dve.tensor_tensor(ctx_lo[:, c, :], norm[:], ctx_hi[:, c, :].bitcast(F32), ALU.subtract
                                  ).then_inc(clo_done, 1)

            def output(b, tt, use):
                dve.wait_ge(aux_done, number(use, 1))
                dve.wait_ge(att_done, TT * b + tt)
                dve.tensor_tensor(att[:], aux[buf(use)][:], o_bias[:], ALU.add).then_inc(aux_read[buf(use)], 1)

            def times_gate(b, tt, use):
                if tt == 0:
                    dve.wait_ge(gate_done, b + 1)
                dve.wait_ge(aux_read[buf(use)], turn(use) + 1)
                dve.tensor_tensor(gate[:, tt, :], att[:], gate[:, tt, :], ALU.mult).then_inc(att_done, 1)

            for a in range(2):
                qk_low(a, 0)
            for s in range(TT):
                v_make(s, (0, 2 + s), 0)
                v_make_low(s, 0, s)
            for h in range(GH):
                for tp in range(NP if h < GH - 1 else 1):
                    maxima(0, h, tp)
            max_low(0, (0, 6), 0)
            for a in range(2):
                qk_low(a, 1)

            def step(b, j):
                g = G * b + j
                first = isinstance(b, int) and g == 0

                def value_sums(h, place):
                    for t, use in at(b, j, h, place, "v"):
                        v_make(v_no(b, j, t), use, v_half(j))

                def value_lows(h, place):
                    for t, use in at(b, j, h, place, "v"):
                        v_make_low(v_no(b, j, t), v_half(j), t)

                for h in range(GH):
                    unit = GH * g + h
                    if h == 3 and "out0" in uses(b, j):
                        times_gate(b - 1, 0, use_no(b, j, "out0"))
                    value_sums(h, "A")
                    for tt, use in at(b, j, h, "A", "out"):
                        output(b - 1, tt, use)
                        times_gate(b - 1, tt, use)
                    high_probs(unit, 0)
                    if h == 0:
                        maxima(g, GH - 1, 1)
                    elif follows(b, j, 1):
                        maxima(g + 1, h - 1, 1)
                    value_lows(h, "A")
                    if h == 2 and follows(b, j, 2):
                        qk_low(1, g + 2)
                    if h >= 2 or not first:
                        head_out(unit - 2, g if h >= 2 else g - 1, (h - 2) % GH)
                    if h == 1 and not first:
                        normalise(g - 1)
                    value_sums(h, "B")
                    for tt, use in at(b, j, h, "B", "out"):
                        output(b - 1, tt, use)
                        times_gate(b - 1, tt, use)
                    high_probs(unit, 1)
                    if follows(b, j, 1):
                        maxima(g + 1, h, 0)
                    value_lows(h, "B")
                    if h == 1 and follows(b, j, 2):
                        qk_low(0, g + 2)
                    if h == 1 and not first:
                        ctx_low_part(g - 1, (j - 1) % G)
                    if h == 0:
                        max_low(1, use_no(b, j, "max1"), g)
                    if h == 2 and follows(b, j, 1):
                        max_low(0, use_no(b, j, "max0"), g + 1)
                    for tt, use in at(b, j, h, "C", "out"):
                        output(b - 1, tt, use)

            over_groups(dve, step)
            head_out(UNITS - 2, G * B - 1, 2)
            head_out(UNITS - 1, G * B - 1, 3)
            normalise(G * B - 1)
            ctx_low_part(G * B - 1, G - 1)
            for tt in range(TT):
                for part in (output, times_gate):
                    part(B - 1, tt, (B - 1, use_no(B - 1, 3, "max1")[1] + 1 + tt))

        @block.gpsimd
        def _(pool):
            for i in range(2):
                pool.memset(stack[1][i][K3:K5, :, :].bitcast(F32), 1.0).then_inc(ones_set, 1)
                pool.wait_ge(ones_set, 2 * i + 1)
                pool.memset(v_cols[i][:, :, :, 2, :].bitcast(F32), 1.0).then_inc(ones_set, 1)
                pool.wait_ge(ones_set, 2 * i + 2)

            def low_probs(unit, pair):
                pool.wait_ge(phi_done, 2 * unit + pair + 1)
                pool.tensor_tensor(p_lo[pair][:], probs[pair][:], p_hi[pair][:].bitcast(F32), ALU.subtract
                                   ).then_inc(plo_done, 1)

            def result(b, tt):
                pool.wait_ge(att_done, TT * b + tt + 1)
                pool.wait_ge(xin_loaded[tt % 2], 16 * (2 * b + tt // 2 + 1))
                pool.tensor_tensor(gate[:, tt, :], gate[:, tt, :], xin[tt % 2][:], ALU.add).then_inc(y_done, 1)

            def step(b, j):
                g = G * b + j
                for h in range(GH):
                    unit = GH * g + h
                    low_probs(unit, 0)
                    if h == 3 and "out0" in uses(b, j):
                        result(b - 1, 0)
                    if h == 1 and "out3" in uses(b, j):
                        result(b - 1, 3)
                    low_probs(unit, 1)
                    if h == 3 and "out0" in uses(b, j):
                        result(b - 1, 1)
                    if h == 0 and "out3" in uses(b, j):
                        result(b - 1, 2)

            over_groups(pool, step)
            for tt in range(TT):
                result(B - 1, tt)

        @block.tensor
        def _(pe):
            def aux_free(use):
                pe.wait_ge(aux_read[buf(use)], turn(use))

            def turned_product(a, c, use):
                aux_free(use)
                cols = slice(a * D + c * P, a * D + (c + 1) * P)
                for k in range(KT):
                    for q, (w, xt) in enumerate(((w_hi, xT_hi), (w_lo, xT_hi), (w_hi, xT_lo))):
                        last = pe.matmul(aux[buf(use)][:], w[:, k, cols], xt[:, k, :],
                                         start=(k == 0 and q == 0), stop=(k == KT - 1 and q == 2))
                last.then_inc(aux_done, 1)

            def v_product(half, s, use):
                aux_free(use)
                cols = slice(2 * D + half * 2 * P, 2 * D + (half + 1) * 2 * P)
                for k in range(KT):
                    for q, (xt, w) in enumerate(((xT_hi, w_hi), (xT_lo, w_hi), (xT_hi, w_lo))):
                        last = pe.matmul(aux[buf(use)][:, 0:2 * P], xt[:, k, s * P:(s + 1) * P], w[:, k, cols],
                                         start=(k == 0 and q == 0), stop=(k == KT - 1 and q == 2))
                last.then_inc(aux_done, 1)

            def turn_maxima(g, pair, use):
                aux_free(use)
                pe.wait_ge(mx_read, 2 * GH * g + GH * (pair + 1))
                pe.transpose(aux[buf(use)][0:2 * TT, 0:P], neg_max[pair][:].rearrange("p h t -> p (h t)"), ident[:]
                             ).then_inc(aux_done, 1)

            def scores_for_max(g, g2, h, tp):
                if h % 2 == 0 and tp == 0:
                    pe.wait_ge(stacked[h // 2], 16 * 6 * (g + 1))
                index = 2 * GH * g + 2 * h + tp
                if not isinstance(index, int) or index > 0:
                    pe.wait_ge(mx_read, index)
                for n in range(2):
                    at = slice((2 * tp + n) * P, (2 * tp + n + 1) * P)
                    last = pe.matmul(mx[:, n, :], stack[0][g2][0:K3, h, at], stack[1][g2][0:K3, h, :],
                                     start=True, stop=True)
                last.then_inc(mx_done, 1)

            def scores(unit, g, g2, h, pair):
                if pair == 0 and h % 2 == 0:
                    pe.wait_ge(neg_stacked[h // 2], 32 * (g + 1))
                if not isinstance(unit, int) or unit > 0 or pair > 0:
                    pe.wait_ge(exp_done, 2 * unit + pair)
                for n in range(2):
                    at = slice((2 * pair + n) * P, (2 * pair + n + 1) * P)
                    last = pe.matmul(sc[:, n, :], stack[1][g2][:, h, at], stack[0][g2][:, h, :],
                                     start=True, stop=True)
                last.then_inc(sc_done, 1)

            def weigh_values(unit, c, h, pair):
                pe.wait_ge(plo_done, 2 * unit + pair + 1)
                if pair == 0 and (not isinstance(unit, int) or unit > 0):
                    pe.wait_ge(ctx_added, unit - 1)
                first = 2 * (h % 2)
                for n in range(2):
                    for q, part in enumerate((p_hi, p_lo)):
                        last = pe.matmul(pv[h % 2][0:VW, :], v_cols[c // 2][:, 2 * pair + n, (c % 2) * 2 + h // 2, first:first + 3, :]
                                         .rearrange("p b d -> p (b d)"),
                                         part[pair][:, n, :], start=(pair == 0 and n == 0 and q == 0),
                                         stop=(pair == 1 and n == 1 and q == 1))
                last.then_inc(pv_done, 1)

            def out_product(b, tt, use):
                aux_free(use)
                if tt == 0:
                    pe.wait_ge(clo_done, G * (b + 1))
                for k in range(KT):
                    for q, (cp, w) in enumerate(((ctx_hi, w_hi), (ctx_lo, w_hi), (ctx_hi, w_lo))):
                        last = pe.matmul(aux[buf(use)][:], cp[:, k, tt * P:(tt + 1) * P], w[:, k, 3 * D:4 * D],
                                         start=(k == 0 and q == 0), stop=(k == KT - 1 and q == 2))
                last.then_inc(aux_done, 1)

            turned_product(0, 0, (0, 0))
            turned_product(1, 0, (0, 1))
            for s in range(TT):
                v_product(0, s, (0, 2 + s))
            for h in range(GH):
                for tp in range(NP if h < GH - 1 else 1):
                    scores_for_max(0, 0, h, tp)
            turn_maxima(0, 0, (0, 6))
            pe.wait_ge(ones_set, 4)
            turned_product(0, 1, (0, 7))
            turned_product(1, 1, (0, 8))

            def step(b, j):
                g = G * b + j
                first = isinstance(b, int) and g == 0

                def extras(h, place):
                    for t, use in at(b, j, h, place, "v"):
                        v_product(v_half(j), t, use)
                    for tt, use in at(b, j, h, place, "out"):
                        out_product(b - 1, tt, use)

                for h in range(GH):
                    unit = GH * g + h
                    scores(unit, g, j % 2, h, 0)
                    extras(h, "A")
                    if h == 2 and follows(b, j, 2):
                        turned_product(1, (j + 2) % G, use_no(b, j, "k"))
                    if h > 0 or not first:
                        weigh_values(unit - 1, j if h > 0 else (j - 1) % G, (h - 1) % GH, 0)
                    if h == 0:
                        scores_for_max(g, j % 2, GH - 1, 1)
                    elif follows(b, j, 1):
                        scores_for_max(g + 1, (j + 1) % 2, h - 1, 1)
                    scores(unit, g, j % 2, h, 1)
                    if h == 1 and follows(b, j, 2):
                        if j == 2:
                            pe.wait_ge(x_turned, 32 * (b + 1))
                        turned_product(0, (j + 2) % G, use_no(b, j, "q"))
                    extras(h, "B")
                    if h > 0 or not first:
                        weigh_values(unit - 1, j if h > 0 else (j - 1) % G, (h - 1) % GH, 1)
                    if follows(b, j, 1):
                        scores_for_max(g + 1, (j + 1) % 2, h, 0)
                    if h == 0:
                        turn_maxima(g, 1, use_no(b, j, "max1"))
                    if h == 2 and follows(b, j, 1):
                        turn_maxima(g + 1, 0, use_no(b, j, "max0"))
                    extras(h, "C")

            over_groups(pe, step)
            for pair in range(NP):
                weigh_values(UNITS - 1, G - 1, GH - 1, pair)
            for tt in range(TT):
                out_product(B - 1, tt, (B - 1, use_no(B - 1, 3, "max1")[1] + 1 + tt))


def recurrent_moe_attention_kernel(nc: bass.Bass, x: bass.AP, qkv_wT: bass.AP, qkv_b: bass.AP, out_wT: bass.AP,
                                   out_b: bass.AP, router_wT: bass.AP, e_bias: bass.AP, W_gate: bass.AP,
                                   W_up: bass.AP, W_down: bass.AP, gateT: bass.AP, upT: bass.AP, downT: bass.AP,
                                   out: bass.AP):
    def scratch(name, shape, dt=F32):
        return nc.dram_tensor(name, shape, dt, kind="Internal").ap()

    xn_rows = scratch("xn_rows", [ROWS, D])
    acc_rows = scratch("acc_rows", [ROWS, D])
    table = scratch("slot_table", [SLOTS, 2], I32)
    wb_hi = scratch("wb_hi", [D, 4 * D])
    wb_lo = scratch("wb_lo", [D, 4 * D])
    xT = scratch("xT", [B, 2, P, KT * S])

    with ExitStack() as ctx:
        ident = ctx.enter_context(nc.sbuf_tensor("ident", [P, P], F32))
        tokens_phase(nc, (ident,), x, router_wT, e_bias, gateT, upT, downT, qkv_wT, out_wT,
                     xn_rows, acc_rows, table, wb_hi, wb_lo, xT)

        w_hi = ctx.enter_context(nc.sbuf_tensor("w_hi", [P, KT, 4 * D], F32R))
        w_lo = ctx.enter_context(nc.sbuf_tensor("w_lo", [P, KT, 4 * D], F32R))
        xT_hi = ctx.enter_context(nc.sbuf_tensor("xT_hi", [P, KT, S], F32R))
        xT_lo = ctx.enter_context(nc.sbuf_tensor("xT_lo", [P, KT, S], F32R))
        qk_bias = ctx.enter_context(nc.sbuf_tensor("qk_bias", [P, 2, G], F32))
        v_bias = ctx.enter_context(nc.sbuf_tensor("v_bias", [P, D], F32))
        o_bias = ctx.enter_context(nc.sbuf_tensor("o_bias", [P, D], F32))
        next_loaded = ctx.enter_context(nc.semaphore("next_loaded"))

        def load_next(sp, part):
            def weights(tile, rows, k):
                sp.dma_start(tile[:, k, :].bitcast(F32), rows[k * P:(k + 1) * P, :]).then_inc(next_loaded, 16)

            if part == 0:
                for k in range(KT):
                    weights(w_hi, wb_hi, k)
            elif part <= KT:
                weights(w_lo, wb_lo, part - 1)
            if part in (KT - 1, KT):
                tile = (xT_hi, xT_lo)[part - KT + 1]
                sp.dma_start(tile[:].bitcast(F32), xT[0, part - KT + 1].rearrange("p (k s) -> p k s", k=KT)
                             ).then_inc(next_loaded, 16)
            if part == KT + 1:
                for n in range(2):
                    sp.dma_start(qk_bias[:, n, :], qkv_b[n * D:(n + 1) * D].rearrange("(c p) -> p c", p=P),
                                 allow_slow_non_contiguous=True).then_inc(next_loaded, 16)
                for tile, row in ((v_bias, qkv_b[2 * D:3 * D]), (o_bias, out_b)):
                    sp.dma_start(tile[:], row.rearrange("(a e) -> a e", a=1).to_broadcast([P, D])
                                 ).then_inc(next_loaded, 16)

        def wait_next(sp):
            sp.wait_ge(next_loaded, 16 * (2 * KT + 2 + 4))

        experts_phase(nc, (ident,), W_gate, W_up, W_down, xn_rows, acc_rows, table, load_next, wait_next)
        attention_phase(nc, (ident,), w_hi, w_lo, xT_hi, xT_lo, qk_bias, v_bias, o_bias, xT, x, acc_rows, out)


def kernel(**inputs):
    import numpy as _np
    import concourse.bacc as _bacc
    from concourse import mybir as _mybir
    from concourse.bass_utils import run_bass_kernel_spmd as _run

    attn = {n: inputs["L0_attn_" + n] for n in ("hidden_states", "Wqkv_w", "Wqkv_b", "out_w", "out_b")}
    ffn = {n: inputs["L0_ffn_" + n] for n in ("router_w", "e_bias", "W_gate", "W_up", "W_down",
                                              "shared_gate", "shared_up", "shared_down")}

    def qk_order(a):
        qk = a[:2 * D].reshape(2 * G, 2, GH // 2, HD, -1).transpose(0, 1, 3, 2, 4)
        return _np.concatenate([qk.reshape(2 * D, -1), a[2 * D:].reshape(D, -1)]).reshape(a.shape)

    laid_out = (
        ("x", attn["hidden_states"].reshape(T, D)),
        ("qkv_wT", qk_order(_np.asarray(attn["Wqkv_w"])).T), ("qkv_b", qk_order(_np.asarray(attn["Wqkv_b"]))),
        ("out_wT", attn["out_w"].T), ("out_b", attn["out_b"]),
        ("router_wT", ffn["router_w"].T), ("e_bias", ffn["e_bias"]),
        ("W_gate", ffn["W_gate"]), ("W_up", ffn["W_up"]), ("W_down", ffn["W_down"]),
        ("gateT", ffn["shared_gate"].T), ("upT", ffn["shared_up"].T), ("downT", ffn["shared_down"].T),
    )
    nc = _bacc.Bacc("TRN2", target_bir_lowering=False, num_devices=1)
    arrays, args = {}, []
    for name, a in laid_out:
        a = _np.ascontiguousarray(a)
        arrays[f"in_{name}_dram"] = a
        args.append(nc.dram_tensor(f"in_{name}_dram", a.shape, _mybir.dt.from_np(a.dtype), kind="ExternalInput").ap())
    args.append(nc.dram_tensor("out_0_dram", (T, D), _mybir.dt.from_np(_np.dtype("float32")), kind="ExternalOutput").ap())
    recurrent_moe_attention_kernel(nc, *args)
    r = _run(nc, [arrays], core_ids=[0])
    return r.results[0]["out_0_dram"].reshape(B, S, D)
```
